# Optimizing a Trainium2 kernel written in Bass

```python
import numpy as np
import jax
import jax.numpy as jnp

def _softmax(x, axis=-1):
    return jax.nn.softmax(x, axis=axis)

def _gelu(x):
    return jax.nn.gelu(x, approximate=True)

def _silu(x):
    return jax.nn.silu(x)

def _sigmoid(x):
    return jax.nn.sigmoid(x)

def _layernorm(x, axis=-1, eps=1e-05):
    m = jnp.mean(x, axis=axis, keepdims=True)
    v = jnp.var(x, axis=axis, keepdims=True)
    return (x - m) / jnp.sqrt(v + eps)

def _scatter_add(tgt, idx, src, axis=0):
    return tgt.at[idx].add(src)

def _segment_sum(src, seg, n):
    return jax.ops.segment_sum(src, seg, n)
kernel_name = 'mk_lm_tower_d1_tok_ids768_r4_98245f'

def setup_inputs(seed: int=0):
    np.random.seed(seed)
    _w = jnp.asarray

    def _rec_inputs():
        import jax
        import jax.numpy as jnp
        _rk = jax.random.key(seed)
        x = jax.random.randint(jax.random.fold_in(_rk, 1), (64, 128), 0, 12563, jnp.int32)
        return x
    x = _rec_inputs()

    def _L0_tok_setup():
        import jax, jax.numpy as jnp
        import numpy as np
        VOCAB, N_TURNS, OUT_DIM, POLY_DEG, MAX_POS = (50257, 8, 192, 4, 512)
        B, S = (16, 512)
        LN_EPS = 1e-12
        key = jax.random.key(seed)
        k1, k2, k3, k4 = jax.random.split(key, 4)
        turns = jax.random.randint(k1, (VOCAB, N_TURNS), -10, 11).astype(jnp.float32)
        poly_coeffs = jax.random.normal(k2, (N_TURNS, POLY_DEG + 1, OUT_DIM), dtype=jnp.float32) * 0.02
        pos_table = jax.random.normal(k3, (MAX_POS, OUT_DIM), dtype=jnp.float32) * 0.02
        ln_gamma = jnp.ones((OUT_DIM,), dtype=jnp.float32)
        ln_beta = jnp.zeros((OUT_DIM,), dtype=jnp.float32)
        input_ids = jax.random.randint(k4, (B, S), 0, VOCAB)
        return {'turns': turns, 'poly_coeffs': poly_coeffs, 'pos_table': pos_table, 'ln_gamma': ln_gamma, 'ln_beta': ln_beta, 'input_ids': input_ids}
    _L0_tok_all = _L0_tok_setup()
    _L0_tok_in = {k: v for k, v in _L0_tok_all.items() if k in ('turns', 'poly_coeffs', 'pos_table', 'ln_gamma', 'ln_beta')}
    del _L0_tok_all

    def _L0_attn_setup():
        import jax, jax.numpy as jnp
        import numpy as np
        DIM = 192
        H = 12
        HD = DIM // H
        LAMBDA_INIT = 0.1
        EPS = 1e-06

        def _qkv(x, W):
            B, N, C = x.shape
            qkv = (x @ W).reshape(B, N, 3, H, HD).transpose(2, 0, 3, 1, 4)
            return (qkv[0], qkv[1], qkv[2])
        key = jax.random.key(seed)
        ks = jax.random.split(key, 6)
        B, N = (2, 512)
        x = jax.random.normal(ks[0], (B, N, DIM), dtype=jnp.float32)
        xpos = jnp.broadcast_to(jnp.arange(N, dtype=jnp.int64), (B, N))
        s = 1.0 / np.sqrt(DIM)
        W_qkv1 = jax.random.normal(ks[1], (DIM, 3 * DIM), dtype=jnp.float32) * s
        W_qkv2 = jax.random.normal(ks[2], (DIM, 3 * DIM), dtype=jnp.float32) * s
        W_proj = jax.random.normal(ks[3], (DIM, DIM), dtype=jnp.float32) * s
        b_proj = jnp.zeros((DIM,), dtype=jnp.float32)
        norm_w = jnp.ones((DIM,), dtype=jnp.float32)
        lambda_1 = jnp.ones((H,), dtype=jnp.float32)
        lambda_2 = jnp.full((H,), 1.0 - LAMBDA_INIT * (1.0 / 12.0), dtype=jnp.float32)
        return {'x': x, 'W_qkv1': W_qkv1, 'W_qkv2': W_qkv2, 'W_proj': W_proj, 'b_proj': b_proj, 'norm_w': norm_w, 'lambda_1': lambda_1, 'lambda_2': lambda_2, 'xpos': xpos}
    _L0_attn_all = _L0_attn_setup()
    _L0_attn_in = {k: v for k, v in _L0_attn_all.items() if k in ('W_qkv1', 'W_qkv2', 'W_proj', 'b_proj', 'norm_w', 'lambda_1', 'lambda_2', 'xpos')}
    del _L0_attn_all

    def _L0_ffn_setup():
        import jax, jax.numpy as jnp
        import numpy as np
        B, T, E = (2, 256, 192)
        H = 768
        N_EXP = 4
        key = jax.random.key(seed)
        ks = jax.random.split(key, 8)
        s_e = 1.0 / np.sqrt(E)
        s_h = 1.0 / np.sqrt(H)
        return {'x': jax.random.normal(ks[0], (B, T, E), dtype=jnp.float32), 'Wg': jax.random.uniform(ks[1], (E, N_EXP), minval=-s_e, maxval=s_e, dtype=jnp.float32), 'bg': jax.random.uniform(ks[2], (N_EXP,), minval=-s_e, maxval=s_e, dtype=jnp.float32), 'W1': jax.random.uniform(ks[3], (N_EXP, E, H), minval=-s_e, maxval=s_e, dtype=jnp.float32), 'b1': jax.random.uniform(ks[4], (N_EXP, H), minval=-s_e, maxval=s_e, dtype=jnp.float32), 'W2': jax.random.uniform(ks[5], (N_EXP, H, E), minval=-s_h, maxval=s_h, dtype=jnp.float32), 'b2': jax.random.uniform(ks[6], (N_EXP, E), minval=-s_h, maxval=s_h, dtype=jnp.float32)}
    _L0_ffn_all = _L0_ffn_setup()
    _L0_ffn_in = {k: v for k, v in _L0_ffn_all.items() if k in ('Wg', 'bg', 'W1', 'b1', 'W2', 'b2')}
    del _L0_ffn_all
    return {'x': x, 'L0_tok_turns': _L0_tok_in['turns'], 'L0_tok_poly_coeffs': _L0_tok_in['poly_coeffs'], 'L0_tok_pos_table': _L0_tok_in['pos_table'], 'L0_tok_ln_gamma': _L0_tok_in['ln_gamma'], 'L0_tok_ln_beta': _L0_tok_in['ln_beta'], 'L0_attn_W_qkv1': _L0_attn_in['W_qkv1'], 'L0_attn_W_qkv2': _L0_attn_in['W_qkv2'], 'L0_attn_W_proj': _L0_attn_in['W_proj'], 'L0_attn_b_proj': _L0_attn_in['b_proj'], 'L0_attn_norm_w': _L0_attn_in['norm_w'], 'L0_attn_lambda_1': _L0_attn_in['lambda_1'], 'L0_attn_lambda_2': _L0_attn_in['lambda_2'], 'L0_attn_xpos': _L0_attn_in['xpos'], 'L0_ffn_Wg': _L0_ffn_in['Wg'], 'L0_ffn_bg': _L0_ffn_in['bg'], 'L0_ffn_W1': _L0_ffn_in['W1'], 'L0_ffn_b1': _L0_ffn_in['b1'], 'L0_ffn_W2': _L0_ffn_in['W2'], 'L0_ffn_b2': _L0_ffn_in['b2']}

def reference(x, L0_tok_turns, L0_tok_poly_coeffs, L0_tok_pos_table, L0_tok_ln_gamma, L0_tok_ln_beta, L0_attn_W_qkv1, L0_attn_W_qkv2, L0_attn_W_proj, L0_attn_b_proj, L0_attn_norm_w, L0_attn_lambda_1, L0_attn_lambda_2, L0_attn_xpos, L0_ffn_Wg, L0_ffn_bg, L0_ffn_W1, L0_ffn_b1, L0_ffn_W2, L0_ffn_b2):
    import jax
    import jax.numpy as jnp

    def _L0_tok_ref(turns, poly_coeffs, pos_table, ln_gamma, ln_beta, input_ids):
        import jax, jax.numpy as jnp
        import numpy as np
        VOCAB, N_TURNS, OUT_DIM, POLY_DEG, MAX_POS = (50257, 8, 192, 4, 512)
        B, S = (16, 512)
        LN_EPS = 1e-12
        b, s = input_ids.shape
        x = turns[input_ids]
        powers = x[..., None] ** jnp.arange(POLY_DEG + 1, dtype=x.dtype)
        emb = jnp.einsum('bstp,tpd->bsd', powers, poly_coeffs)
        emb = emb + pos_table[:s][None, :, :]
        mu = jnp.mean(emb, axis=-1, keepdims=True)
        var = jnp.mean(jnp.square(emb - mu), axis=-1, keepdims=True)
        out = (emb - mu) * jax.lax.rsqrt(var + LN_EPS) * ln_gamma + ln_beta
        return out

    def _L0_attn_ref(x, W_qkv1, W_qkv2, W_proj, b_proj, norm_w, lambda_1, lambda_2, xpos):
        import jax, jax.numpy as jnp
        import numpy as np
        DIM = 192
        H = 12
        HD = DIM // H
        LAMBDA_INIT = 0.1
        EPS = 1e-06

        def _qkv(x, W):
            B, N, C = x.shape
            qkv = (x @ W).reshape(B, N, 3, H, HD).transpose(2, 0, 3, 1, 4)
            return (qkv[0], qkv[1], qkv[2])
        B, N, C = x.shape
        scale = HD ** (-0.5)
        q1, k1, v1 = _qkv(x, W_qkv1)
        q2, k2, v2 = _qkv(x, W_qkv2)
        attn1 = jax.nn.softmax(jnp.einsum('bhnd,bhmd->bhnm', q1, k1) * scale, axis=-1)
        attn2 = jax.nn.softmax(jnp.einsum('bhnd,bhmd->bhnm', q2, k2) * scale, axis=-1)
        lam = (lambda_1 - lambda_2 + LAMBDA_INIT)[None, :, None, None]
        diff_attn = attn1 - lam * attn2
        out = jnp.einsum('bhnm,bhmd->bhnd', diff_attn, v1)
        out = out.transpose(0, 2, 1, 3).reshape(B, N, C)
        o32 = out.astype(jnp.float32)
        rms = jax.lax.rsqrt(jnp.mean(o32 * o32, axis=-1, keepdims=True) + EPS)
        out = (o32 * rms * norm_w).astype(out.dtype)
        return out @ W_proj + b_proj

    def _L0_ffn_ref(x, Wg, bg, W1, b1, W2, b2):
        import jax, jax.numpy as jnp
        import numpy as np
        B, T, E = (2, 256, 192)
        H = 768
        N_EXP = 4
        gate_logits = jnp.einsum('bte,en->btn', x, Wg) + bg
        top = jnp.argmax(gate_logits, axis=-1)
        h = jax.nn.gelu(jnp.einsum('bte,neh->nbth', x, W1) + b1[:, None, None, :], approximate=False)
        y = jnp.einsum('nbth,nhe->nbte', h, W2) + b2[:, None, None, :]
        onehot = jax.nn.one_hot(top, N_EXP, dtype=x.dtype)
        out = jnp.einsum('nbte,btn->bte', y, onehot)
        return out
    h = _L0_tok_ref(L0_tok_turns, L0_tok_poly_coeffs, L0_tok_pos_table, L0_tok_ln_gamma, L0_tok_ln_beta, x)
    h = h + _L0_attn_ref(_layernorm(h, axis=-1), L0_attn_W_qkv1, L0_attn_W_qkv2, L0_attn_W_proj, L0_attn_b_proj, L0_attn_norm_w, L0_attn_lambda_1, L0_attn_lambda_2, L0_attn_xpos)
    h = h + _L0_ffn_ref(_layernorm(h, axis=-1), L0_ffn_Wg, L0_ffn_bg, L0_ffn_W1, L0_ffn_b1, L0_ffn_W2, L0_ffn_b2)
    return h

_drawn_inputs = setup_inputs


def setup_inputs(seed=0):
    import zlib

    import numpy as np

    out = dict(_drawn_inputs(seed))
    spreads = {'L0_tok_ln_gamma': (1.0, 0.2),
     'L0_tok_ln_beta': (0.0, 0.1),
     'L0_attn_b_proj': (0.0, 0.1),
     'L0_attn_norm_w': (1.0, 0.2),
     'L0_attn_lambda_1': (1.0, 0.2),
     'L0_attn_lambda_2': (0.9916666746139526, 0.2)}
    factors = {'L0_tok_pos_table': 200.0, 'L0_ffn_b1': 5.924, 'L0_ffn_b2': 3.973}
    for name, (base, spread) in spreads.items():
        noise = np.random.default_rng([zlib.crc32(name.encode()), seed]).standard_normal(out[name].shape)
        drawn = base * np.exp(spread * noise) if base else spread * noise
        out[name] = jnp.asarray(drawn.astype(out[name].dtype))
    for name, factor in factors.items():
        out[name] = (out[name] * factor).astype(out[name].dtype)
    return out
```

```python
from contextlib import ExitStack

import concourse.bass as bass
from concourse import mybir

ALU = mybir.AluOpType
ACT = mybir.ActivationFunctionType
AX = mybir.AxisListType
F32 = mybir.dt.float32
F16 = mybir.dt.float16
I32 = mybir.dt.int32

P = 128
NB = 64
GB = 2
NG = NB // GB
GT = GB * P
D = 192
TAIL = D - P
HEADS, HD = 12, 16
VH = 2 * HEADS
PAIRS = VH // 2
CH = 6
NCH = CH * GB
TURNS, POLY = 8, 5
SPLIT = 2 * D
QK = 4 * D
WC = QK + D
HIDDEN, EXPERTS = 768, 4
HT = HIDDEN // P
TOK = NB * P
TILE = 256
TILES = TOK // TILE + EXPERTS - 1
CAP = TOK + TILE
ROWS = EXPERTS * CAP + TILE
ROW = D + D + 16
NO_TOKEN = 1 << 20
IDW = 2 * D
SCALE = HD ** -0.5
MAXT = TOK // TILE
STAGE = EXPERTS * 2 * HIDDEN + EXPERTS * HIDDEN // P * D
SLOTS = NCH
LAG_T, LAG_PV = 17, 19

PE_TASKS = [
    (0, "F3", 1, "A"), (1, "NM", -1, "B"), (1, "F4", 1, "A"), (2, "KO", -2, "B", 1), (2, "F5", 1, "A"),
    (3, "RK", -4, "B"), (3, "F6", 1, "A"), (4, "F1", 2, "B"), (4, "KT", -3, "A"), (5, "KO", -2, "B", 2),
    (6, "F2", 2, "B"), (6, "KP", -3, "A"), (7, "V", 1, "A"), (8, "KO", -2, "B", 3), (10, "KG", -3, "A"),
    (11, "KO", -1, "B", 0), (11, "GL", -3, "B"),
]
READ_BY = {"F1": ("pwT_ready", 1, 1), "F2": ("emb_set", 1, 1), "F3": ("xT_ready", 1, 1), "F4": ("qkl_set", 3, 1),
           "F5": ("qkl_set", 3, 2), "F6": ("qkl_set", 3, 3), "V": ("v_set", 1, 1), "NM": ("nmT_set", 1, 1),
           "KO0": ("o1_set", 2, 1), "KO1": ("o2_set", 2, 1), "KO2": ("o1_set", 2, 2), "KO3": ("o2_set", 2, 2),
           "RK": ("base_set", 1, 1), "KT": ("oT_set", 1, 1), "KP": ("h1_set", 2, 2), "KG": ("gT_set", 1, 1),
           "GL": ("lg_set", 1, 1)}
FIRST, LAST = -3, NG + 3
LOOP0, UNROLL = 6, 3
TRIPS = (NG - 3 - LOOP0) // UNROLL
UNROLL_B, LOOP0_B = 4, 3
TRIPS_B = (TILES - 1 - LOOP0_B) // UNROLL_B


class At:

    def __init__(self, it, const, count=NG, unroll=UNROLL):
        self.it, self.const, self.count, self.unroll = it, const, count, unroll

    def active(self, off):
        return self.it is not None or 0 <= self.const + off < self.count

    def before(self):
        return At(self.it, self.const - 1, self.count, self.unroll)

    def par(self, off, n=3):
        return (self.const + off) % n

    def val(self, off, mul, add):
        v = mul * (self.const + off) + add
        assert self.it is None or v > 0
        return v if self.it is None else self.it * (self.unroll * mul) + v

    def turned(self, off, per, n=3):
        v = per * ((self.const + off) // n + 1)
        assert self.it is None or v > 0
        return v if self.it is None else self.it * (self.unroll // n * per) + v


def ge(eng, sem, value):
    if not isinstance(value, int) or value > 0:
        eng.wait_ge(sem, value)


def over_steps(eng, step):
    for s in range(FIRST, LOOP0):
        step(At(None, s))
    with eng.Fori(0, TRIPS) as it:
        for j in range(UNROLL):
            step(At(it, LOOP0 + j))
    for s in range(LOOP0 + UNROLL * TRIPS, LAST + 1):
        step(At(None, s))


def over_tiles(eng, step):
    for s in range(-1, LOOP0_B):
        step(At(None, s, TILES, UNROLL_B))
    with eng.Fori(0, TRIPS_B) as it:
        for j in range(UNROLL_B):
            step(At(it, LOOP0_B + j, TILES, UNROLL_B))
    for s in range(LOOP0_B + UNROLL_B * TRIPS_B, TILES + 1):
        step(At(None, s, TILES, UNROLL_B))


def chunk_of(slot, lag):
    n = slot - lag
    return n // NCH, n % NCH


def build(nc, x, turns, poly, pos_table, ln_gamma, ln_beta, w_qkv1, w_qkv2, w_proj, b_proj, norm_w,
          lambda_1, lambda_2, xpos, wg, bg, w1, b1, w2, b2, out):
    ctx = ExitStack()
    with ctx:
        def sb(name, shape, dt):
            return ctx.enter_context(nc.sbuf_tensor(name, shape, dt))

        def bank(name, dt=F32):
            return ctx.enter_context(nc.psum_tensor(name, [P, 2048 // (4 if dt == F32 else 2)], dt))

        def sem(name):
            return ctx.enter_context(nc.semaphore(name))

        def mid(ap, n):
            return ap.unsqueeze(1).broadcast_to([ap.shape[0], n, ap.shape[1]])

        def last(ap, n):
            return ap.unsqueeze(len(ap.shape)).broadcast_to([*ap.shape, n])

        ident = sb("ident", [P, P], F32)
        ident16 = sb("ident16", [P, P], F16)
        earlier = sb("earlier", [P, P], F16)
        ones16 = sb("ones16", [P, P], F16)
        token_no = sb("token_no", [P, NB], I32)
        x_in = sb("x_in", [NB, P], I32)
        x_f = sb("x_f", [NB, P], F32)
        ids = sb("ids", [P, NB], I32)
        poly_sb = sb("poly_sb", [TURNS * POLY, D], F32)
        pos_sb = sb("pos_sb", [P, D], F32)
        gamma = sb("gamma", [P, D], F32)
        beta = sb("beta", [P, D], F32)
        bproj = sb("bproj", [P, D], F32)
        lam = sb("lam", [P, HEADS], F32)
        lam2 = sb("lam2", [P, HEADS], F32)
        bgate = sb("bgate", [P, EXPERTS], F32)
        normw = sb("normw", [P, 2], F32)
        mhalf = sb("mhalf", [P, GB], F32)
        wst = sb("wst", [P, 2, WC], F32)
        wqkv = sb("wqkv", [P, 2, 2, WC], F16)
        wpst = sb("wpst", [P, 2, D], F32)
        wp = sb("wp", [P, 2, 2, D], F16)
        wgst = sb("wgst", [P, 2, EXPERTS], F32)
        wgs = sb("wgs", [P, 2, 2, EXPERTS], F16)
        zrow = sb("zrow", [PAIRS, GT], F16)

        idx = sb("idx", [P, 3, GB], I32)
        turn = sb("turn", [P, 3, GB, TURNS], F32)
        powers = sb("powers", [P, GB, TURNS, POLY], F32)
        powersT = sb("powersT", [TURNS * POLY, GT], F32)
        emb = sb("emb", [P, GB, D], F32)
        bst = sb("bst", [P, GB, 6], F32)
        mv1 = sb("mv1", [P, GB, 2], F32)
        mv2 = sb("mv2", [P, GB, 2], F32)
        mv3 = sb("mv3", [P, GB, 2], F32)
        bst2 = sb("bst2", [P, GB, 6], F32)
        bst3 = sb("bst3", [P, GB, 6], F32)
        rs1 = sb("rs1", [P, 2, GB], F32)
        rs2 = sb("rs2", [P, 2, GB], F32)
        rs3 = sb("rs3", [P, 2, GB], F32)
        rms = sb("rms", [P, 2, GB], F32)
        sumsq = sb("sumsq", [P, GB], F32)
        sq = sb("sq", [P, GB, D], F32)
        e1 = sb("e1", [P, GB, D], F32)
        e2 = sb("e2", [P, GB, D], F32)
        h0 = sb("h0", [P, GB, D], F32)
        hb = sb("hb", [P, NB, D], F32)
        xn = sb("xn", [P, GB, D], F32)
        xs = sb("xs", [P, GB, SPLIT], F16)
        xT = sb("xT", [P, 3, GT], F16)
        qkh = sb("qkh", [P, 6, GT], F16)
        qkl = sb("qkl", [P, 6, GT], F16)
        Qs_all = sb("Qs_all", [P, 3, PAIRS, 2, GT], F16)
        Ks_all = sb("Ks_all", [P, 3, PAIRS, GT], F16)
        Qs = [Qs_all[:, c] for c in range(3)]
        Ks = [Ks_all[:, c] for c in range(3)]
        Vx = [sb(f"Vx{c}", [P, GB, HEADS, HD + 1], F32) for c in range(3)]
        nm = [sb(f"nm{c}", [P, GB, 2, PAIRS], F16) for c in range(3)]
        nmT = sb("nmT", [VH, GT], F16)
        probs = [sb(f"probs{c}", [P, 512], F32) for c in range(4)]
        ot = [sb(f"ot{c}", [P, 3 * P], F32) for c in range(2)]
        rc1 = sb("rc1", [P, HEADS], F32)
        rc2 = sb("rc2", [P, 2, HEADS], F32)
        o1 = sb("o1", [P, HEADS, HD], F32)
        o2 = sb("o2", [P, HEADS, HD], F32)
        oo = sb("oo", [P, GB, D], F32)
        os16 = sb("os16", [P, GB, SPLIT], F16)
        oT = sb("oT", [P, 3, GT], F16)
        row = [sb(f"row{c}", [P, GB, ROW], F32) for c in range(4)]
        xn3 = sb("xn3", [P, GB, D], F32)
        gT = sb("gT", [P, 3, GT], F16)
        ekey = sb("ekey", [P, EXPERTS], F32)
        ekey_i = sb("ekey_i", [P, EXPERTS], I32)
        base_i = sb("base_i", [P, EXPERTS], I32)
        base = sb("base", [P, GB, EXPERTS], F32)
        lg = sb("lg", [P, GB, EXPERTS], F32)
        top = sb("top", [P, GB], F32)
        hit = sb("hit", [P, GB, EXPERTS], F32)
        best = sb("best", [P, GB], F32)
        chosen = sb("chosen", [P, GB, EXPERTS], F16)
        where = sb("where", [P, GB, EXPERTS], F32)
        where2 = sb("where2", [P, GB, EXPERTS], F32)
        slot_f = sb("slot_f", [P, GB], F32)
        slot_i = [sb(f"slot_i{c}", [P, GB], I32) for c in range(3)]

        b1r = sb("b1r", [EXPERTS * HT, P], F32)
        b1T = sb("b1T", [P, EXPERTS * HT], F32)
        b2_sb = sb("b2_sb", [P, EXPERTS * D], F32)
        steps_i = sb("steps_i", [1, MAXT + TILES], I32)
        steps_f = sb("steps_f", [1, MAXT + TILES], F32)
        first_row = sb("first_row", [P, EXPERTS], F32)
        cnt = sb("cnt", [1, EXPERTS], F32)
        over = sb("over", [1, EXPERTS, MAXT], F32)
        tl = sb("tl", [1, EXPERTS], F32)
        cum = sb("cum", [1, EXPERTS], F32)
        past = sb("past", [1, TILES, EXPERTS], F32)
        skips = sb("skips", [1, TILES, EXPERTS], F32)
        ef = sb("ef", [1, TILES], F32)
        skip = sb("skip", [1, TILES], F32)
        tr = [sb(f"tr{c}", [1, TILES], F32) for c in range(5)]
        tab_e = sb("tab_e", [1, TILES], I32)
        tab_row = sb("tab_row", [1, TILES], I32)
        pad_at = sb("pad_at", [1, EXPERTS], I32)

        stage = hb[:, 0:STAGE // D, :].rearrange("p n d -> p (n d)")
        W1N, W2N = EXPERTS * 2 * HIDDEN, EXPERTS * HT * D
        stage1 = stage[:, 0:W1N].rearrange("p (e r h) -> p e r h", e=EXPERTS, r=2)
        stage2 = stage[:, W1N:W1N + W2N].rearrange("p (e n) -> p e n", e=EXPERTS)
        w1f = Qs_all[:, 0:2].rearrange("p c t a n -> p (c t a n)")
        w2f = Ks_all[:, :].rearrange("p c t n -> p (c t n)")
        w1s = w1f.rearrange("p (e r x h) -> p e r x h", e=EXPERTS, r=2, x=2)
        w2s = w2f.rearrange("p (e x n) -> p e x n", e=EXPERTS, x=2)
        hid = Qs[2].rearrange("p t a n -> p (t a n)").rearrange("p (c x k n) -> p c x k n", c=2, x=2, k=HT)
        xe, xn_e, ysum = (xT, oT), (xn, xn3), e1

        s_bank = [bank(f"s_bank{c}") for c in range(2)]
        t_bank = [bank(f"t_bank{c}") for c in range(2)]
        o_bank = [bank(f"o_bank{c}") for c in range(2)]
        misc = {"A": bank("misc_a"), "B": bank("misc_b")}
        u_bank = s_bank + t_bank

        qk_dram = nc.dram_tensor("qk_dram", [2, QK, GT], F16, kind="Internal").ap()
        routed = nc.dram_tensor("routed", [ROWS, ROW], F32, kind="Internal").ap()

        names = ("x_in_done consts_in w_in wp_in setup_pool ids_t ids_x ids_done setup_dve w_scaled vx_set zero_set "
                 "idx_set pw_set pw1 pw2 pw_ready f1_ready pwT_ready f2_ready emb_set st1_set mv1_set v1_set rs1_set e1_set "
                 "gm_set h0_set hb_set st2_set mv2_set v2_set rs2_set xn_set xh_set xs_set f3_ready xT_ready f4_ready qkh_set qkl_set "
                 "v_ready v_set scr_w s_ready s_used nm_ready nmT_set t_ready p_ready pv_done o_set ko_ready rc_set o1_set rc2_set "
                 "o2_set oo_set sq_set rq_set rms_set oh_set os_set kt_ready oT_set kp_ready h1_set st3_set mv3_set v3_set rs3_set xn3_set "
                 "x3h_set x3_set kg_ready gT_set gl_ready lg_set top_set hit_set best_set chosen_set rk_ready wh_set wh2_set "
                 "slotf_set slot_set base_set base1_set id_set waits_apart "
                 "b1_in b1_ready table table_set pads_out ffn_in w1h_set w2h_set w1l_set w2l_set ffn_set "
                 "tT_ready xe_set u_ready g_set hh_set hl_set dn_ready ysum_set y_set").split()
        S = {n: sem(n) for n in names}
        turns_in = [sem(f"turns_in{c}") for c in range(3)]
        ops_in = [sem(f"ops_in{c}") for c in range(3)]
        nm_in = [sem(f"nm_in{c}") for c in range(3)]
        rows_out = [sem(f"rows_out{c}") for c in range(3)]
        tile_in = [sem(f"tile_in{c}") for c in range(4)]
        outs = [sem(f"outs{c}") for c in range(2)]

        def apart(eng, sem_, value):
            if isinstance(value, int):
                ge(eng, sem_, value)
            else:
                eng.wait_ge(sem_, value).then_inc(S["waits_apart"], 1)

        block = ctx.enter_context(nc.Block())

        @block.sync
        def _(sp):
            sp.dma_start(x_in[:, :], x).then_inc(S["x_in_done"], 16)
            segs = [(w_qkv1, 0, 0), (w_qkv2, 0, D), (w_qkv1, D, 2 * D), (w_qkv2, D, 3 * D), (w_qkv1, 2 * D, 4 * D)]
            for w, c0, d0 in segs:
                sp.dma_start(wst[:, 0, d0:d0 + D], w[0:P, c0:c0 + D]).then_inc(S["w_in"], 16)
                for r in (0, TAIL):
                    sp.dma_start(wst[r:r + TAIL, 1, d0:d0 + D], w[P:D, c0:c0 + D]).then_inc(S["w_in"], 16)
            sp.dma_start(b1r[:, :], b1.rearrange("e (t p) -> (e t) p", p=P)).then_inc(S["b1_in"], 16)
            n = 0
            for to, of in ((poly_sb[:, :], poly.rearrange("t p d -> (t p) d")), (pos_sb[:, :], pos_table[0:P, :]),
                           (gamma[:, :], ln_gamma.partition_broadcast(P)), (beta[:, :], ln_beta.partition_broadcast(P)),
                           (bproj[:, :], b_proj.partition_broadcast(P)), (lam[:, :], lambda_1.partition_broadcast(P)),
                           (lam2[:, :], lambda_2.partition_broadcast(P)), (bgate[:, :], bg.partition_broadcast(P)),
                           (normw[:, 0:1], norm_w[0:P].unsqueeze(1)), (normw[0:TAIL, 1:2], norm_w[P:D].unsqueeze(1)),
                           (normw[TAIL:P, 1:2], norm_w[P:D].unsqueeze(1)),
                           (wpst[:, 0, :], w_proj[0:P, :]), (wpst[0:TAIL, 1, :], w_proj[P:D, :]),
                           (wpst[TAIL:P, 1, :], w_proj[P:D, :]),
                           (wgst[:, 0, :], wg[0:P, :]), (wgst[0:TAIL, 1, :], wg[P:D, :]), (wgst[TAIL:P, 1, :], wg[P:D, :]),
                           (b2_sb[:, :], b2.rearrange("e d -> (e d)").partition_broadcast(P))):
                sp.dma_start(to, of).then_inc(S["consts_in"], 16)
                n += 1
            assert n == 18
            ge(sp, S["zero_set"], 1)

            def fixed(value):
                return value if isinstance(value, int) else sp.snap(value)

            def step(at):
                v_nm, v_qk = fixed(at.val(-1, 1, 1)), fixed(at.val(1, 3, 3))
                v_scr, v_t = fixed(at.val(1, 32, 32)), fixed(at.val(1, NCH, -2 * NCH))
                neg_max(at, v_nm)
                if at.active(1):
                    apart(sp, S["qkh_set"], v_qk)
                    apart(sp, S["qkl_set"], v_qk)
                if at.active(1):
                    ge(sp, S["t_ready"], v_t)
                    for part, t in ((0, qkh), (1, qkl)):
                        sp.dma_start(qk_dram[part].rearrange("(t p) n -> p t n", p=P), t[:, :, :]).then_inc(S["scr_w"], 16)
                    ge(sp, S["scr_w"], v_scr)
                    c = at.par(1)
                    for side, (dst, parts) in enumerate((("q", (0, 0, 1)), ("k", (0, 1, 0)))):
                        for a in range(2):
                            for r, part in enumerate(parts):
                                rows = slice(64 * a + HD * r, 64 * a + HD * r + HD)
                                src = qk_dram[part, side * 2 * D:(side + 1) * 2 * D].rearrange(
                                    "(p a d) n -> a d p n", a=2, d=HD)[a]
                                to = Qs[c][rows, :, a, :] if dst == "q" else Ks[c][rows, :, :]
                                sp.dma_start(to, src).then_inc(ops_in[c], 16)
                    for a in range(2):
                        sp.dma_start(Qs[c][64 * a + 48:64 * a + 49, :, a, :], zrow[:, :]).then_inc(ops_in[c], 16)

            def neg_max(at, v_nm):
                if at.active(-1):
                    c = at.par(-1)
                    ge(sp, S["nmT_set"], v_nm)
                    for a in range(2):
                        sp.dma_start(Qs[c][64 * a + 48:64 * a + 49, :, a, :],
                                     nmT[PAIRS * a:PAIRS * a + PAIRS, :]).then_inc(nm_in[c], 16)

            over_steps(sp, step)
            sp.wait_ge(S["h1_set"], STAGE // D)
            sp.dma_start(stage1[:, :, 0, :], w1[:, 0:P, :].rearrange("e p h -> p e h")).then_inc(S["ffn_in"], 16)
            for r in (0, TAIL):
                sp.dma_start(stage1[r:r + TAIL, :, 1, :], w1[:, P:D, :].rearrange("e p h -> p e h"))\
                    .then_inc(S["ffn_in"], 16)
            sp.dma_start(stage2.rearrange("p e (k d) -> p e k d", d=D), w2.rearrange("e (k p) d -> p e k d", p=P))\
                .then_inc(S["ffn_in"], 16)
            sp.wait_ge(S["table_set"], 3)
            for e in range(EXPERTS):
                start = sp.value_load(pad_at[0:1, e:e + 1], min_val=e * CAP, max_val=e * CAP + TOK)
                sp.dma_start(routed[bass.ds(start, TILE)].rearrange("(p j) w -> p j w", j=2), row[3][:, :, :])\
                    .then_inc(S["pads_out"], 16)
            sp.dma_start(routed[EXPERTS * CAP:ROWS].rearrange("(p j) w -> p j w", j=2), row[3][:, :, :])\
                .then_inc(S["pads_out"], 16)
            sp.wait_ge(S["pads_out"], 16 * (EXPERTS + 1))
            for c in range(3):
                sp.wait_ge(rows_out[c], 32 * ((NG - 1 - c) // 3 + 1))

            def load(at):
                if at.active(0):
                    c = at.par(0, 4)
                    start = sp.value_load(tab_row[0:1, bass.ds(at.val(0, 1, 0), 1)], min_val=0, max_val=EXPERTS * CAP)
                    if at.it is not None or at.const >= 4:
                        ge(sp, outs[at.par(0, 2)], at.turned(-4, 32, 2))
                    sp.dma_start(row[c][:, :, :], routed[bass.ds(start, TILE)].rearrange("(p j) w -> p j w", j=2))\
                        .then_inc(tile_in[c], 16)

            for t in range(4):
                load(At(None, t, TILES, UNROLL_B))
            with sp.Fori(0, TILES // 4 - 1) as it:
                for j in range(4):
                    load(At(it, 4 + j, TILES, UNROLL_B))
            for t in range(TILES // 4 * 4, TILES):
                load(At(None, t, TILES, UNROLL_B))
            for c in range(2):
                sp.wait_ge(outs[c], 32 * ((TILES - 1 - c) // 2 + 1))

        @block.gpsimd
        def _(pool):
            nsetup = 0

            def setup(ins):
                nonlocal nsetup
                nsetup += 1
                ins.then_inc(S["setup_pool"], 1)

            setup(pool.memset(ident[:, :], 0.0))
            setup(pool.memset(ident16[:, :], 0.0))
            setup(pool.memset(earlier[:, :], 1.0))
            setup(pool.memset(ones16[:, :], 1.0))
            setup(pool.memset(mhalf[:, :], -0.5))
            setup(pool.memset(powers[:, :, :, 0:1], 1.0))
            setup(pool.iota(token_no[:, :], pattern=[[P, NB]], base=0, channel_multiplier=1))
            setup(pool.iota(ekey_i[:, :], pattern=[[-1, EXPERTS]], base=EXPERTS, channel_multiplier=0))
            setup(pool.iota(base_i[:, :], pattern=[[CAP, EXPERTS]], base=0, channel_multiplier=0))
            setup(pool.iota(steps_i[:, 0:MAXT], pattern=[[TILE, MAXT]], base=0, channel_multiplier=0))
            setup(pool.iota(steps_i[:, MAXT:], pattern=[[1, TILES]], base=0, channel_multiplier=0))
            pool.wait_ge(S["setup_pool"], nsetup)
            for m in (ident, ident16):
                setup(pool.affine_select(out=m[:, :], in_=m[:, :], compare_op=ALU.not_equal, fill=1.0, base=0,
                                         pattern=[[-1, P]], channel_multiplier=1))
            setup(pool.affine_select(out=earlier[:, :], in_=earlier[:, :], compare_op=ALU.is_ge, fill=0.0, base=-1,
                                     pattern=[[1, P]], channel_multiplier=-1))
            assert nsetup == 14
            pool.memset(zrow[:, :], 0.0).then_inc(S["vx_set"], 1)
            for c in range(3):
                pool.memset(row[c][:, :, IDW:ROW], 0.0).then_inc(S["vx_set"], 1)
            pool.memset(row[3][:, :, 0:IDW], 0.0).then_inc(S["vx_set"], 1)
            pool.memset(row[3][:, :, IDW:ROW].bitcast(I32), NO_TOKEN).then_inc(S["vx_set"], 1)
            for c in range(3):
                pool.memset(Qs[c][:, :, :, :], 0.0).then_inc(S["vx_set"], 1)
            pool.wait_ge(S["vx_set"], 9)
            pool.memset(idx[:, :, :], 0).then_inc(S["zero_set"], 1)
            pool.wait_ge(S["zero_set"], 1)
            pool.wait_ge(S["ids_done"], 1)

            def rsqrt(dst, var, ready, value, mid_sem, done, eps, scale=1.0):
                apart(pool, ready, value)
                pool.tensor_scalar(dst[:, 0, :], var, scale, eps, ALU.mult, ALU.add).then_inc(mid_sem[0], 1)
                ge(pool, mid_sem[0], mid_sem[1])
                pool.tensor_tensor(dst[:, 1, :], dst[:, 0, :], mhalf[:, :], ALU.pow).then_inc(done, 1)

            def split(dst, src, half_sem, value, done):
                pool.tensor_copy(dst[:, :, 0:D], src[:, :, :]).then_inc(half_sem, 1)
                ge(pool, half_sem, value)
                pool.tensor_tensor(dst[:, :, D:D + TAIL], src[:, :, P:D], dst[:, :, P:D], ALU.subtract)\
                    .then_inc(done, 1)
                pool.tensor_tensor(dst[:, :, D + TAIL:SPLIT], src[:, :, 0:P], dst[:, :, 0:P], ALU.subtract)\
                    .then_inc(done, 1)

            def step(at):
                if at.active(2):
                    t = turn[:, at.par(2)]
                    ge(pool, turns_in[at.par(2)], at.turned(2, 32))
                    apart(pool, S["f1_ready"], at.val(2, 1, 0))
                    pool.tensor_copy(powers[:, :, :, 1], t).then_inc(S["pw_set"], 1)
                    pool.tensor_tensor(powers[:, :, :, 2], t, t, ALU.mult).then_inc(S["pw1"], 1)
                    ge(pool, S["pw1"], at.val(2, 1, 1))
                    pool.tensor_tensor(powers[:, :, :, 3], powers[:, :, :, 2], t, ALU.mult).then_inc(S["pw2"], 1)
                    pool.tensor_tensor(powers[:, :, :, 4], powers[:, :, :, 2], powers[:, :, :, 2], ALU.mult)\
                        .then_inc(S["pw_ready"], 1)
                if at.active(3):
                    c = at.par(3)
                    apart(pool, turns_in[c], at.turned(0, 32) if at.active(0) else 0)
                    pool.tensor_copy(idx[:, c, :], ids[:, bass.ds(at.val(3, GB, 0), GB)]).then_inc(S["idx_set"], 1)
                    ge(pool, S["pw_ready"], at.val(3, 1, -2))
                    apart(pool, S["idx_set"], at.val(3, 1, 1))
                    for b in range(GB):
                        pool.indirect_dma_start(
                            out=turn[:, c, b, :], out_offset=None, in_=turns,
                            in_offset=bass.IndirectOffsetOnAxis(ap=idx[:, c, b:b + 1], axis=0)).then_inc(turns_in[c], 16)
                if at.active(-4):
                    scatter(at)
                if at.active(2):
                    rsqrt(rs1, mv1[:, :, 1], S["mv1_set"], at.val(2, GB, GB), (S["v1_set"], at.val(2, 1, 1)),
                          S["rs1_set"], 1e-12)
                if at.active(-3):
                    rsqrt(rs3, mv3[:, :, 1], S["mv3_set"], at.val(-3, GB, GB), (S["v3_set"], at.val(-3, 1, 1)),
                          S["rs3_set"], 1e-5)
                if at.active(2):
                    ge(pool, S["e1_set"], at.val(2, GB, GB))
                    pool.tensor_tensor(e2[:, :, :], e1[:, :, :], mid(gamma[:, :], GB), ALU.mult).then_inc(S["gm_set"], 1)
                    ge(pool, S["gm_set"], at.val(2, 1, 1))
                    ge(pool, S["xn_set"], at.val(2, GB, 0))
                    pool.tensor_tensor(h0[:, :, :], e2[:, :, :], mid(beta[:, :], GB), ALU.add).then_inc(S["h0_set"], 1)
                    ge(pool, S["h0_set"], at.val(2, 1, 1))
                    pool.tensor_tensor(hb[:, bass.ds(at.val(2, GB, 0), GB), :], h0[:, :, :], mid(bproj[:, :], GB), ALU.add)\
                        .then_inc(S["hb_set"], 1)
                if at.active(-3):
                    c = at.par(-3)
                    apart(pool, S["xn3_set"], at.val(-3, GB, GB))
                    split(row[c][:, :, 0:D].bitcast(F16), xn3, S["x3h_set"], at.val(-3, 1, 1), S["x3_set"])
                if at.active(2):
                    rsqrt(rs2, mv2[:, :, 1], S["mv2_set"], at.val(2, GB, GB), (S["v2_set"], at.val(2, 1, 1)),
                          S["rs2_set"], 1e-5)
                if at.active(-2):
                    ge(pool, S["oo_set"], at.val(-2, GB, GB))
                    apart(pool, S["kt_ready"], at.val(-2, 1, 0))
                    split(os16, oo, S["oh_set"], at.val(-2, 1, 1), S["os_set"])
                    rsqrt(rms, sumsq[:, :], S["sq_set"], at.val(-2, GB, GB), (S["rq_set"], at.val(-2, 1, 1)),
                          S["rms_set"], 1e-6, 1.0 / D)
                if at.active(2):
                    ge(pool, S["xn_set"], at.val(2, GB, GB))
                    apart(pool, S["f3_ready"], at.val(2, 1, 0))
                    split(xs, xn, S["xh_set"], at.val(2, 1, 1), S["xs_set"])

            def scatter(at):
                c = at.par(-4)
                ge(pool, S["id_set"], at.val(-4, 1, 1))
                apart(pool, S["slot_set"], at.val(-4, 1, 1))
                for b in range(GB):
                    pool.indirect_dma_start(
                        out=routed, out_offset=bass.IndirectOffsetOnAxis(ap=slot_i[c][:, b:b + 1], axis=0),
                        in_=row[c][:, b, :], in_offset=None).then_inc(rows_out[c], 16)

            over_steps(pool, step)

            def expert_step(at):
                if at.active(0):
                    for k in range(3):
                        g = probs[(3 * at.const + k) % 4]
                        ge(pool, S["g_set"], at.val(0, 6, 2 * k + 2))
                        apart(pool, S["dn_ready"], at.val(0, 1, -1))
                        pool.tensor_copy(hid[:, at.par(0, 2), 0, 2 * k:2 * k + 2, :],
                                         g[:, :].rearrange("p (t n) -> p t n", t=2)).then_inc(S["hh_set"], 1)
                if at.active(-1):
                    c = at.par(-1, 2)
                    apart(pool, S["y_set"], at.val(-1, 1, 1))
                    for j in range(2):
                        pool.indirect_dma_start(
                            out=out.rearrange("b s d -> (b s) d"), out_offset=bass.IndirectOffsetOnAxis(
                                ap=row[at.par(-1, 4)][:, j, IDW:IDW + 1].bitcast(I32), axis=0),
                            in_=xn_e[c][:, j, :], in_offset=None, bounds_check=TOK - 1, oob_is_err=False)\
                            .then_inc(outs[c], 16)

            over_tiles(pool, expert_step)

        @block.tensor
        def _(pe):
            pe.wait_ge(S["setup_pool"], 14)
            pe.wait_ge(S["ids_x"], 1)
            pe.transpose(misc["A"][:, 0:NB], x_f[:, :], ident[0:NB, 0:NB]).then_inc(S["ids_t"], 1)
            pe.wait_ge(S["b1_in"], 16)
            pe.transpose(misc["B"][:, 0:EXPERTS * HT], b1r[:, :], ident[0:EXPERTS * HT, 0:EXPERTS * HT])\
                .then_inc(S["b1_ready"], 1)
            pe.wait_ge(S["ids_done"], 1)
            pe.wait_ge(S["setup_dve"], 1)

            def claim(at, n):
                order = [(at, t) for t in PE_TASKS[:n]][::-1] + [(at.before(), t) for t in PE_TASKS[::-1]]
                for at_, t in order:
                    if t[3] == PE_TASKS[n][3] and at_.active(t[2]):
                        name, per, nth = READ_BY[t[1] + "".join(map(str, t[4:]))]
                        ge(pe, S[name], at_.val(t[2], per, nth))
                        break
                return misc[PE_TASKS[n][3]]

            TERMS = ((0, 0, 0), (0, 0, 1), (2, 0, 0), (1, 1, 0), (1, 1, 1))

            def transposes3(dst, src, ready):
                for k in range(3):
                    for b in range(GB):
                        mm = pe.transpose(dst[:, k * GT + b * P:k * GT + b * P + P], src[:, b, k * P:k * P + P],
                                          ident16[:, :])
                mm.then_inc(ready, 1)

            def tokens_by(dst, xT_, w, n, ready):
                for b in range(GB):
                    for i, (k, r, part) in enumerate(TERMS):
                        mm = pe.matmul(dst[:, b * n:b * n + n], xT_[:, k, b * P:b * P + P], w[:, r, part],
                                       start=i == 0, stop=i == len(TERMS) - 1)
                mm.then_inc(ready, 1)

            def task(at, n):
                name, off, _, *arg = PE_TASKS[n][1:]
                if not at.active(off):
                    return
                m = claim(at, n)
                m16 = m[:, :].bitcast(F16)
                if name == "F1":
                    ge(pe, S["pw_ready"], at.val(off, 1, 1))
                    ge(pe, S["pw2"], at.val(off, 1, 1))
                    apart(pe, S["pw_set"], at.val(off, 1, 1))
                    for b in range(GB):
                        mm = pe.transpose(m[0:TURNS * POLY, b * P:b * P + P],
                                          powers[:, b].rearrange("s t p -> s (t p)"), ident[:, :])
                    mm.then_inc(S["f1_ready"], 1)
                elif name == "F2":
                    ge(pe, S["pwT_ready"], at.val(off, 1, 1))
                    for b in range(GB):
                        mm = pe.matmul(m[:, b * D:b * D + D], powersT[:, b * P:b * P + P], poly_sb[:, :],
                                       start=True, stop=True)
                    mm.then_inc(S["f2_ready"], 1)
                elif name == "F3":
                    ge(pe, S["xs_set"], at.val(off, 2, 2))
                    transposes3(m16, xs, S["f3_ready"])
                elif name in ("F4", "F5", "F6"):
                    t0 = 2 * (int(name[1]) - 4)
                    ge(pe, S["xT_ready"], at.val(off, 1, 1))
                    for t in (t0, t0 + 1):
                        for i, (k, r, part) in enumerate(TERMS):
                            mm = pe.matmul(m[:, (t - t0) * GT:(t - t0) * GT + GT], wqkv[:, r, part, t * P:t * P + P],
                                           xT[:, k, :], start=i == 0, stop=i == len(TERMS) - 1)
                    mm.then_inc(S["f4_ready"], 1)
                elif name == "V":
                    tokens_by(m, xT, wqkv[:, :, :, QK:WC], D, S["v_ready"])
                elif name == "NM":
                    ge(pe, S["s_used"], at.val(off, NCH, NCH))
                    for b in range(GB):
                        mm = pe.transpose(m16[0:VH, b * P:b * P + P],
                                          nm[at.par(off)][:, b].rearrange("n a p -> n (a p)"), ident16[:, :])
                    mm.then_inc(S["nm_ready"], 1)
                elif name == "KO":
                    w = arg[0]
                    ge(pe, S["o_set"], at.val(off, 4, w + 1))
                    for c in range(3):
                        mm = pe.transpose(m[:, c * P:c * P + P], ot[w % 2][:, c * P:c * P + P], ident[:, :])
                    mm.then_inc(S["ko_ready"], 1)
                elif name == "KT":
                    ge(pe, S["os_set"], at.val(off, 2, 2))
                    transposes3(m16, os16, S["kt_ready"])
                elif name == "KP":
                    ge(pe, S["oT_set"], at.val(off, 1, 1))
                    tokens_by(m, oT, wp, D, S["kp_ready"])
                elif name == "KG":
                    ge(pe, S["x3_set"], at.val(off, 2, 2))
                    transposes3(m16, row[at.par(off)][:, :, 0:D].bitcast(F16), S["kg_ready"])
                elif name == "GL":
                    ge(pe, S["gT_set"], at.val(off, 1, 1))
                    tokens_by(m, gT, wgs, EXPERTS, S["gl_ready"])
                elif name == "RK":
                    ge(pe, S["chosen_set"], at.val(off, 1, 1))
                    E = EXPERTS
                    both = chosen[:, :, :].rearrange("n b e -> n (b e)")
                    pe.matmul(m[:, 0:GB * E], earlier[:, :], both, start=True, stop=True)
                    pe.matmul(m[:, GB * E:2 * GB * E], ones16[:, :], both, start=True, stop=True)\
                        .then_inc(S["rk_ready"], 1)

            def step(at):
                for slot in range(SLOTS):
                    if at.active(0):
                        c, b, cc = at.par(0), slot // CH, slot % CH
                        if slot == 0:
                            ge(pe, ops_in[c], at.turned(0, 14 * 16))
                        ge(pe, S["s_used"], at.val(0, NCH, slot - 1))
                        for a in range(2):
                            for pp in range(2):
                                p = 2 * cc + pp
                                mm = pe.matmul(s_bank[slot % 2][:, (2 * a + pp) * P:(2 * a + pp) * P + P],
                                               Qs[c][:, p, a, b * P:b * P + P], Ks[c][:, p, b * P:b * P + P],
                                               start=True, stop=True)
                        mm.then_inc(S["s_ready"], 1)
                    off, k = chunk_of(slot, LAG_T)
                    if at.active(off):
                        c, b, cc = at.par(off), k // CH, k % CH
                        if k == 0:
                            ge(pe, nm_in[c], at.turned(off, 32))
                        ge(pe, S["p_ready"], at.val(off, NCH, k - 1))
                        for pp in range(2):
                            p = 2 * cc + pp
                            mm = pe.matmul(t_bank[k % 2][:, pp * 2 * P:(pp + 1) * 2 * P], Ks[c][:, p, b * P:b * P + P],
                                           Qs[c][:, p, :, b * P:b * P + P], start=True, stop=True)
                        mm.then_inc(S["t_ready"], 1)
                    off, k = chunk_of(slot, LAG_PV)
                    if at.active(off):
                        c, b, cc = at.par(off), k // CH, k % CH
                        w = k // 3
                        if k == 0:
                            ge(pe, S["v_set"], at.val(off, 1, 1))
                        if k % 3 == 0:
                            ge(pe, S["o_set"], at.val(off, 4, w - 1))
                        ge(pe, S["p_ready"], at.val(off, NCH, k + 1))
                        for j in range(4):
                            head = (4 * cc + j) % HEADS
                            mm = pe.matmul(o_bank[w % 2][32 * j:32 * j + HD + 1, (cc % 3) * P:(cc % 3) * P + P],
                                           Vx[c][:, b, head, :], probs[k % 4][:, j * P:j * P + P], start=True, stop=True)
                        mm.then_inc(S["pv_done"], 1)
                    for n, t in enumerate(PE_TASKS):
                        if t[0] == slot:
                            task(at, n)

            over_steps(pe, step)

            pe.wait_ge(S["ffn_set"], 2)

            def expert_step(at):
                if at.active(1):
                    m = misc["AB"[at.par(1, 2)]]
                    c = at.par(1, 4)
                    ge(pe, S["xe_set"], at.val(1, 1, -1))
                    ge(pe, tile_in[c], at.turned(1, 16, 4))
                    transposes3(m[:, :].bitcast(F16), row[c][:, :, 0:D].bitcast(F16), S["tT_ready"])
                if at.active(0):
                    e = pe.value_load(tab_e[0:1, bass.ds(at.val(0, 1, 0), 1)], min_val=0, max_val=EXPERTS - 1)
                    ge(pe, S["xe_set"], at.val(0, 1, 1))
                    for k in range(3):
                        bank_ = u_bank[(3 * at.const + k) % 4]
                        ge(pe, S["g_set"], at.val(0, 6, 2 * (k - 3)))
                        for t in (2 * k, 2 * k + 1):
                            for i, (ck, r, part) in enumerate(TERMS):
                                at_w = e * (4 * HIDDEN) + ((2 * r + part) * HIDDEN + t * P)
                                mm = pe.matmul(bank_[:, (t - 2 * k) * GT:(t - 2 * k + 1) * GT],
                                               w1f[:, bass.ds(at_w, P)], xe[at.par(0, 2)][:, ck, :],
                                               start=i == 0, stop=i == len(TERMS) - 1)
                        mm.then_inc(S["u_ready"], 1)
                if at.active(-1):
                    e = pe.value_load(tab_e[0:1, bass.ds(at.val(-1, 1, 0), 1)], min_val=0, max_val=EXPERTS - 1)
                    c = at.par(-1, 2)
                    ge(pe, S["hl_set"], at.val(-1, 3, 3))
                    ge(pe, S["ysum_set"], at.val(-1, 1, -1))
                    for j in range(2):
                        n, steps = 0, [(k, x, w) for k in range(HT) for x, w in ((0, 0), (0, 1), (1, 0))]
                        for n, (k, x, w) in enumerate(steps):
                            mm = pe.matmul(o_bank[c][:, j * D:j * D + D], hid[:, c, x, k, j * P:j * P + P],
                                           w2f[:, bass.ds(e * (2 * HT * D) + (w * HT + k) * D, D)],
                                           start=n == 0, stop=n == len(steps) - 1)
                    mm.then_inc(S["dn_ready"], 1)

            over_tiles(pe, expert_step)

        @block.scalar
        def _(act):
            def copy(dst, src, done):
                nc.scalar.activation(dst, src, ACT.Copy).then_inc(done, 1)

            def step(at):
                for slot in range(SLOTS):
                    off, k = chunk_of(slot, LAG_T)
                    if at.active(off):
                        ge(act, S["t_ready"], at.val(off, NCH, k + 1))
                        ge(act, S["pv_done"], at.val(off, NCH, k - 3))
                        nc.scalar.activation(probs[k % 4][:, :], t_bank[k % 2][:, :], ACT.Exp, scale=SCALE)\
                            .then_inc(S["p_ready"], 1)
                    if slot == 0 and at.active(1):
                        ge(act, S["f3_ready"], at.val(1, 1, 1))
                        ge(act, S["v_ready"], at.val(1, 1, 0))
                        copy(xT[:, :, :].rearrange("p k n -> p (k n)"), misc["A"][:, :].bitcast(F16)[:, 0:3 * GT],
                             S["xT_ready"])
                    if slot == 1 and at.active(-1):
                        ge(act, S["nm_ready"], at.val(-1, 1, 1))
                        if at.active(-2):
                            ge(act, nm_in[at.par(-2)], at.turned(-2, 32))
                        copy(nmT[:, :], misc["B"][:, :].bitcast(F16)[0:VH, 0:GT], S["nmT_set"])
                    if slot in (1, 2, 3) and at.active(1):
                        ge(act, S["f4_ready"], at.val(1, 3, slot))
                        ge(act, S["scr_w"], at.val(1, 32, 0))
                        nc.scalar.activation(qkh[:, 2 * slot - 2:2 * slot, :].rearrange("p t n -> p (t n)"), misc["A"][:, :],
                                             ACT.Copy).then_inc(S["qkh_set"], 1)
                    if slot in (1, 4, 7, 10):
                        w = {10: 0, 1: 1, 4: 2, 7: 3}[slot]
                        off = -1 if w == 0 else -2
                        if at.active(off):
                            ge(act, S["pv_done"], at.val(off, NCH, 3 * w + 3))
                            ge(act, S["ko_ready"], at.val(off, 4, w - 1))
                            copy(ot[w % 2][:, :], o_bank[w % 2][:, 0:3 * P], S["o_set"])
                    if slot == 4 and at.active(2):
                        ge(act, S["f1_ready"], at.val(2, 1, 1))
                        ge(act, S["f2_ready"], at.val(2, 1, 0))
                        copy(powersT[:, :], misc["B"][0:TURNS * POLY, 0:GT], S["pwT_ready"])
                    if slot == 4 and at.active(-3):
                        ge(act, S["kt_ready"], at.val(-3, 1, 1))
                        ge(act, S["kp_ready"], at.val(-3, 1, 0))
                        copy(oT[:, :, :].rearrange("p k n -> p (k n)"), misc["A"][:, :].bitcast(F16)[:, 0:3 * GT],
                             S["oT_set"])
                    if slot == 7 and at.active(1):
                        ge(act, S["v_ready"], at.val(1, 1, 1))
                        ge(act, S["pv_done"], at.val(1, NCH, -2 * NCH))
                        copy(Vx[at.par(1)][:, :, :, 0:HD],
                             misc["A"][:, 0:GB * D].rearrange("p (b h d) -> p b h d", b=GB, h=HEADS), S["v_set"])
                    if slot == 9 and at.active(-2):
                        ge(act, S["rq_set"], at.val(-2, 1, 0))
                        for b in range(GB):
                            ge(act, S["oo_set"], at.val(-2, GB, b + 1))
                            ge(act, S["sq_set"], at.val(-2, GB, b - 1))
                            nc.scalar.activation(sq[:, b, :], oo[:, b, :], ACT.Square,
                                                 accum_out=sumsq[:, b:b + 1]).then_inc(S["sq_set"], 1)
                    if slot == 10 and at.active(-3):
                        ge(act, S["kg_ready"], at.val(-3, 1, 1))
                        ge(act, S["gl_ready"], at.val(-3, 1, 0))
                        copy(gT[:, :, :].rearrange("p k n -> p (k n)"), misc["A"][:, :].bitcast(F16)[:, 0:3 * GT],
                             S["gT_set"])

            over_steps(act, step)

            act.wait_ge(S["ffn_in"], 64)
            act.wait_ge(S["t_ready"], NCH * NG)
            copy(w1s[:, :, :, 0, :], stage1, S["w1h_set"])
            copy(w2s[:, :, 0, :], stage2, S["w2h_set"])

            act.wait_ge(S["table_set"], 3)

            def expert_step(at):
                if at.active(1):
                    ge(act, S["tT_ready"], at.val(1, 1, 1))
                    ge(act, S["u_ready"], at.val(1, 3, -3))
                    copy(xe[at.par(1, 2)][:, :, :].rearrange("p k n -> p (k n)"),
                         misc["AB"[at.par(1, 2)]][:, :].bitcast(F16)[:, 0:3 * GT], S["xe_set"])
                if at.active(0):
                    e = act.value_load(tab_e[0:1, bass.ds(at.val(0, 1, 0), 1)], min_val=0, max_val=EXPERTS - 1)
                    for k in range(3):
                        u = (3 * at.const + k) % 4
                        ge(act, S["hl_set"], at.val(0, 3, k - 3))
                        ge(act, S["u_ready"], at.val(0, 3, k + 1))
                        for t in range(2):
                            nc.scalar.activation(probs[u][:, t * GT:t * GT + GT], u_bank[u][:, t * GT:t * GT + GT],
                                                 ACT.Gelu, bias=b1T[:, bass.ds(e * HT + (2 * k + t), 1)])\
                                .then_inc(S["g_set"], 1)

            over_tiles(act, expert_step)

        @block.vector
        def _(dve):
            V = nc.vector
            dve.wait_ge(S["x_in_done"], 16)
            V.tensor_copy(x_f[:, :], x_in[:, :]).then_inc(S["ids_x"], 1)
            dve.wait_ge(S["ids_t"], 1)
            V.tensor_copy(ids[:, :], misc["A"][:, 0:NB]).then_inc(S["ids_done"], 1)
            dve.wait_ge(S["b1_ready"], 1)
            V.tensor_copy(b1T[:, :], misc["B"][:, 0:EXPERTS * HT]).then_inc(S["w_scaled"], 1)
            dve.wait_ge(S["w_in"], 15 * 16)
            V.tensor_copy(wqkv[:, :, 0, :], wst[:, :, :]).then_inc(S["w_scaled"], 1)
            dve.wait_ge(S["consts_in"], 18 * 16)
            for r in range(2):
                V.tensor_scalar(wpst[:, r, :], wpst[:, r, :], normw[:, r:r + 1], None, ALU.mult)\
                    .then_inc(S["w_scaled"], 1)
            V.tensor_copy(wgs[:, :, 0, :], wgst[:, :, :]).then_inc(S["w_scaled"], 1)
            V.tensor_tensor(lam[:, :], lam[:, :], lam2[:, :], ALU.subtract).then_inc(S["w_scaled"], 1)
            dve.wait_ge(S["w_scaled"], 6)
            V.tensor_tensor(wqkv[:, :, 1, :], wst[:, :, :], wqkv[:, :, 0, :], ALU.subtract).then_inc(S["w_scaled"], 1)
            V.tensor_tensor(wgs[:, :, 1, :], wgst[:, :, :], wgs[:, :, 0, :], ALU.subtract).then_inc(S["w_scaled"], 1)
            V.tensor_copy(wp[:, :, 0, :], wpst[:, :, :]).then_inc(S["w_scaled"], 1)
            V.tensor_scalar(lam[:, :], lam[:, :], 0.1, None, ALU.add).then_inc(S["w_scaled"], 1)
            dve.wait_ge(S["setup_pool"], 11)
            V.tensor_copy(ekey[:, :], ekey_i[:, :]).then_inc(S["w_scaled"], 1)
            V.tensor_copy(base[:, 0, :], base_i[:, :]).then_inc(S["w_scaled"], 1)
            V.tensor_copy(first_row[:, :], base_i[:, :]).then_inc(S["w_scaled"], 1)
            V.tensor_copy(steps_f[:, :], steps_i[:, :]).then_inc(S["w_scaled"], 1)
            for c in range(3):
                V.memset(Ks[c][:, :, :], 1.0).then_inc(S["w_scaled"], 1)
                V.memset(Vx[c][:, :, :, HD:HD + 1], 1.0).then_inc(S["w_scaled"], 1)
            for c in range(2):
                V.memset(o_bank[c][:, :], 0.0).then_inc(S["w_scaled"], 1)
            dve.wait_ge(S["w_scaled"], 22)
            V.tensor_tensor(wp[:, :, 1, :], wpst[:, :, :], wp[:, :, 0, :], ALU.subtract).then_inc(S["setup_dve"], 1)

            A, B = misc["A"], misc["B"]

            def stats(src, st, mv, at, off, st_sem, mv_sem):
                for b in range(GB):
                    V.bn_stats(st[:, b, :], src[:, b, :]).then_inc(st_sem, 1)
                for b in range(GB):
                    apart(dve, st_sem, at.val(off, GB, b + 1))
                    V.bn_aggr(mv[:, b, :], st[:, b, :]).then_inc(mv_sem, 1)

            def apply(dst, src, mv, rs, done):
                for b in range(GB):
                    V.tensor_scalar(dst[:, b, :], src[:, b, :], mv[:, b, 0:1], rs[:, 1, b:b + 1],
                                    ALU.subtract, ALU.mult).then_inc(done, 1)

            def combine(at, off, w):
                b, second = w // 2, w % 2
                ge(dve, S["ko_ready"], at.val(off, 4, w + 1))
                o = B[:, 0:3 * P].rearrange("n (h r) -> n h r", r=32)
                if not second:
                    V.reciprocal(rc1[:, :], o[:, :, HD]).then_inc(S["rc_set"], 1)
                    ge(dve, S["rc_set"], at.val(off, GB, b + 1))
                    V.tensor_tensor(o1[:, :, :], o[:, :, 0:HD], last(rc1[:, :], HD), ALU.mult)\
                        .then_inc(S["o1_set"], 1)
                else:
                    V.reciprocal(rc2[:, 0, :], o[:, :, HD]).then_inc(S["rc2_set"], 1)
                    ge(dve, S["rc2_set"], at.val(off, 2 * GB, 2 * b + 1))
                    V.tensor_tensor(rc2[:, 1, :], rc2[:, 0, :], lam[:, :], ALU.mult).then_inc(S["rc2_set"], 1)
                    ge(dve, S["rc2_set"], at.val(off, 2 * GB, 2 * b + 2))
                    V.tensor_tensor(o2[:, :, :], o[:, :, 0:HD], last(rc2[:, 1, :], HD), ALU.mult)\
                        .then_inc(S["o2_set"], 1)
                    ge(dve, S["o2_set"], at.val(off, GB, b + 1))
                    ge(dve, S["o1_set"], at.val(off, GB, b + 1))
                    if b == 0:
                        ge(dve, S["os_set"], at.val(off, 2, 0))
                        ge(dve, S["sq_set"], at.val(off, GB, 0))
                    V.tensor_tensor(oo[:, b, :].rearrange("n (h d) -> n h d", d=HD), o1[:, :, :], o2[:, :, :],
                                    ALU.subtract).then_inc(S["oo_set"], 1)

            def step(at):
                for slot in range(SLOTS):
                    if at.active(0):
                        b, cc = slot // CH, slot % CH
                        ge(dve, S["s_ready"], at.val(0, NCH, slot + 1))
                        if slot == 0:
                            ge(dve, S["nm_ready"], at.val(0, 1, -2))
                        V.tensor_reduce(nm[at.par(0)][:, b, :, 2 * cc:2 * cc + 2],
                                        s_bank[slot % 2][:, :].rearrange("n (a p m) -> n a p m", a=2, p=2),
                                        AX.X, ALU.max, negate=True).then_inc(S["s_used"], 1)
                    if slot == 0 and at.active(-4):
                        ge(dve, S["gl_ready"], at.val(-4, 1, 1))
                        V.tensor_tensor(lg[:, :, :], B[:, 0:GB * EXPERTS].rearrange("n (b e) -> n b e", b=GB),
                                        mid(bgate[:, :], GB), ALU.add).then_inc(S["lg_set"], 1)
                        ge(dve, S["lg_set"], at.val(-4, 1, 1))
                        V.tensor_reduce(top[:, :], lg[:, :, :], AX.X, ALU.max).then_inc(S["top_set"], 1)
                        ge(dve, S["top_set"], at.val(-4, 1, 1))
                        V.tensor_tensor(hit[:, :, :], lg[:, :, :], last(top[:, :], EXPERTS), ALU.is_ge)\
                            .then_inc(S["hit_set"], 1)
                        ge(dve, S["hit_set"], at.val(-4, 2, 1))
                        V.tensor_tensor(hit[:, :, :], hit[:, :, :], mid(ekey[:, :], GB), ALU.mult).then_inc(S["hit_set"], 1)
                        ge(dve, S["hit_set"], at.val(-4, 2, 2))
                        V.tensor_reduce(best[:, :], hit[:, :, :], AX.X, ALU.max).then_inc(S["best_set"], 1)
                        ge(dve, S["best_set"], at.val(-4, 1, 1))
                        V.tensor_tensor(chosen[:, :, :], hit[:, :, :], last(best[:, :], EXPERTS), ALU.is_equal)\
                            .then_inc(S["chosen_set"], 1)
                    if slot in (1, 2, 3) and at.active(1):
                        ge(dve, S["qkh_set"], at.val(1, 3, slot))
                        V.tensor_tensor(qkl[:, 2 * slot - 2:2 * slot, :].rearrange("p t n -> p (t n)"), A[:, :],
                                        qkh[:, 2 * slot - 2:2 * slot, :].rearrange("p t n -> p (t n)"), ALU.subtract)\
                            .then_inc(S["qkl_set"], 1)
                    if slot == 4 and at.active(-4):
                        off, E = -4, EXPERTS
                        ge(dve, S["rk_ready"], at.val(off, 1, 1))
                        ge(dve, S["base_set"], at.val(off, 1, 0))
                        V.tensor_tensor(base[:, 1, :], base[:, 0, :], B[:, 2 * E:3 * E], ALU.add)\
                            .then_inc(S["base1_set"], 1)
                        ge(dve, S["base1_set"], at.val(off, 1, 1))
                        V.tensor_tensor(where[:, :, :], B[:, 0:GB * E].rearrange("n (b e) -> n b e", b=GB),
                                        base[:, :, :], ALU.add).then_inc(S["wh_set"], 1)
                        ge(dve, S["wh_set"], at.val(off, 1, 1))
                        V.tensor_tensor(base[:, 0, :], base[:, 1, :], B[:, 3 * E:4 * E], ALU.add)\
                            .then_inc(S["base_set"], 1)
                        V.tensor_tensor(where2[:, :, :], where[:, :, :], chosen[:, :, :], ALU.mult)\
                            .then_inc(S["wh2_set"], 1)
                        ge(dve, S["wh2_set"], at.val(off, 1, 1))
                        V.tensor_reduce(slot_f[:, :], where2[:, :, :], AX.X, ALU.add).then_inc(S["slotf_set"], 1)
                        V.tensor_copy(row[at.par(off)][:, :, IDW:IDW + 1].bitcast(I32),
                                      token_no[:, bass.ds(at.val(off, GB, 0), GB)].unsqueeze(2)).then_inc(S["id_set"], 1)
                        ge(dve, S["slotf_set"], at.val(off, 1, 1))
                        V.tensor_copy(slot_i[at.par(off)][:, :], slot_f[:, :]).then_inc(S["slot_set"], 1)
                    if slot == 2 and at.active(-2):
                        combine(at, -2, 1)
                    if slot == 5 and at.active(-2):
                        combine(at, -2, 2)
                    if slot == 6 and at.active(2):
                        ge(dve, S["f2_ready"], at.val(2, 1, 1))
                        ge(dve, S["e1_set"], at.val(2, GB, 0))
                        V.tensor_tensor(emb[:, :, :], B[:, 0:GB * D].rearrange("n (b d) -> n b d", b=GB),
                                        mid(pos_sb[:, :], GB), ALU.add).then_inc(S["emb_set"], 1)
                        ge(dve, S["emb_set"], at.val(2, 1, 1))
                        ge(dve, S["v1_set"], at.val(2, 1, 0))
                        stats(emb, bst, mv1, at, 2, S["st1_set"], S["mv1_set"])
                    if slot == 7 and at.active(-3):
                        c = at.par(-3)
                        ge(dve, S["kp_ready"], at.val(-3, 1, 1))
                        ge(dve, S["rms_set"], at.val(-3, 1, 1))
                        if at.active(-6):
                            ge(dve, rows_out[c], at.turned(-6, 32))
                        for b in range(GB):
                            ins = V.scalar_tensor_tensor(
                                out=row[c][:, b, D:2 * D], in0=A[:, b * D:b * D + D], scalar=rms[:, 1, b:b + 1],
                                in1=hb[:, bass.ds(at.val(-3, GB, b), 1), :].rearrange("n o d -> n (o d)"),
                                op0=ALU.mult, op1=ALU.add)
                            ins.then_inc(S["h1_set"], 1)
                        for b in range(GB):
                            ge(dve, S["h1_set"], at.val(-3, GB, b + 1))
                            V.bn_stats(bst3[:, b, :], row[c][:, b, D:2 * D]).then_inc(S["st3_set"], 1)
                        for b in range(GB):
                            apart(dve, S["st3_set"], at.val(-3, GB, b + 1))
                            V.bn_aggr(mv3[:, b, :], bst3[:, b, :]).then_inc(S["mv3_set"], 1)
                    if slot == 7 and at.active(2):
                        ge(dve, S["rs1_set"], at.val(2, 1, 1))
                        ge(dve, S["gm_set"], at.val(2, 1, 0))
                        apply(e1, emb, mv1, rs1, S["e1_set"])
                    if slot == 8 and at.active(-2):
                        combine(at, -2, 3)
                    if slot == 8 and at.active(-3):
                        ge(dve, S["rs3_set"], at.val(-3, 1, 1))
                        ge(dve, S["x3_set"], at.val(-3, 2, 0))
                        apply(xn3, row[at.par(-3)][:, :, D:2 * D], mv3, rs3, S["xn3_set"])
                    if slot == 9 and at.active(2):
                        ge(dve, S["h0_set"], at.val(2, 1, 1))
                        stats(h0, bst2, mv2, at, 2, S["st2_set"], S["mv2_set"])
                    if slot == 10 and at.active(2):
                        ge(dve, S["rs2_set"], at.val(2, 1, 1))
                        ge(dve, S["xs_set"], at.val(2, 2, 0))
                        apply(xn, h0, mv2, rs2, S["xn_set"])
                    if slot == 11 and at.active(-1):
                        combine(at, -1, 0)

            over_steps(dve, step)

            steps_256, tiles_ = steps_f[:, 0:MAXT], steps_f[:, MAXT:MAXT + TILES]
            done = 0

            def link(ins):
                nonlocal done
                done += 1
                ins.then_inc(S["table"], 1)
                dve.wait_ge(S["table"], done)

            dve.wait_ge(S["base_set"], NG)
            V.tensor_copy(pad_at[:, :], base[0:1, 0, :]).then_inc(S["table_set"], 1)
            link(V.tensor_tensor(cnt[:, :], base[0:1, 0, :], first_row[0:1, :], ALU.subtract))
            link(V.tensor_tensor(over[:, :, :], last(cnt[:, :], MAXT), mid(steps_256, EXPERTS), ALU.is_gt))
            link(V.tensor_reduce(tl[:, :], over[:, :, :], AX.X, ALU.add))
            link(V.tensor_copy(cum[:, 0:1], tl[:, 0:1]))
            for e in range(1, EXPERTS):
                link(V.tensor_tensor(cum[:, e:e + 1], cum[:, e - 1:e], tl[:, e:e + 1], ALU.add))
            link(V.tensor_tensor(past[:, :, :], last(tiles_, EXPERTS), mid(cum[:, :], TILES), ALU.is_ge))
            link(V.tensor_reduce(ef[:, :], past[:, :, 0:EXPERTS - 1], AX.X, ALU.add))
            V.tensor_copy(tab_e[:, :], ef[:, :]).then_inc(S["table_set"], 1)
            link(V.tensor_tensor(skips[:, :, :], past[:, :, :], mid(tl[:, :], TILES), ALU.mult))
            link(V.tensor_reduce(skip[:, :], skips[:, :, 0:EXPERTS - 1], AX.X, ALU.add))
            link(V.scalar_tensor_tensor(out=tr[0][:, :], in0=ef[:, :], scalar=float(CAP // TILE), in1=tiles_,
                                        op0=ALU.mult, op1=ALU.add))
            link(V.tensor_tensor(tr[1][:, :], tr[0][:, :], skip[:, :], ALU.subtract))
            link(V.tensor_scalar(tr[2][:, :], tr[1][:, :], -1.0, float(EXPERTS * CAP // TILE), ALU.mult, ALU.add))
            link(V.tensor_tensor(tr[3][:, :], tr[2][:, :], past[:, :, EXPERTS - 1], ALU.mult))
            link(V.tensor_tensor(tr[4][:, :], tr[1][:, :], tr[3][:, :], ALU.add))
            V.tensor_scalar(tab_row[:, :], tr[4][:, :], float(TILE), None, ALU.mult).then_inc(S["table_set"], 1)
            dve.wait_ge(S["w1h_set"], 1)
            V.tensor_tensor(w1s[:, :, :, 1, :], stage1, w1s[:, :, :, 0, :], ALU.subtract).then_inc(S["ffn_set"], 1)
            dve.wait_ge(S["w2h_set"], 1)
            V.tensor_tensor(w2s[:, :, 1, :], stage2, w2s[:, :, 0, :], ALU.subtract).then_inc(S["ffn_set"], 1)
            dve.wait_ge(S["table_set"], 3)

            def expert_step(at):
                if at.active(0):
                    for k in range(3):
                        c, g = at.par(0, 2), probs[(3 * at.const + k) % 4]
                        ge(dve, S["hh_set"], at.val(0, 3, k + 1))
                        V.tensor_tensor(hid[:, c, 1, 2 * k:2 * k + 2, :], g[:, :].rearrange("p (t n) -> p t n", t=2),
                                        hid[:, c, 0, 2 * k:2 * k + 2, :], ALU.subtract).then_inc(S["hl_set"], 1)
                if at.active(-1):
                    c = at.par(-1, 2)
                    e = dve.value_load(tab_e[0:1, bass.ds(at.val(-1, 1, 0), 1)], min_val=0, max_val=EXPERTS - 1)
                    ge(dve, S["dn_ready"], at.val(-1, 1, 1))
                    ge(dve, S["y_set"], at.val(-1, 1, 0))
                    V.tensor_tensor(ysum[:, :, :], o_bank[c][:, 0:GB * D].rearrange("n (j d) -> n j d", j=2),
                                    mid(b2_sb[:, bass.ds(e * D, D)], 2), ALU.add).then_inc(S["ysum_set"], 1)
                    ge(dve, S["ysum_set"], at.val(-1, 1, 1))
                    if at.active(-3):
                        ge(dve, outs[c], at.turned(-3, 32, 2))
                    V.tensor_tensor(xn_e[c][:, :, :], ysum[:, :, :], row[at.par(-1, 4)][:, :, D:2 * D], ALU.add)\
                        .then_inc(S["y_set"], 1)

            over_tiles(dve, expert_step)


_INS = ['x', 'L0_tok_turns', 'L0_tok_poly_coeffs', 'L0_tok_pos_table', 'L0_tok_ln_gamma', 'L0_tok_ln_beta',
        'L0_attn_W_qkv1', 'L0_attn_W_qkv2', 'L0_attn_W_proj', 'L0_attn_b_proj', 'L0_attn_norm_w', 'L0_attn_lambda_1',
        'L0_attn_lambda_2', 'L0_attn_xpos', 'L0_ffn_Wg', 'L0_ffn_bg', 'L0_ffn_W1', 'L0_ffn_b1', 'L0_ffn_W2', 'L0_ffn_b2']


def kernel(**inputs):
    import numpy as np
    import concourse.bacc as bacc
    from concourse.bass_utils import run_bass_kernel_spmd

    nc = bacc.Bacc("TRN2", target_bir_lowering=False, num_devices=1)
    arrays, args = {}, []
    for name in _INS:
        a = np.ascontiguousarray(inputs[name])
        arrays[f"in_{name}_dram"] = a
        args.append(nc.dram_tensor(f"in_{name}_dram", a.shape, mybir.dt.from_np(a.dtype), kind="ExternalInput").ap())
    args.append(nc.dram_tensor("out_0_dram", (NB, P, D), F32, kind="ExternalOutput").ap())
    build(nc, *args)
    r = run_bass_kernel_spmd(nc, [arrays], core_ids=[0])
    return r.results[0]["out_0_dram"]
```

```python
from contextlib import ExitStack

import concourse.bass as bass
from concourse import mybir

ALU = mybir.AluOpType
ACT = mybir.ActivationFunctionType
AX = mybir.AxisListType
F32 = mybir.dt.float32
F16 = mybir.dt.float16
I32 = mybir.dt.int32

P = 128
NB = 64
GB = 2
NG = NB // GB
GT = GB * P
D = 192
TAIL = D - P
HEADS, HD = 12, 16
VH = 2 * HEADS
PAIRS = VH // 2
CH = 6
NCH = CH * GB
TURNS, POLY = 8, 5
SPLIT = 2 * D
QK = 4 * D
WC = QK + D
HIDDEN, EXPERTS = 768, 4
HT = HIDDEN // P
TOK = NB * P
TILE = 256
TILES = TOK // TILE + EXPERTS - 1
CAP = TOK + TILE
ROWS = EXPERTS * CAP + TILE
ROW = D + D + 16
NO_TOKEN = 1 << 20
ONES16 = 0x3C003C00
IDW = 2 * D
SCALE = HD ** -0.5
CONSTS = 14
MAXT = TOK // TILE
STAGE = EXPERTS * 2 * HIDDEN + EXPERTS * HIDDEN // P * D
SLOTS = NCH
TBANKS = 1
LAG_T, LAG_PV = 17, 19

PE_PLAN = {"KG": (0, -4), "F1": (1, 3), "NM": (1, -1), "F6": (1, 1), "KO1": (2, -2), "KT": (4, -3), "F2": (4, 3),
           "GL": (4, -4), "V": (5, 1), "KO2": (5, -2), "KP": (5, -3), "F3": (7, 2), "KO3": (9, -2), "F4": (9, 2),
           "RK": (9, -4), "F5": (10, 2), "KO0": (11, -1)}
ACT_PLAN = {"xT": (8, 2), "qkh0": (10, 2), "qkh1": (11, 2), "qkh2": (2, 1), "nmT": (2, -1), "o0": (10, -1),
            "o1": (1, -2), "o2": (4, -2), "o3": (8, -2), "powersT": (1, 3), "oT": (4, -3), "v": (6, 1),
            "sq": (11, -2), "oh": (10, -2), "x3h": (10, -3), "gT": (0, -4), "xh": (4, 2)}
DVE_PLAN = {"qkl0": (11, 2), "qkl1": (0, 1), "qkl2": (3, 1), "c0": (0, -2), "c1": (3, -2), "c2": (6, -2),
            "c3": (9, -2), "E1": (5, 3), "E2": (8, 3), "st2": (0, 2), "xn": (3, 2), "h1": (6, -3), "st3": (7, -3),
            "xn3": (9, -3), "g1": (5, -4), "g2": (6, -4), "g3": (8, -4), "r1": (10, -4), "r2": (11, -4),
            "r3": (1, -5)}
POOL_PLAN = {"SO": (0, -3), "rms": (0, -3), "scatter": (0, -5), "R2": (1, 2), "XL": (4, 2), "R1": (7, 3),
             "gather": (8, 4), "R3": (8, -3), "H0": (9, 3), "PW": (11, 4), "X3L": (9, -3)}
PE_TASKS = sorted(PE_PLAN, key=lambda name: PE_PLAN[name][0])
MISC = 3
BANK_OF = {"KG": 1, "F1": 0, "NM": 1, "F6": 2, "KO1": 0, "KT": 1, "F2": 0, "GL": 2, "KO2": 1, "KP": 0, "V": 2,
           "F3": 1, "KO3": 2, "F4": 1, "RK": 0, "F5": 2, "KO0": 0}
READ_BY = {"F1": ("pwT_ready", 1, 1), "F2": ("emb_set", 1, 1), "F3": ("xT_ready", 1, 1), "F4": ("qkl_set", 3, 1),
           "F5": ("qkl_set", 3, 2), "F6": ("qkl_set", 3, 3), "V": ("v_set", 1, 1), "NM": ("nmT_set", 1, 1),
           "KO0": ("o1_set", 2, 1), "KO1": ("o2_set", 2, 1), "KO2": ("o1_set", 2, 2), "KO3": ("o2_set", 2, 2),
           "RK": ("base_set", 1, 1), "KT": ("oT_set", 1, 1), "KP": ("h1_set", 2, 2), "KG": ("gT_set", 1, 1),
           "GL": ("lg_set", 1, 1)}
FIRST, LAST = -4, NG + 4
LOOP0, UNROLL = 7, 3
TRIPS = (NG - 4 - LOOP0) // UNROLL
UNROLL_B, LOOP0_B = 4, 3
TRIPS_B = (TILES - 1 - LOOP0_B) // UNROLL_B


class At:

    def __init__(self, it, const, count=NG, unroll=UNROLL):
        self.it, self.const, self.count, self.unroll = it, const, count, unroll

    def active(self, off):
        return self.it is not None or 0 <= self.const + off < self.count

    def before(self):
        return At(self.it, self.const - 1, self.count, self.unroll)

    def par(self, off, n=3):
        return (self.const + off) % n

    def val(self, off, mul, add):
        v = mul * (self.const + off) + add
        assert self.it is None or v > 0
        return v if self.it is None else self.it * (self.unroll * mul) + v

    def turned(self, off, per, n=3):
        v = per * ((self.const + off) // n + 1)
        assert self.it is None or v > 0
        return v if self.it is None else self.it * (self.unroll // n * per) + v


def ge(eng, sem, value):
    if not isinstance(value, int) or value > 0:
        eng.wait_ge(sem, value)


def over_steps(eng, step):
    for s in range(FIRST, LOOP0):
        step(At(None, s))
    with eng.Fori(0, TRIPS) as it:
        for j in range(UNROLL):
            step(At(it, LOOP0 + j))
    for s in range(LOOP0 + UNROLL * TRIPS, LAST + 1):
        step(At(None, s))


def over_tiles(eng, step):
    for s in range(-1, LOOP0_B):
        step(At(None, s, TILES, UNROLL_B))
    with eng.Fori(0, TRIPS_B) as it:
        for j in range(UNROLL_B):
            step(At(it, LOOP0_B + j, TILES, UNROLL_B))
    for s in range(LOOP0_B + UNROLL_B * TRIPS_B, TILES + 1):
        step(At(None, s, TILES, UNROLL_B))


def chunk_of(slot, lag):
    n = slot - lag
    return n // NCH, n % NCH


def build(nc, x, turns, poly, pos_table, ln_gamma, ln_beta, w_qkv1, w_qkv2, w_proj, b_proj, norm_w,
          lambda_1, lambda_2, xpos, wg, bg, w1, b1, w2, b2, out):
    ctx = ExitStack()
    with ctx:
        def sb(name, shape, dt):
            return ctx.enter_context(nc.sbuf_tensor(name, shape, dt))

        def bank(name, dt=F32):
            return ctx.enter_context(nc.psum_tensor(name, [P, 2048 // (4 if dt == F32 else 2)], dt))

        def sem(name):
            return ctx.enter_context(nc.semaphore(name))

        def mid(ap, n):
            return ap.unsqueeze(1).broadcast_to([ap.shape[0], n, ap.shape[1]])

        def last(ap, n):
            return ap.unsqueeze(len(ap.shape)).broadcast_to([*ap.shape, n])

        ident = sb("ident", [P, P], F32)
        ident16 = sb("ident16", [P, P], F16)
        earlier = sb("earlier", [P, P], F16)
        ones16 = sb("ones16", [P, P], F16)
        token_no = sb("token_no", [P, NB], I32)
        x_in = sb("x_in", [NB, P], I32)
        x_f = sb("x_f", [NB, P], F32)
        ids = sb("ids", [P, NB], I32)
        poly_sb = sb("poly_sb", [TURNS * POLY, D], F32)
        pos_sb = sb("pos_sb", [P, D], F32)
        gamma = sb("gamma", [P, D], F32)
        beta = sb("beta", [P, D], F32)
        bproj = sb("bproj", [P, D], F32)
        lam = sb("lam", [P, HEADS], F32)
        lam2 = sb("lam2", [P, HEADS], F32)
        bgate = sb("bgate", [P, EXPERTS], F32)
        normw = sb("normw", [P, 2], F32)
        mhalf = sb("mhalf", [P, GB], F32)
        wst = sb("wst", [P, 2, WC], F32)
        wqkv = sb("wqkv", [P, 2, 2, WC], F16)
        wpst = sb("wpst", [P, 2, D], F32)
        wp = sb("wp", [P, 2, 2, D], F16)
        wgst = sb("wgst", [P, 2, EXPERTS], F32)
        wgs = sb("wgs", [P, 2, 2, EXPERTS], F16)
        zrow = sb("zrow", [PAIRS, GT], F16)

        idx = sb("idx", [P, 3, GB], I32)
        turn = sb("turn", [P, 3, GB, TURNS], F32)
        powers = sb("powers", [P, GB, TURNS, POLY], F32)
        powersT = sb("powersT", [TURNS * POLY, GT], F32)
        emb = sb("emb", [P, GB, D], F32)
        bst = sb("bst", [P, GB, 6], F32)
        mv1 = sb("mv1", [P, GB, 2], F32)
        mv2 = sb("mv2", [P, GB, 2], F32)
        mv3 = sb("mv3", [P, GB, 2], F32)
        bst2 = sb("bst2", [P, GB, 6], F32)
        bst3 = sb("bst3", [P, GB, 6], F32)
        rs1 = sb("rs1", [P, 2, GB], F32)
        rs2 = sb("rs2", [P, 2, GB], F32)
        rs3 = sb("rs3", [P, 2, GB], F32)
        rms = sb("rms", [P, 2, GB], F32)
        sumsq = sb("sumsq", [P, GB], F32)
        sq = sb("sq", [P, GB, D], F32)
        e1 = sb("e1", [P, GB, D], F32)
        e2 = sb("e2", [P, GB, D], F32)
        h0 = sb("h0", [P, GB, D], F32)
        hb = sb("hb", [P, NB, D], F32)
        xn = sb("xn", [P, GB, D], F32)
        xs = sb("xs", [P, GB, SPLIT], F16)
        xT = sb("xT", [P, 3, GT], F16)
        qkh = sb("qkh", [P, 6, GT], F16)
        qkl = sb("qkl", [P, 6, GT], F16)
        Qs_all = sb("Qs_all", [P, 3, PAIRS, 2, GT], F16)
        Ks_all = sb("Ks_all", [P, 3, PAIRS, GT], F16)
        Qs = [Qs_all[:, c] for c in range(3)]
        Ks = [Ks_all[:, c] for c in range(3)]
        Vx = [sb(f"Vx{c}", [P, GB, HEADS, HD + 1], F32) for c in range(3)]
        nm = [sb(f"nm{c}", [P, GB, 2, PAIRS], F16) for c in range(3)]
        nmT = sb("nmT", [VH, GT], F16)
        probs = [sb(f"probs{c}", [P, 512], F32) for c in range(4)]
        ot = [sb(f"ot{c}", [P, 3 * P], F32) for c in range(2)]
        rc1 = sb("rc1", [P, HEADS], F32)
        rc2 = sb("rc2", [P, 2, HEADS], F32)
        o1 = sb("o1", [P, HEADS, HD], F32)
        o2 = sb("o2", [P, HEADS, HD], F32)
        oo = sb("oo", [P, GB, D], F32)
        os16 = sb("os16", [P, GB, SPLIT], F16)
        oT = sb("oT", [P, 3, GT], F16)
        row = [sb(f"row{c}", [P, GB, ROW], F32) for c in range(4)]
        xn3 = sb("xn3", [P, GB, D], F32)
        gT = sb("gT", [P, 3, GT], F16)
        ekey = sb("ekey", [P, EXPERTS], F32)
        ekey_i = sb("ekey_i", [P, EXPERTS], I32)
        base_i = sb("base_i", [P, EXPERTS], I32)
        base = sb("base", [P, GB, EXPERTS], F32)
        lg = sb("lg", [P, GB, EXPERTS], F32)
        top = sb("top", [P, GB], F32)
        hit = sb("hit", [P, GB, EXPERTS], F32)
        best = sb("best", [P, GB], F32)
        chosen = sb("chosen", [P, GB, EXPERTS], F16)
        where = sb("where", [P, GB, EXPERTS], F32)
        where2 = sb("where2", [P, GB, EXPERTS], F32)
        slot_f = sb("slot_f", [P, GB], F32)
        slot_i = [sb(f"slot_i{c}", [P, GB], I32) for c in range(3)]

        tokens = sb("tokens", [P, 2, 2], I32)
        b1r = sb("b1r", [EXPERTS * HT, P], F32)
        b1T = sb("b1T", [P, EXPERTS * HT], F32)
        b2_sb = sb("b2_sb", [P, EXPERTS * D], F32)
        steps_i = sb("steps_i", [1, MAXT + TILES], I32)
        steps_f = sb("steps_f", [1, MAXT + TILES], F32)
        first_row = sb("first_row", [P, EXPERTS], F32)
        cnt = sb("cnt", [1, EXPERTS], F32)
        over = sb("over", [1, EXPERTS, MAXT], F32)
        tl = sb("tl", [1, EXPERTS], F32)
        cum = sb("cum", [1, EXPERTS], F32)
        past = sb("past", [1, TILES, EXPERTS], F32)
        skips = sb("skips", [1, TILES, EXPERTS], F32)
        ef = sb("ef", [1, TILES], F32)
        skip = sb("skip", [1, TILES], F32)
        tr = [sb(f"tr{c}", [1, TILES], F32) for c in range(5)]
        tab_e = sb("tab_e", [1, TILES], I32)
        tab_row = sb("tab_row", [1, TILES], I32)
        pad_at = sb("pad_at", [1, EXPERTS], I32)

        stage = hb[:, 0:STAGE // D, :].rearrange("p n d -> p (n d)")
        W1N, W2N = EXPERTS * 2 * HIDDEN, EXPERTS * HT * D
        stage1 = stage[:, 0:W1N].rearrange("p (e r h) -> p e r h", e=EXPERTS, r=2)
        stage2 = stage[:, W1N:W1N + W2N].rearrange("p (e n) -> p e n", e=EXPERTS)
        w1f = Qs_all[:, 0:2].rearrange("p c t a n -> p (c t a n)")
        w2f = Ks_all[:, :].rearrange("p c t n -> p (c t n)")
        w1s = w1f.rearrange("p (e r x h) -> p e r x h", e=EXPERTS, r=2, x=2)
        w2s = w2f.rearrange("p (e x n) -> p e x n", e=EXPERTS, x=2)
        hid = Qs[2].rearrange("p t a n -> p (t a n)").rearrange("p (c x k n) -> p c x k n", c=2, x=2, k=HT)
        xe, xn_e, ysum = (xT, oT), (xn, xn3), e1

        s_bank = [bank(f"s_bank{c}") for c in range(2)]
        t_bank = [bank(f"t_bank{c}") for c in range(TBANKS)]
        o_bank = [bank(f"o_bank{c}") for c in range(2)]
        misc = [bank(f"misc{c}") for c in range(MISC)]
        u_bank = (s_bank + t_bank + misc[2:])[:4]

        qk_dram = nc.dram_tensor("qk_dram", [2, QK, GT], F16, kind="Internal").ap()
        routed = nc.dram_tensor("routed", [ROWS, ROW], F32, kind="Internal").ap()

        names = ("x_in_done emb_in consts_in w_in wqkv_set ones_set pads_set setup_pool ids_t ids_x ids_done setup_dve w_scaled vx_set zero_set "
                 "idx_set pw_set pw1 pw2 pw_ready f1_ready pwT_ready f2_ready emb_set st1_set mv1_set v1_set rs1_set e1_set "
                 "gm_set h0_set hb_set st2_set mv2_set v2_set rs2_set xn_set xh_set xs_set f3_ready xT_ready f4_ready qkh_set qkl_set "
                 "v_ready v_set scr_w s_ready s_used nm_ready nmT_set t_ready p_ready pv_done o_set ko_ready rc_set o1_set rc2_set "
                 "o2_set oo_set sq_set rq_set rms_set oh_set os_set kt_ready oT_set kp_ready h1_set st3_set mv3_set v3_set rs3_set xn3_set "
                 "x3h_set x3_set kg_ready gT_set gl_ready lg_set top_set hit_set best_set chosen_set rk_ready wh_set wh2_set "
                 "slotf_set slot_set base_set base1_set id_set waits_apart "
                 "b1_in b1_ready table table_set pads_out ffn_in w1h_set w2h_set w1l_set w2l_set ffn_set "
                 "tT_ready xe_set u_ready g_set hh_set hl_set dn_ready ysum_set token_set y_set").split()
        S = {n: sem(n) for n in names}
        turns_in = [sem(f"turns_in{c}") for c in range(3)]
        ops_in = [sem(f"ops_in{c}") for c in range(3)]
        nm_in = [sem(f"nm_in{c}") for c in range(3)]
        rows_out = [sem(f"rows_out{c}") for c in range(3)]
        tile_in = [sem(f"tile_in{c}") for c in range(4)]
        outs = [sem(f"outs{c}") for c in range(2)]

        def apart(eng, sem_, value):
            if isinstance(value, int):
                ge(eng, sem_, value)
            else:
                eng.wait_ge(sem_, value).then_inc(S["waits_apart"], 1)

        block = ctx.enter_context(nc.Block())

        @block.sync
        def _(sp):
            sp.dma_start(x_in[:, :], x).then_inc(S["x_in_done"], 16)
            for to, of in ((poly_sb[:, :], poly.rearrange("t p d -> (t p) d")), (pos_sb[:, :], pos_table[0:P, :]),
                           (gamma[:, :], ln_gamma.partition_broadcast(P)), (beta[:, :], ln_beta.partition_broadcast(P)),
                           (bproj[:, :], b_proj.partition_broadcast(P))):
                sp.dma_start(to, of).then_inc(S["emb_in"], 16)
            for rows, src, r in ((slice(0, P), slice(0, P), 0), (slice(0, TAIL), slice(P, D), 1),
                                 (slice(TAIL, P), slice(P, D), 1)):
                cols = wst[rows, r, :].rearrange("p (s d) -> p s d", d=D)
                sp.dma_start(cols[:, 0::2], w_qkv1[src, :].rearrange("p (s d) -> p s d", d=D)).then_inc(S["w_in"], 16)
                sp.dma_start(cols[:, 1::2], w_qkv2[src, 0:2 * D].rearrange("p (s d) -> p s d", d=D))\
                    .then_inc(S["w_in"], 16)
            def fixed(value):
                return value if isinstance(value, int) else sp.snap(value)

            def step(at):
                v_nm, v_qk = fixed(at.val(-1, 1, 1)), fixed(at.val(1, 3, 3))
                v_scr, v_t = fixed(at.val(1, 32, 32)), fixed(at.val(1, NCH, -2 * NCH))
                neg_max(at, v_nm)
                if at.active(1):
                    apart(sp, S["qkh_set"], v_qk)
                    apart(sp, S["qkl_set"], v_qk)
                if at.active(1):
                    for part, t in ((0, qkh), (1, qkl)):
                        sp.dma_start(qk_dram[part].rearrange("(t p) n -> p t n", p=P), t[:, :, :]).then_inc(S["scr_w"], 16)
                    apart(sp, S["scr_w"], v_scr)
                    c = at.par(1)
                    apart(sp, S["t_ready"], v_t)
                    if at.it is None and at.const + 1 < 3:
                        sp.wait_ge(S["zero_set"], at.const + 2)
                        sp.wait_ge(S["ones_set"], at.const + 2)
                    for side, (dst, parts) in enumerate((("q", (0, 0, 1)), ("k", (0, 1, 0)))):
                        for a in range(2):
                            for r, part in enumerate(parts):
                                rows = slice(64 * a + HD * r, 64 * a + HD * r + HD)
                                src = qk_dram[part, side * 2 * D:(side + 1) * 2 * D].rearrange(
                                    "(p a d) n -> a d p n", a=2, d=HD)[a]
                                to = Qs[c][rows, :, a, :] if dst == "q" else Ks[c][rows, :, :]
                                sp.dma_start(to, src).then_inc(ops_in[c], 16)
                    for a in range(2):
                        sp.dma_start(Qs[c][64 * a + 48:64 * a + 49, :, a, :], zrow[:, :]).then_inc(ops_in[c], 16)

            def neg_max(at, v_nm):
                if at.active(-1):
                    c = at.par(-1)
                    ge(sp, S["nmT_set"], v_nm)
                    for a in range(2):
                        sp.dma_start(Qs[c][64 * a + 48:64 * a + 49, :, a, :],
                                     nmT[PAIRS * a:PAIRS * a + PAIRS, :]).then_inc(nm_in[c], 16)

            over_steps(sp, step)
            sp.wait_ge(S["h1_set"], STAGE // D)
            sp.dma_start(stage1[:, :, 0, :], w1[:, 0:P, :].rearrange("e p h -> p e h")).then_inc(S["ffn_in"], 16)
            for r in (0, TAIL):
                sp.dma_start(stage1[r:r + TAIL, :, 1, :], w1[:, P:D, :].rearrange("e p h -> p e h"))\
                    .then_inc(S["ffn_in"], 16)
            sp.dma_start(stage2.rearrange("p e (k d) -> p e k d", d=D), w2.rearrange("e (k p) d -> p e k d", p=P))\
                .then_inc(S["ffn_in"], 16)
            sp.wait_ge(S["pads_set"], 1)
            for e in range(EXPERTS):
                start = sp.value_load(pad_at[0:1, e:e + 1], min_val=e * CAP, max_val=e * CAP + TOK)
                sp.dma_start(routed[bass.ds(start, TILE)].rearrange("(p j) w -> p j w", j=2), row[3][:, :, :])\
                    .then_inc(S["pads_out"], 16)
            sp.dma_start(routed[EXPERTS * CAP:ROWS].rearrange("(p j) w -> p j w", j=2), row[3][:, :, :])\
                .then_inc(S["pads_out"], 16)
            sp.wait_ge(S["pads_out"], 16 * (EXPERTS + 1))
            sp.wait_ge(S["table_set"], 2)
            for c in range(3):
                sp.wait_ge(rows_out[c], 32 * ((NG - 1 - c) // 3 + 1))

            def load(at):
                if at.active(0):
                    c = at.par(0, 4)
                    start = sp.value_load(tab_row[0:1, bass.ds(at.val(0, 1, 0), 1)], min_val=0, max_val=EXPERTS * CAP)
                    if at.active(-4):
                        ge(sp, S["token_set"], at.val(-4, 1, 1))
                        apart(sp, S["y_set"], at.val(-4, 1, 1))
                    sp.dma_start(row[c][:, :, :], routed[bass.ds(start, TILE)].rearrange("(p j) w -> p j w", j=2))\
                        .then_inc(tile_in[c], 16)

            for t in range(4):
                load(At(None, t, TILES, UNROLL_B))
            with sp.Fori(0, TILES // 4 - 1) as it:
                for j in range(4):
                    load(At(it, 4 + j, TILES, UNROLL_B))
            for t in range(TILES // 4 * 4, TILES):
                load(At(None, t, TILES, UNROLL_B))
            for c in range(2):
                sp.wait_ge(outs[c], 32 * ((TILES - 1 - c) // 2 + 1))

        @block.gpsimd
        def _(pool):
            nsetup = 0

            def setup(ins):
                nonlocal nsetup
                nsetup += 1
                ins.then_inc(S["setup_pool"], 1)

            setup(pool.memset(ident[:, :], 0.0))
            setup(pool.memset(ident16[:, :], 0.0))
            setup(pool.memset(earlier[:, :], 1.0))
            setup(pool.memset(ones16[:, :], 1.0))
            setup(pool.memset(mhalf[:, :], -0.5))
            setup(pool.memset(powers[:, :, :, 0:1], 1.0))
            setup(pool.iota(token_no[:, :], pattern=[[P, NB]], base=0, channel_multiplier=1))
            setup(pool.iota(ekey_i[:, :], pattern=[[-1, EXPERTS]], base=EXPERTS, channel_multiplier=0))
            setup(pool.iota(base_i[:, :], pattern=[[CAP, EXPERTS]], base=0, channel_multiplier=0))
            setup(pool.iota(steps_i[:, 0:MAXT], pattern=[[TILE, MAXT]], base=0, channel_multiplier=0))
            setup(pool.iota(steps_i[:, MAXT:], pattern=[[1, TILES]], base=0, channel_multiplier=0))
            pool.wait_ge(S["setup_pool"], nsetup)
            for m in (ident, ident16):
                setup(pool.affine_select(out=m[:, :], in_=m[:, :], compare_op=ALU.not_equal, fill=1.0, base=0,
                                         pattern=[[-1, P]], channel_multiplier=1))
            setup(pool.affine_select(out=earlier[:, :], in_=earlier[:, :], compare_op=ALU.is_ge, fill=0.0, base=-1,
                                     pattern=[[1, P]], channel_multiplier=-1))
            assert nsetup == 14
            pool.memset(zrow[:, :], 0.0).then_inc(S["vx_set"], 1)
            for c in range(3):
                pool.memset(row[c][:, :, IDW:ROW], 0.0).then_inc(S["vx_set"], 1)
            pool.memset(row[3][:, :, 0:IDW], 0.0).then_inc(S["vx_set"], 1)
            pool.memset(row[3][:, :, IDW:ROW].bitcast(I32), NO_TOKEN).then_inc(S["vx_set"], 1)
            pool.memset(idx[:, :, :], 0).then_inc(S["vx_set"], 1)
            pool.wait_ge(S["vx_set"], 7)
            pool.wait_ge(S["ids_done"], 1)

            def rsqrt(dst, var, ready, value, mid_sem, done, eps, scale=1.0):
                apart(pool, ready, value)
                pool.tensor_scalar(dst[:, 0, :], var, scale, eps, ALU.mult, ALU.add).then_inc(mid_sem[0], 1)
                ge(pool, mid_sem[0], mid_sem[1])
                pool.tensor_tensor(dst[:, 1, :], dst[:, 0, :], mhalf[:, :], ALU.pow).then_inc(done, 1)

            def low(dst, src, high_set, value, done):
                ge(pool, high_set, value)
                pool.tensor_tensor(dst[:, :, D:D + TAIL], src[:, :, P:D], dst[:, :, P:D], ALU.subtract)\
                    .then_inc(done, 1)
                pool.tensor_tensor(dst[:, :, D + TAIL:SPLIT], src[:, :, 0:P], dst[:, :, 0:P], ALU.subtract)\
                    .then_inc(done, 1)

            def step(at):
                for slot in range(SLOTS):
                    slot_step(at, slot)
                if at.it is None and at.const < FIRST + 3:
                    c = at.const - FIRST
                    pool.memset(Qs[c].rearrange("p t a n -> p (t a n)").bitcast(F32), 0.0).then_inc(S["zero_set"], 1)

            def slot_step(at, slot):
                def due(name):
                    return POOL_PLAN[name][0] == slot and at.active(POOL_PLAN[name][1])

                if due("SO"):
                    off = POOL_PLAN["SO"][1]
                    low(os16, oo, S["oh_set"], at.val(off, 1, 1), S["os_set"])
                if due("rms"):
                    off = POOL_PLAN["rms"][1]
                    rsqrt(rms, sumsq[:, :], S["sq_set"], at.val(off, GB, GB), (S["rq_set"], at.val(off, 1, 1)),
                          S["rms_set"], 1e-6, 1.0 / D)
                if due("R2"):
                    off = POOL_PLAN["R2"][1]
                    rsqrt(rs2, mv2[:, :, 1], S["mv2_set"], at.val(off, GB, GB), (S["v2_set"], at.val(off, 1, 1)),
                          S["rs2_set"], 1e-5)
                if due("scatter"):
                    off = POOL_PLAN["scatter"][1]
                    c = at.par(off)
                    ge(pool, S["id_set"], at.val(off, 1, 1))
                    apart(pool, S["slot_set"], at.val(off, 1, 1))
                    for b in range(GB):
                        pool.indirect_dma_start(
                            out=routed, out_offset=bass.IndirectOffsetOnAxis(ap=slot_i[c][:, b:b + 1], axis=0),
                            in_=row[c][:, b, :], in_offset=None).then_inc(rows_out[c], 16)
                if due("XL"):
                    off = POOL_PLAN["XL"][1]
                    low(xs, xn, S["xh_set"], at.val(off, 1, 1), S["xs_set"])
                if due("R1"):
                    off = POOL_PLAN["R1"][1]
                    rsqrt(rs1, mv1[:, :, 1], S["mv1_set"], at.val(off, GB, GB), (S["v1_set"], at.val(off, 1, 1)),
                          S["rs1_set"], 1e-12)
                if due("gather"):
                    off = POOL_PLAN["gather"][1]
                    c = at.par(off)
                    apart(pool, turns_in[c], at.turned(off - 3, 32) if at.active(off - 3) else 0)
                    pool.tensor_copy(idx[:, c, :], ids[:, bass.ds(at.val(off, GB, 0), GB)]).then_inc(S["idx_set"], 1)
                    ge(pool, S["pw_ready"], at.val(off, 1, -2))
                    apart(pool, S["idx_set"], at.val(off, 1, 1))
                    for b in range(GB):
                        pool.indirect_dma_start(
                            out=turn[:, c, b, :], out_offset=None, in_=turns,
                            in_offset=bass.IndirectOffsetOnAxis(ap=idx[:, c, b:b + 1], axis=0)).then_inc(turns_in[c], 16)
                if due("R3"):
                    off = POOL_PLAN["R3"][1]
                    rsqrt(rs3, mv3[:, :, 1], S["mv3_set"], at.val(off, GB, GB), (S["v3_set"], at.val(off, 1, 1)),
                          S["rs3_set"], 1e-5)
                if due("H0"):
                    off = POOL_PLAN["H0"][1]
                    ge(pool, S["e1_set"], at.val(off, GB, GB))
                    pool.tensor_tensor(e2[:, :, :], e1[:, :, :], mid(gamma[:, :], GB), ALU.mult).then_inc(S["gm_set"], 1)
                    ge(pool, S["gm_set"], at.val(off, 1, 1))
                    ge(pool, S["xn_set"], at.val(off, GB, 0))
                    pool.tensor_tensor(h0[:, :, :], e2[:, :, :], mid(beta[:, :], GB), ALU.add).then_inc(S["h0_set"], 1)
                    ge(pool, S["h0_set"], at.val(off, 1, 1))
                    pool.tensor_tensor(hb[:, bass.ds(at.val(off, GB, 0), GB), :], h0[:, :, :], mid(bproj[:, :], GB),
                                       ALU.add).then_inc(S["hb_set"], 1)
                if due("PW"):
                    off = POOL_PLAN["PW"][1]
                    t = turn[:, at.par(off)]
                    ge(pool, turns_in[at.par(off)], at.turned(off, 32))
                    apart(pool, S["f1_ready"], at.val(off, 1, 0))
                    pool.tensor_copy(powers[:, :, :, 1], t).then_inc(S["pw_set"], 1)
                    pool.tensor_tensor(powers[:, :, :, 2], t, t, ALU.mult).then_inc(S["pw1"], 1)
                    ge(pool, S["pw1"], at.val(off, 1, 1))
                    pool.tensor_tensor(powers[:, :, :, 3], powers[:, :, :, 2], t, ALU.mult).then_inc(S["pw2"], 1)
                    pool.tensor_tensor(powers[:, :, :, 4], powers[:, :, :, 2], powers[:, :, :, 2], ALU.mult)\
                        .then_inc(S["pw_ready"], 1)
                if due("X3L"):
                    off = POOL_PLAN["X3L"][1]
                    low(row[at.par(off)][:, :, 0:D].bitcast(F16), xn3, S["x3h_set"], at.val(off, 1, 1), S["x3_set"])

            over_steps(pool, step)

            def expert_step(at):
                if at.active(-1):
                    c = at.par(-1, 2)
                    ge(pool, S["token_set"], at.val(-1, 1, 1))
                    apart(pool, S["y_set"], at.val(-1, 1, 1))
                    for j in range(2):
                        pool.indirect_dma_start(
                            out=out.rearrange("b s d -> (b s) d"), out_offset=bass.IndirectOffsetOnAxis(
                                ap=tokens[:, c, j:j + 1], axis=0),
                            in_=xn_e[c][:, j, :], in_offset=None, bounds_check=TOK - 1, oob_is_err=False)\
                            .then_inc(outs[c], 16)

            over_tiles(pool, expert_step)

        @block.tensor
        def _(pe):
            pe.wait_ge(S["setup_pool"], 14)
            pe.wait_ge(S["ids_x"], 1)
            pe.transpose(misc[0][:, 0:NB], x_f[:, :], ident[0:NB, 0:NB]).then_inc(S["ids_t"], 1)
            pe.wait_ge(S["ids_done"], 1)
            pe.wait_ge(S["emb_in"], 5 * 16)
            def claim(at, name):
                n = PE_TASKS.index(name)
                order = [(at, t) for t in PE_TASKS[:n]][::-1] + [(at.before(), t) for t in PE_TASKS[::-1]]
                for at_, t in order:
                    if BANK_OF[t] == BANK_OF[name] and at_.active(PE_PLAN[t][1]):
                        sem_name, per, nth = READ_BY[t]
                        ge(pe, S[sem_name], at_.val(PE_PLAN[t][1], per, nth))
                        break
                return misc[BANK_OF[name]]

            TERMS = ((0, 0, 0), (0, 0, 1), (2, 0, 0), (1, 1, 0), (1, 1, 1))

            def transposes3(dst, src, ready):
                for k in range(3):
                    for b in range(GB):
                        mm = pe.transpose(dst[:, k * GT + b * P:k * GT + b * P + P], src[:, b, k * P:k * P + P],
                                          ident16[:, :])
                mm.then_inc(ready, 1)

            def tokens_by(dst, xT_, w, n, ready):
                for b in range(GB):
                    for i, (k, r, part) in enumerate(TERMS):
                        mm = pe.matmul(dst[:, b * n:b * n + n], xT_[:, k, b * P:b * P + P], w[:, r, part],
                                       start=i == 0, stop=i == len(TERMS) - 1)
                mm.then_inc(ready, 1)

            def task(at, name):
                off = PE_PLAN[name][1]
                if not at.active(off):
                    return
                m = claim(at, name)
                m16 = m[:, :].bitcast(F16)
                if name == "F1":
                    ge(pe, S["pw_ready"], at.val(off, 1, 1))
                    ge(pe, S["pw2"], at.val(off, 1, 1))
                    apart(pe, S["pw_set"], at.val(off, 1, 1))
                    for b in range(GB):
                        mm = pe.transpose(m[0:TURNS * POLY, b * P:b * P + P],
                                          powers[:, b].rearrange("s t p -> s (t p)"), ident[:, :])
                    mm.then_inc(S["f1_ready"], 1)
                elif name == "F2":
                    ge(pe, S["pwT_ready"], at.val(off, 1, 1))
                    for b in range(GB):
                        mm = pe.matmul(m[:, b * D:b * D + D], powersT[:, b * P:b * P + P], poly_sb[:, :],
                                       start=True, stop=True)
                    mm.then_inc(S["f2_ready"], 1)
                elif name == "F3":
                    ge(pe, S["xs_set"], at.val(off, 2, 2))
                    transposes3(m16, xs, S["f3_ready"])
                elif name in ("F4", "F5", "F6"):
                    t0 = 2 * (int(name[1]) - 4)
                    ge(pe, S["xT_ready"], at.val(off, 1, 1))
                    for t in (t0, t0 + 1):
                        for i, (k, r, part) in enumerate(TERMS):
                            mm = pe.matmul(m[:, (t - t0) * GT:(t - t0) * GT + GT], wqkv[:, r, part, t * P:t * P + P],
                                           xT[:, k, :], start=i == 0, stop=i == len(TERMS) - 1)
                    mm.then_inc(S["f4_ready"], 1)
                elif name == "V":
                    tokens_by(m, xT, wqkv[:, :, :, QK:WC], D, S["v_ready"])
                elif name == "NM":
                    ge(pe, S["s_used"], at.val(off, NCH, NCH))
                    for b in range(GB):
                        mm = pe.transpose(m16[0:VH, b * P:b * P + P],
                                          nm[at.par(off)][:, b].rearrange("n a p -> n (a p)"), ident16[:, :])
                    mm.then_inc(S["nm_ready"], 1)
                elif name in ("KO0", "KO1", "KO2", "KO3"):
                    w = int(name[2])
                    ge(pe, S["o_set"], at.val(off, 4, w + 1))
                    for c in range(3):
                        mm = pe.transpose(m[:, c * P:c * P + P], ot[w % 2][:, c * P:c * P + P], ident[:, :])
                    mm.then_inc(S["ko_ready"], 1)
                elif name == "KT":
                    ge(pe, S["os_set"], at.val(off, 2, 2))
                    transposes3(m16, os16, S["kt_ready"])
                elif name == "KP":
                    ge(pe, S["oT_set"], at.val(off, 1, 1))
                    tokens_by(m, oT, wp, D, S["kp_ready"])
                elif name == "KG":
                    ge(pe, S["x3_set"], at.val(off, 2, 2))
                    transposes3(m16, row[at.par(off)][:, :, 0:D].bitcast(F16), S["kg_ready"])
                elif name == "GL":
                    ge(pe, S["gT_set"], at.val(off, 1, 1))
                    tokens_by(m, gT, wgs, EXPERTS, S["gl_ready"])
                elif name == "RK":
                    ge(pe, S["chosen_set"], at.val(off, 1, 1))
                    E = EXPERTS
                    both = chosen[:, :, :].rearrange("n b e -> n (b e)")
                    pe.matmul(m[:, 0:GB * E], earlier[:, :], both, start=True, stop=True)
                    pe.matmul(m[:, GB * E:2 * GB * E], ones16[:, :], both, start=True, stop=True)\
                        .then_inc(S["rk_ready"], 1)

            def step(at):
                if at.it is None and at.const == -2:
                    pe.wait_ge(S["wqkv_set"], 2)
                if at.it is None and at.const == 1:
                    pe.wait_ge(S["consts_in"], CONSTS * 16)
                    pe.transpose(o_bank[1][:, 0:EXPERTS * HT], b1r[:, :], ident[0:EXPERTS * HT, 0:EXPERTS * HT])\
                        .then_inc(S["b1_ready"], 1)
                    pe.wait_ge(S["setup_dve"], 1)
                for slot in range(SLOTS):
                    if at.active(0):
                        c, b, cc = at.par(0), slot // CH, slot % CH
                        if slot == 0:
                            ge(pe, ops_in[c], at.turned(0, 14 * 16))
                        ge(pe, S["s_used"], at.val(0, NCH, slot - 1))
                        for a in range(2):
                            for pp in range(2):
                                p = 2 * cc + pp
                                mm = pe.matmul(s_bank[slot % 2][:, (2 * a + pp) * P:(2 * a + pp) * P + P],
                                               Qs[c][:, p, a, b * P:b * P + P], Ks[c][:, p, b * P:b * P + P],
                                               start=True, stop=True)
                        mm.then_inc(S["s_ready"], 1)
                    off, k = chunk_of(slot, LAG_T)
                    if at.active(off):
                        c, b, cc = at.par(off), k // CH, k % CH
                        if k == 0:
                            ge(pe, nm_in[c], at.turned(off, 32))
                        ge(pe, S["p_ready"], at.val(off, NCH, k + 1 - TBANKS))
                        for pp in range(2):
                            p = 2 * cc + pp
                            mm = pe.matmul(t_bank[k % TBANKS][:, pp * 2 * P:(pp + 1) * 2 * P], Ks[c][:, p, b * P:b * P + P],
                                           Qs[c][:, p, :, b * P:b * P + P], start=True, stop=True)
                        mm.then_inc(S["t_ready"], 1)
                    off, k = chunk_of(slot, LAG_PV)
                    if at.active(off):
                        c, b, cc = at.par(off), k // CH, k % CH
                        w = k // 3
                        if k == 0:
                            ge(pe, S["v_set"], at.val(off, 1, 1))
                        if k % 3 == 0:
                            ge(pe, S["o_set"], at.val(off, 4, w - 1))
                        ge(pe, S["p_ready"], at.val(off, NCH, k + 1))
                        for j in range(4):
                            head = (4 * cc + j) % HEADS
                            mm = pe.matmul(o_bank[w % 2][32 * j:32 * j + HD + 1, (cc % 3) * P:(cc % 3) * P + P],
                                           Vx[c][:, b, head, :], probs[k % 4][:, j * P:j * P + P], start=True, stop=True)
                        mm.then_inc(S["pv_done"], 1)
                    for name in PE_TASKS:
                        if PE_PLAN[name][0] == slot:
                            task(at, name)

            over_steps(pe, step)

            pe.wait_ge(S["ffn_set"], 2 * EXPERTS)
            pe.wait_ge(S["table_set"], 2)

            def expert_of(at, off):
                return pe.value_load(tab_e[0:1, bass.ds(at.val(off, 1, 0), 1)], min_val=0, max_val=EXPERTS - 1)

            def expert_step(at):
                e_up = expert_of(at, 0) if at.active(0) else None
                e_down = expert_of(at, -1) if at.active(-1) else None
                if at.active(1):
                    m = misc[at.par(1, 2)]
                    c = at.par(1, 4)
                    ge(pe, S["xe_set"], at.val(1, 1, -1))
                    ge(pe, tile_in[c], at.turned(1, 16, 4))
                    transposes3(m[:, :].bitcast(F16), row[c][:, :, 0:D].bitcast(F16), S["tT_ready"])
                if at.active(0):
                    ge(pe, S["xe_set"], at.val(0, 1, 1))
                    for k in range(3):
                        bank_ = u_bank[(3 * at.const + k) % 4]
                        ge(pe, S["g_set"], at.val(0, 6, 2 * (k - 3)))
                        for t in (2 * k, 2 * k + 1):
                            for i, (ck, r, part) in enumerate(TERMS):
                                at_w = e_up * (4 * HIDDEN) + ((2 * r + part) * HIDDEN + t * P)
                                mm = pe.matmul(bank_[:, (t - 2 * k) * GT:(t - 2 * k + 1) * GT],
                                               w1f[:, bass.ds(at_w, P)], xe[at.par(0, 2)][:, ck, :],
                                               start=i == 0, stop=i == len(TERMS) - 1)
                        mm.then_inc(S["u_ready"], 1)
                if at.active(-1):
                    c = at.par(-1, 2)
                    ge(pe, S["hl_set"], at.val(-1, 3, 3))
                    ge(pe, S["ysum_set"], at.val(-1, 1, -1))
                    for j in range(2):
                        n, steps = 0, [(k, x, w) for k in range(HT) for x, w in ((0, 0), (0, 1), (1, 0))]
                        for n, (k, x, w) in enumerate(steps):
                            mm = pe.matmul(o_bank[c][:, j * D:j * D + D], hid[:, c, x, k, j * P:j * P + P],
                                           w2f[:, bass.ds(e_down * (2 * HT * D) + (w * HT + k) * D, D)],
                                           start=n == 0, stop=n == len(steps) - 1)
                    mm.then_inc(S["dn_ready"], 1)

            over_tiles(pe, expert_step)

        @block.scalar
        def _(act):
            def copy(dst, src, done):
                nc.scalar.activation(dst, src, ACT.Copy).then_inc(done, 1)

            n = 0
            for to, of in ((wpst[:, 0, :], w_proj[0:P, :]), (wpst[0:TAIL, 1, :], w_proj[P:D, :]),
                           (wpst[TAIL:P, 1, :], w_proj[P:D, :]),
                           (normw[:, 0:1], norm_w[0:P].unsqueeze(1)), (normw[0:TAIL, 1:2], norm_w[P:D].unsqueeze(1)),
                           (normw[TAIL:P, 1:2], norm_w[P:D].unsqueeze(1)),
                           (wgst[:, 0, :], wg[0:P, :]), (wgst[0:TAIL, 1, :], wg[P:D, :]), (wgst[TAIL:P, 1, :], wg[P:D, :]),
                           (lam[:, :], lambda_1.partition_broadcast(P)), (lam2[:, :], lambda_2.partition_broadcast(P)),
                           (bgate[:, :], bg.partition_broadcast(P)),
                           (b1r[:, :], b1.rearrange("e (t p) -> (e t) p", p=P)),
                           (b2_sb[:, :], b2.rearrange("e d -> (e d)").partition_broadcast(P))):
                nc.scalar.dma_start(to, of).then_inc(S["consts_in"], 16)
                n += 1
            assert n == CONSTS

            def expert_weights(at, slot):
                if at.it is None and at.const == NG + 2 and slot == 8:
                    act.wait_ge(S["ffn_in"], 64)
                    act.wait_ge(S["t_ready"], NCH * NG)
                e = (at.const - NG - 2) * 2 + (slot - 8) // 2
                if at.it is None and slot in (8, 10) and 0 <= e < EXPERTS:
                    copy(w1s[:, e, :, 0, :], stage1[:, e], S["w1h_set"])
                    copy(w2s[:, e, 0, :], stage2[:, e], S["w2h_set"])
                if at.it is None and at.const == LAST and slot == SLOTS - 1:
                    nc.scalar.activation(sq[0:1, 0, 0:1], sumsq[0:1, 0:1], ACT.Gelu).then_inc(S["w2h_set"], 1)

            def step(at):
                for slot in range(SLOTS):
                    expert_weights(at, slot)
                    off, k = chunk_of(slot, LAG_T)
                    if at.active(off):
                        ge(act, S["t_ready"], at.val(off, NCH, k + 1))
                        ge(act, S["pv_done"], at.val(off, NCH, k - 3))
                        nc.scalar.activation(probs[k % 4][:, :], t_bank[k % TBANKS][:, :], ACT.Exp, scale=SCALE)\
                            .then_inc(S["p_ready"], 1)
                    def due(name):
                        return ACT_PLAN[name][0] == slot and at.active(ACT_PLAN[name][1])

                    for w in range(4):
                        if due(f"o{w}"):
                            off = ACT_PLAN[f"o{w}"][1]
                            ge(act, S["pv_done"], at.val(off, NCH, 3 * w + 3))
                            ge(act, S["ko_ready"], at.val(off, 4, w - 1))
                            copy(ot[w % 2][:, :], o_bank[w % 2][:, 0:3 * P], S["o_set"])
                    for t in range(3):
                        if due(f"qkh{t}"):
                            off = ACT_PLAN[f"qkh{t}"][1]
                            ge(act, S["f4_ready"], at.val(off, 3, t + 1))
                            ge(act, S["scr_w"], at.val(off, 32, 0))
                            copy(qkh[:, 2 * t:2 * t + 2, :].rearrange("p t n -> p (t n)"),
                                 misc[BANK_OF[f"F{4 + t}"]][:, :], S["qkh_set"])
                    if due("xT"):
                        off = ACT_PLAN["xT"][1]
                        ge(act, S["f3_ready"], at.val(off, 1, 1))
                        ge(act, S["v_ready"], at.val(off, 1, 0))
                        copy(xT[:, :, :].rearrange("p k n -> p (k n)"),
                             misc[BANK_OF["F3"]][:, :].bitcast(F16)[:, 0:3 * GT], S["xT_ready"])
                    if due("powersT"):
                        off = ACT_PLAN["powersT"][1]
                        ge(act, S["f1_ready"], at.val(off, 1, 1))
                        ge(act, S["f2_ready"], at.val(off, 1, 0))
                        copy(powersT[:, :], misc[BANK_OF["F1"]][0:TURNS * POLY, 0:GT], S["pwT_ready"])
                    if due("nmT"):
                        off = ACT_PLAN["nmT"][1]
                        ge(act, S["nm_ready"], at.val(off, 1, 1))
                        if at.active(off - 1):
                            ge(act, nm_in[at.par(off - 1)], at.turned(off - 1, 32))
                        copy(nmT[:, :], misc[BANK_OF["NM"]][:, :].bitcast(F16)[0:VH, 0:GT], S["nmT_set"])
                    if due("oh"):
                        off = ACT_PLAN["oh"][1]
                        ge(act, S["oo_set"], at.val(off, GB, GB))
                        ge(act, S["kt_ready"], at.val(off, 1, 0))
                        copy(os16[:, :, 0:D], oo[:, :, :], S["oh_set"])
                    if due("oT"):
                        off = ACT_PLAN["oT"][1]
                        ge(act, S["kt_ready"], at.val(off, 1, 1))
                        ge(act, S["kp_ready"], at.val(off, 1, 0))
                        copy(oT[:, :, :].rearrange("p k n -> p (k n)"),
                             misc[BANK_OF["KT"]][:, :].bitcast(F16)[:, 0:3 * GT], S["oT_set"])
                    if due("v"):
                        off = ACT_PLAN["v"][1]
                        ge(act, S["v_ready"], at.val(off, 1, 1))
                        ge(act, S["pv_done"], at.val(off, NCH, -2 * NCH))
                        copy(Vx[at.par(off)][:, :, :, 0:HD],
                             misc[BANK_OF["V"]][:, 0:GB * D].rearrange("p (b h d) -> p b h d", b=GB, h=HEADS), S["v_set"])
                    if due("xh"):
                        off = ACT_PLAN["xh"][1]
                        ge(act, S["xn_set"], at.val(off, GB, GB))
                        ge(act, S["f3_ready"], at.val(off, 1, 0))
                        copy(xs[:, :, 0:D], xn[:, :, :], S["xh_set"])
                    if due("sq"):
                        off = ACT_PLAN["sq"][1]
                        ge(act, S["rq_set"], at.val(off, 1, 0))
                        for b in range(GB):
                            ge(act, S["oo_set"], at.val(off, GB, b + 1))
                            ge(act, S["sq_set"], at.val(off, GB, b - 1))
                            nc.scalar.activation(sq[:, b, :], oo[:, b, :], ACT.Square,
                                                 accum_out=sumsq[:, b:b + 1]).then_inc(S["sq_set"], 1)
                    if due("x3h"):
                        off = ACT_PLAN["x3h"][1]
                        ge(act, S["xn3_set"], at.val(off, GB, GB))
                        copy(row[at.par(off)][:, :, 0:D].bitcast(F16)[:, :, 0:D], xn3[:, :, :], S["x3h_set"])
                    if due("gT"):
                        off = ACT_PLAN["gT"][1]
                        ge(act, S["kg_ready"], at.val(off, 1, 1))
                        ge(act, S["gl_ready"], at.val(off, 1, 0))
                        copy(gT[:, :, :].rearrange("p k n -> p (k n)"),
                             misc[BANK_OF["KG"]][:, :].bitcast(F16)[:, 0:3 * GT], S["gT_set"])

            over_steps(act, step)

            act.wait_ge(S["table_set"], 2)

            def expert_step(at):
                if at.active(1):
                    ge(act, S["tT_ready"], at.val(1, 1, 1))
                    ge(act, S["u_ready"], at.val(1, 3, -3))
                    copy(xe[at.par(1, 2)][:, :, :].rearrange("p k n -> p (k n)"),
                         misc[at.par(1, 2)][:, :].bitcast(F16)[:, 0:3 * GT], S["xe_set"])
                if at.active(0):
                    e = act.value_load(tab_e[0:1, bass.ds(at.val(0, 1, 0), 1)], min_val=0, max_val=EXPERTS - 1)
                    for k in range(3):
                        u = (3 * at.const + k) % 4
                        ge(act, S["hl_set"], at.val(0, 3, k - 3))
                        ge(act, S["u_ready"], at.val(0, 3, k + 1))
                        for t in range(2):
                            nc.scalar.activation(probs[u][:, t * GT:t * GT + GT], u_bank[u][:, t * GT:t * GT + GT],
                                                 ACT.Gelu, bias=b1T[:, bass.ds(e * HT + (2 * k + t), 1)])\
                                .then_inc(S["g_set"], 1)

            over_tiles(act, expert_step)

        @block.vector
        def _(dve):
            V = nc.vector
            dve.wait_ge(S["x_in_done"], 16)
            V.tensor_copy(x_f[:, :], x_in[:, :]).then_inc(S["ids_x"], 1)
            dve.wait_ge(S["ids_t"], 1)
            V.tensor_copy(ids[:, :], misc[0][:, 0:NB]).then_inc(S["ids_done"], 1)

            def prepare(at):
                if at.const == FIRST + 1:
                    dve.wait_ge(S["w_in"], 6 * 16)
                    V.tensor_copy(wqkv[:, :, 0, :], wst[:, :, :]).then_inc(S["wqkv_set"], 1)
                    dve.wait_ge(S["wqkv_set"], 1)
                    V.tensor_tensor(wqkv[:, :, 1, :], wst[:, :, :], wqkv[:, :, 0, :], ALU.subtract)\
                        .then_inc(S["wqkv_set"], 1)
                if FIRST < at.const <= FIRST + 3:
                    c = at.const - FIRST - 1
                    V.memset(Ks[c].rearrange("p t n -> p (t n)").bitcast(I32), ONES16).then_inc(S["ones_set"], 1)
                    V.memset(Vx[c][:, :, :, HD:HD + 1], 1.0).then_inc(S["w_scaled"], 1)
                if at.const == 1:
                    for c in range(2):
                        if c == 1:
                            dve.wait_ge(S["b1_ready"], 1)
                            V.tensor_copy(b1T[:, :], o_bank[1][:, 0:EXPERTS * HT]).then_inc(S["w_scaled"], 1)
                            dve.wait_ge(S["w_scaled"], 5)
                        V.memset(o_bank[c][:, :], 0.0).then_inc(S["w_scaled"], 1)
                    for r in range(2):
                        V.tensor_scalar(wpst[:, r, :], wpst[:, r, :], normw[:, r:r + 1], None, ALU.mult)\
                            .then_inc(S["w_scaled"], 1)
                    V.tensor_copy(wgs[:, :, 0, :], wgst[:, :, :]).then_inc(S["w_scaled"], 1)
                    V.tensor_tensor(lam[:, :], lam[:, :], lam2[:, :], ALU.subtract).then_inc(S["w_scaled"], 1)
                    dve.wait_ge(S["w_scaled"], 10)
                    V.tensor_tensor(wgs[:, :, 1, :], wgst[:, :, :], wgs[:, :, 0, :], ALU.subtract)\
                        .then_inc(S["w_scaled"], 1)
                    V.tensor_copy(wp[:, :, 0, :], wpst[:, :, :]).then_inc(S["w_scaled"], 1)
                    V.tensor_scalar(lam[:, :], lam[:, :], 0.1, None, ALU.add).then_inc(S["w_scaled"], 1)
                    dve.wait_ge(S["setup_pool"], 11)
                    V.tensor_copy(ekey[:, :], ekey_i[:, :]).then_inc(S["w_scaled"], 1)
                    V.tensor_copy(base[:, 0, :], base_i[:, :]).then_inc(S["w_scaled"], 1)
                    V.tensor_copy(first_row[:, :], base_i[:, :]).then_inc(S["w_scaled"], 1)
                    V.tensor_copy(steps_f[:, :], steps_i[:, :]).then_inc(S["w_scaled"], 1)
                    dve.wait_ge(S["w_scaled"], 17)
                    V.tensor_tensor(wp[:, :, 1, :], wpst[:, :, :], wp[:, :, 0, :], ALU.subtract)\
                        .then_inc(S["setup_dve"], 1)

            def expert_weights(e):
                dve.wait_ge(S["w1h_set"], e + 1)
                V.tensor_tensor(w1s[:, e, :, 1, :], stage1[:, e], w1s[:, e, :, 0, :], ALU.subtract)\
                    .then_inc(S["ffn_set"], 1)
                dve.wait_ge(S["w2h_set"], e + 1)
                V.tensor_tensor(w2s[:, e, 1, :], stage2[:, e], w2s[:, e, 0, :], ALU.subtract)\
                    .then_inc(S["ffn_set"], 1)

            def stats(src, st, mv, at, off, st_sem, mv_sem):
                for b in range(GB):
                    V.bn_stats(st[:, b, :], src[:, b, :]).then_inc(st_sem, 1)
                for b in range(GB):
                    apart(dve, st_sem, at.val(off, GB, b + 1))
                    V.bn_aggr(mv[:, b, :], st[:, b, :]).then_inc(mv_sem, 1)

            def apply(dst, src, mv, rs, done):
                for b in range(GB):
                    V.tensor_scalar(dst[:, b, :], src[:, b, :], mv[:, b, 0:1], rs[:, 1, b:b + 1],
                                    ALU.subtract, ALU.mult).then_inc(done, 1)

            def step(at):
                if at.it is None:
                    prepare(at)
                for slot in range(SLOTS):
                    slot_step(at, slot)
                    if at.it is None and at.const == LAST - 1 and slot in (0, 6):
                        expert_weights(slot // 6)

            def maxima(at, slot):
                if at.active(0):
                    b, cc = slot // CH, slot % CH
                    ge(dve, S["s_ready"], at.val(0, NCH, slot + 1))
                    if slot == 0:
                        ge(dve, S["nm_ready"], at.val(0, 1, -2))
                    V.tensor_reduce(nm[at.par(0)][:, b, :, 2 * cc:2 * cc + 2],
                                    s_bank[slot % 2][:, :].rearrange("n (a p m) -> n a p m", a=2, p=2),
                                    AX.X, ALU.max, negate=True).then_inc(S["s_used"], 1)

            def slot_step(at, slot):
                E = EXPERTS

                def due(name):
                    return DVE_PLAN[name][0] == slot and at.active(DVE_PLAN[name][1])

                for w in range(4):
                    if due(f"c{w}"):
                        off, b = DVE_PLAN[f"c{w}"][1], w // 2
                        o = misc[BANK_OF[f"KO{w}"]][:, 0:3 * P].rearrange("n (h r) -> n h r", r=32)
                        ge(dve, S["ko_ready"], at.val(off, 4, w + 1))
                        if w % 2 == 0:
                            V.reciprocal(rc1[:, :], o[:, :, HD]).then_inc(S["rc_set"], 1)
                        else:
                            V.reciprocal(rc2[:, 0, :], o[:, :, HD]).then_inc(S["rc2_set"], 1)
                if due("g1"):
                    off = DVE_PLAN["g1"][1]
                    ge(dve, S["gl_ready"], at.val(off, 1, 1))
                    V.tensor_tensor(lg[:, :, :], misc[BANK_OF["GL"]][:, 0:GB * E].rearrange("n (b e) -> n b e", b=GB),
                                    mid(bgate[:, :], GB), ALU.add).then_inc(S["lg_set"], 1)
                if due("g2"):
                    off = DVE_PLAN["g2"][1]
                    ge(dve, S["top_set"], at.val(off, 1, 1))
                    V.tensor_tensor(hit[:, :, :], lg[:, :, :], last(top[:, :], E), ALU.is_ge).then_inc(S["hit_set"], 1)
                if due("g3"):
                    off = DVE_PLAN["g3"][1]
                    ge(dve, S["hit_set"], at.val(off, 2, 2))
                    V.tensor_reduce(best[:, :], hit[:, :, :], AX.X, ALU.max).then_inc(S["best_set"], 1)
                if due("r1"):
                    off = DVE_PLAN["r1"][1]
                    ge(dve, S["rk_ready"], at.val(off, 1, 1))
                    ge(dve, S["base_set"], at.val(off, 1, 0))
                    V.tensor_tensor(base[:, 1, :], base[:, 0, :], misc[BANK_OF["RK"]][:, 2 * E:3 * E], ALU.add)\
                        .then_inc(S["base1_set"], 1)
                if due("r2"):
                    off = DVE_PLAN["r2"][1]
                    ge(dve, S["wh_set"], at.val(off, 1, 1))
                    V.tensor_tensor(base[:, 0, :], base[:, 1, :], misc[BANK_OF["RK"]][:, 3 * E:4 * E], ALU.add)\
                        .then_inc(S["base_set"], 1)
                    V.tensor_tensor(where2[:, :, :], where[:, :, :], chosen[:, :, :], ALU.mult).then_inc(S["wh2_set"], 1)
                    V.tensor_copy(row[at.par(off)][:, :, IDW:IDW + 1].bitcast(I32),
                                  token_no[:, bass.ds(at.val(off, GB, 0), GB)].unsqueeze(2)).then_inc(S["id_set"], 1)
                if due("r3"):
                    off = DVE_PLAN["r3"][1]
                    ge(dve, S["slotf_set"], at.val(off, 1, 1))
                    V.tensor_copy(slot_i[at.par(off)][:, :], slot_f[:, :]).then_inc(S["slot_set"], 1)

                maxima(at, slot)

                for w in range(4):
                    if due(f"c{w}"):
                        off, b = DVE_PLAN[f"c{w}"][1], w // 2
                        o = misc[BANK_OF[f"KO{w}"]][:, 0:3 * P].rearrange("n (h r) -> n h r", r=32)
                        if w % 2 == 0:
                            ge(dve, S["rc_set"], at.val(off, GB, b + 1))
                            V.tensor_tensor(o1[:, :, :], o[:, :, 0:HD], last(rc1[:, :], HD), ALU.mult)\
                                .then_inc(S["o1_set"], 1)
                        else:
                            ge(dve, S["rc2_set"], at.val(off, 2 * GB, 2 * b + 1))
                            V.tensor_tensor(rc2[:, 1, :], rc2[:, 0, :], lam[:, :], ALU.mult).then_inc(S["rc2_set"], 1)
                            ge(dve, S["rc2_set"], at.val(off, 2 * GB, 2 * b + 2))
                            V.tensor_tensor(o2[:, :, :], o[:, :, 0:HD], last(rc2[:, 1, :], HD), ALU.mult)\
                                .then_inc(S["o2_set"], 1)
                            ge(dve, S["o2_set"], at.val(off, GB, b + 1))
                            ge(dve, S["o1_set"], at.val(off, GB, b + 1))
                            if b == 0:
                                ge(dve, S["os_set"], at.val(off, 2, 0))
                                ge(dve, S["sq_set"], at.val(off, GB, 0))
                            V.tensor_tensor(oo[:, b, :].rearrange("n (h d) -> n h d", d=HD), o1[:, :, :], o2[:, :, :],
                                            ALU.subtract).then_inc(S["oo_set"], 1)
                if due("g1"):
                    off = DVE_PLAN["g1"][1]
                    ge(dve, S["lg_set"], at.val(off, 1, 1))
                    V.tensor_reduce(top[:, :], lg[:, :, :], AX.X, ALU.max).then_inc(S["top_set"], 1)
                if due("g2"):
                    off = DVE_PLAN["g2"][1]
                    ge(dve, S["hit_set"], at.val(off, 2, 1))
                    V.tensor_tensor(hit[:, :, :], hit[:, :, :], mid(ekey[:, :], GB), ALU.mult).then_inc(S["hit_set"], 1)
                if due("g3"):
                    off = DVE_PLAN["g3"][1]
                    ge(dve, S["best_set"], at.val(off, 1, 1))
                    ge(dve, S["wh2_set"], at.val(off, 1, 0))
                    V.tensor_tensor(chosen[:, :, :], hit[:, :, :], last(best[:, :], E), ALU.is_equal)\
                        .then_inc(S["chosen_set"], 1)
                if due("r1"):
                    off = DVE_PLAN["r1"][1]
                    ge(dve, S["base1_set"], at.val(off, 1, 1))
                    V.tensor_tensor(where[:, :, :], misc[BANK_OF["RK"]][:, 0:GB * E].rearrange("n (b e) -> n b e", b=GB),
                                    base[:, :, :], ALU.add).then_inc(S["wh_set"], 1)
                if due("r2"):
                    off = DVE_PLAN["r2"][1]
                    ge(dve, S["wh2_set"], at.val(off, 1, 1))
                    V.tensor_reduce(slot_f[:, :], where2[:, :, :], AX.X, ALU.add).then_inc(S["slotf_set"], 1)
                for t in range(3):
                    if due(f"qkl{t}"):
                        off = DVE_PLAN[f"qkl{t}"][1]
                        ge(dve, S["qkh_set"], at.val(off, 3, t + 1))
                        V.tensor_tensor(qkl[:, 2 * t:2 * t + 2, :].rearrange("p t n -> p (t n)"),
                                        misc[BANK_OF[f"F{4 + t}"]][:, :],
                                        qkh[:, 2 * t:2 * t + 2, :].rearrange("p t n -> p (t n)"), ALU.subtract)\
                            .then_inc(S["qkl_set"], 1)
                if due("E1"):
                    off = DVE_PLAN["E1"][1]
                    ge(dve, S["f2_ready"], at.val(off, 1, 1))
                    ge(dve, S["e1_set"], at.val(off, GB, 0))
                    V.tensor_tensor(emb[:, :, :], misc[BANK_OF["F2"]][:, 0:GB * D].rearrange("n (b d) -> n b d", b=GB),
                                    mid(pos_sb[:, :], GB), ALU.add).then_inc(S["emb_set"], 1)
                    ge(dve, S["emb_set"], at.val(off, 1, 1))
                    ge(dve, S["v1_set"], at.val(off, 1, 0))
                    stats(emb, bst, mv1, at, off, S["st1_set"], S["mv1_set"])
                if due("h1"):
                    off = DVE_PLAN["h1"][1]
                    c = at.par(off)
                    ge(dve, S["kp_ready"], at.val(off, 1, 1))
                    ge(dve, S["rms_set"], at.val(off, 1, 1))
                    if at.active(off - 3):
                        ge(dve, rows_out[c], at.turned(off - 3, 32))
                    for b in range(GB):
                        V.scalar_tensor_tensor(
                            out=row[c][:, b, D:2 * D], in0=misc[BANK_OF["KP"]][:, b * D:b * D + D],
                            scalar=rms[:, 1, b:b + 1],
                            in1=hb[:, bass.ds(at.val(off, GB, b), 1), :].rearrange("n o d -> n (o d)"),
                            op0=ALU.mult, op1=ALU.add).then_inc(S["h1_set"], 1)
                if due("st3"):
                    off = DVE_PLAN["st3"][1]
                    ge(dve, S["h1_set"], at.val(off, GB, GB))
                    ge(dve, S["v3_set"], at.val(off, 1, 0))
                    stats(row[at.par(off)][:, :, D:2 * D], bst3, mv3, at, off, S["st3_set"], S["mv3_set"])
                if due("E2"):
                    off = DVE_PLAN["E2"][1]
                    ge(dve, S["rs1_set"], at.val(off, 1, 1))
                    ge(dve, S["gm_set"], at.val(off, 1, 0))
                    apply(e1, emb, mv1, rs1, S["e1_set"])
                if due("xn3"):
                    off = DVE_PLAN["xn3"][1]
                    ge(dve, S["rs3_set"], at.val(off, 1, 1))
                    ge(dve, S["x3_set"], at.val(off, 2, 0))
                    apply(xn3, row[at.par(off)][:, :, D:2 * D], mv3, rs3, S["xn3_set"])
                if due("st2"):
                    off = DVE_PLAN["st2"][1]
                    ge(dve, S["h0_set"], at.val(off, 1, 1))
                    ge(dve, S["v2_set"], at.val(off, 1, 0))
                    stats(h0, bst2, mv2, at, off, S["st2_set"], S["mv2_set"])
                if due("xn"):
                    off = DVE_PLAN["xn"][1]
                    ge(dve, S["rs2_set"], at.val(off, 1, 1))
                    ge(dve, S["xs_set"], at.val(off, 2, 0))
                    apply(xn, h0, mv2, rs2, S["xn_set"])

            over_steps(dve, step)

            steps_256, tiles_ = steps_f[:, 0:MAXT], steps_f[:, MAXT:MAXT + TILES]
            done = 0

            def link(ins):
                nonlocal done
                done += 1
                ins.then_inc(S["table"], 1)
                dve.wait_ge(S["table"], done)

            dve.wait_ge(S["base_set"], NG)
            V.tensor_copy(pad_at[:, :], base[0:1, 0, :]).then_inc(S["pads_set"], 1)
            link(V.tensor_tensor(cnt[:, :], base[0:1, 0, :], first_row[0:1, :], ALU.subtract))
            link(V.tensor_tensor(over[:, :, :], last(cnt[:, :], MAXT), mid(steps_256, EXPERTS), ALU.is_gt))
            link(V.tensor_reduce(tl[:, :], over[:, :, :], AX.X, ALU.add))
            link(V.tensor_copy(cum[:, 0:1], tl[:, 0:1]))
            for e in range(1, EXPERTS):
                link(V.tensor_tensor(cum[:, e:e + 1], cum[:, e - 1:e], tl[:, e:e + 1], ALU.add))
            link(V.tensor_tensor(past[:, :, :], last(tiles_, EXPERTS), mid(cum[:, :], TILES), ALU.is_ge))
            link(V.tensor_reduce(ef[:, :], past[:, :, 0:EXPERTS - 1], AX.X, ALU.add))
            V.tensor_copy(tab_e[:, :], ef[:, :]).then_inc(S["table_set"], 1)
            link(V.tensor_tensor(skips[:, :, :], past[:, :, :], mid(tl[:, :], TILES), ALU.mult))
            link(V.tensor_reduce(skip[:, :], skips[:, :, 0:EXPERTS - 1], AX.X, ALU.add))
            link(V.scalar_tensor_tensor(out=tr[0][:, :], in0=ef[:, :], scalar=float(CAP // TILE), in1=tiles_,
                                        op0=ALU.mult, op1=ALU.add))
            link(V.tensor_tensor(tr[1][:, :], tr[0][:, :], skip[:, :], ALU.subtract))
            link(V.tensor_scalar(tr[2][:, :], tr[1][:, :], -1.0, float(EXPERTS * CAP // TILE), ALU.mult, ALU.add))
            link(V.tensor_tensor(tr[3][:, :], tr[2][:, :], past[:, :, EXPERTS - 1], ALU.mult))
            link(V.tensor_tensor(tr[4][:, :], tr[1][:, :], tr[3][:, :], ALU.add))
            V.tensor_scalar(tab_row[:, :], tr[4][:, :], float(TILE), None, ALU.mult).then_inc(S["table_set"], 1)
            for e in range(2, EXPERTS):
                expert_weights(e)
            dve.wait_ge(S["table_set"], 2)

            def expert_step(at):
                if at.active(0):
                    for k in range(3):
                        c, g = at.par(0, 2), probs[(3 * at.const + k) % 4]
                        g = g[:, :].rearrange("p (t n) -> p t n", t=2)
                        ge(dve, S["g_set"], at.val(0, 6, 2 * k + 2))
                        V.tensor_copy(hid[:, c, 0, 2 * k:2 * k + 2, :], g).then_inc(S["hh_set"], 1)
                        ge(dve, S["hh_set"], at.val(0, 3, k + 1))
                        V.tensor_tensor(hid[:, c, 1, 2 * k:2 * k + 2, :], g, hid[:, c, 0, 2 * k:2 * k + 2, :],
                                        ALU.subtract).then_inc(S["hl_set"], 1)
                if at.active(-1):
                    c = at.par(-1, 2)
                    e = dve.value_load(tab_e[0:1, bass.ds(at.val(-1, 1, 0), 1)], min_val=0, max_val=EXPERTS - 1)
                    ge(dve, S["dn_ready"], at.val(-1, 1, 1))
                    ge(dve, S["y_set"], at.val(-1, 1, 0))
                    V.tensor_tensor(ysum[:, :, :], o_bank[c][:, 0:GB * D].rearrange("n (j d) -> n j d", j=2),
                                    mid(b2_sb[:, bass.ds(e * D, D)], 2), ALU.add).then_inc(S["ysum_set"], 1)
                    ge(dve, S["ysum_set"], at.val(-1, 1, 1))
                    if at.active(-3):
                        ge(dve, outs[c], at.turned(-3, 32, 2))
                    V.tensor_copy(tokens[:, c, :].unsqueeze(2), row[at.par(-1, 4)][:, :, IDW:IDW + 1].bitcast(I32))\
                        .then_inc(S["token_set"], 1)
                    V.tensor_tensor(xn_e[c][:, :, :], ysum[:, :, :], row[at.par(-1, 4)][:, :, D:2 * D], ALU.add)\
                        .then_inc(S["y_set"], 1)

            over_tiles(dve, expert_step)


_INS = ['x', 'L0_tok_turns', 'L0_tok_poly_coeffs', 'L0_tok_pos_table', 'L0_tok_ln_gamma', 'L0_tok_ln_beta',
        'L0_attn_W_qkv1', 'L0_attn_W_qkv2', 'L0_attn_W_proj', 'L0_attn_b_proj', 'L0_attn_norm_w', 'L0_attn_lambda_1',
        'L0_attn_lambda_2', 'L0_attn_xpos', 'L0_ffn_Wg', 'L0_ffn_bg', 'L0_ffn_W1', 'L0_ffn_b1', 'L0_ffn_W2', 'L0_ffn_b2']


def kernel(**inputs):
    import numpy as np
    import concourse.bacc as bacc
    from concourse.bass_utils import run_bass_kernel_spmd

    nc = bacc.Bacc("TRN2", target_bir_lowering=False, num_devices=1)
    arrays, args = {}, []
    for name in _INS:
        a = np.ascontiguousarray(inputs[name])
        arrays[f"in_{name}_dram"] = a
        args.append(nc.dram_tensor(f"in_{name}_dram", a.shape, mybir.dt.from_np(a.dtype), kind="ExternalInput").ap())
    args.append(nc.dram_tensor("out_0_dram", (NB, P, D), F32, kind="ExternalOutput").ap())
    build(nc, *args)
    r = run_bass_kernel_spmd(nc, [arrays], core_ids=[0])
    return r.results[0]["out_0_dram"]
```

```python
from contextlib import ExitStack

import concourse.bass as bass
from concourse import mybir

ALU = mybir.AluOpType
ACT = mybir.ActivationFunctionType
AX = mybir.AxisListType
F32 = mybir.dt.float32
F16 = mybir.dt.float16
I32 = mybir.dt.int32

P = 128
NB = 64
GB = 2
NG = NB // GB
GT = GB * P
D = 192
TAIL = D - P
HEADS, HD = 12, 16
VH = 2 * HEADS
PAIRS = VH // 2
CH = 6
NCH = CH * GB
TURNS, POLY = 8, 5
SPLIT = 2 * D
QK = 4 * D
WC = QK + D
HIDDEN, EXPERTS = 768, 4
HT = HIDDEN // P
TOK = NB * P
TILE = 256
TILES = TOK // TILE + EXPERTS - 1
CAP = TOK + TILE
ROWS = EXPERTS * CAP + TILE
ROW = D + D + 16
NO_TOKEN = 1 << 20
ONES16 = 0x3C003C00
IDW = 2 * D
SCALE = HD ** -0.5
CONSTS = 14
MAXT = TOK // TILE
STAGE = EXPERTS * 2 * HIDDEN + EXPERTS * HIDDEN // P * D
SLOTS = NCH
TBANKS, OBANKS = 1, 1
LAG_T, LAG_PV = 17, 19

PE_PLAN = {"F5b": (0, 1), "F1": (0, 3), "NM": (1, -1), "F6a": (1, 1), "RK": (1, -5), "F6b": (2, 1), "KO1": (2, -2),
           "KT": (3, -3), "F2": (3, 3), "KO2": (5, -2), "KG": (5, -4), "KPa": (5, -3), "Va": (6, 1),
           "KPb": (6, -3), "F3": (7, 2), "Vb": (8, 1), "KO3": (9, -2), "GL": (9, -4), "F4a": (9, 2),
           "F4b": (10, 2), "KO0": (10, -1), "F5a": (11, 2)}
ACT_PLAN = {"xT": (8, 2), "qkh0": (10, 2), "qkh1": (1, 1), "qkh2": (3, 1), "nmT": (1, -1), "o0": (9, -1),
            "o1": (0, -2), "o2": (3, -2), "o3": (6, -2), "powersT": (1, 3), "oT": (4, -3), "v": (8, 1),
            "sq0": (7, -2), "sq1": (0, -3), "oh": (1, -3), "x3h": (2, -4), "gT": (6, -4), "xh0": (2, 2),
            "xh1": (4, 2)}
DVE_PLAN = {"m0": (5, -2), "m1": (10, -2), "oo0": (6, -2), "oo1": (11, -2), "st1": (5, 3), "ag1": (6, 3),
            "ag2": (11, 3), "ag3": (10, -3), "qkl0": (0, 1), "qkl1": (1, 1), "qkl2": (4, 1), "c0": (11, -1),
            "c1": (3, -2), "c2": (8, -2), "c3": (9, -2), "E1": (4, 3), "E2": (6, 3), "st2": (10, 3), "h1": (8, -3),
            "st3": (9, -3), "xn3": (1, -4), "g1": (9, -4), "g2": (10, -4), "g3": (11, -4), "r1": (2, -5),
            "r2": (3, -5), "r3": (4, -5)}
POOL_PLAN = {"SO": (1, -3), "rms": (1, -3), "scatter": (4, -5), "R2": (11, 3), "XL": (5, 2), "R1": (5, 3),
             "gather": (7, 4), "R3": (0, -4), "H0": (8, 3), "PW": (9, 4), "X3L": (2, -4)}
PE_TASKS = sorted(PE_PLAN, key=lambda name: PE_PLAN[name][0])
MISC = 4
BANK_OF = {"F1": 1, "NM": 3, "F6": 0, "RK": 1, "KT": 2, "KO1": 3, "F2": 1, "KO2": 2, "KG": 0, "KP": 3, "V": 1,
           "F3": 0, "KO3": 2, "GL": 3, "F4": 0, "F5": 2, "KO0": 3}
READ_BY = {"F1": ("pwT_ready", 1, 1), "F2": ("emb_set", 1, 1), "F3": ("xT_ready", 1, 1), "F4": ("qkl_set", 3, 1),
           "F5": ("qkl_set", 3, 2), "F6": ("qkl_set", 3, 3), "V": ("v_set", 1, 1), "NM": ("nmT_set", 1, 1),
           "KO0": ("o1_set", 2, 1), "KO1": ("o2_set", 2, 1), "KO2": ("o1_set", 2, 2), "KO3": ("o2_set", 2, 2),
           "RK": ("base_set", 1, 1), "KT": ("oT_set", 1, 1), "KP": ("h1_set", 2, 2), "KG": ("gT_set", 1, 1),
           "GL": ("lg_set", 1, 1)}
FIRST, LAST = -4, NG + 4
LOOP0, UNROLL = 7, 3
TRIPS = (NG - 4 - LOOP0) // UNROLL
UNROLL_B, LOOP0_B = 4, 3
TRIPS_B = (TILES - 1 - LOOP0_B) // UNROLL_B




class At:

    def __init__(self, it, const, count=NG, unroll=UNROLL):
        self.it, self.const, self.count, self.unroll = it, const, count, unroll

    def active(self, off):
        return self.it is not None or 0 <= self.const + off < self.count

    def before(self):
        return At(self.it, self.const - 1, self.count, self.unroll)

    def par(self, off, n=3):
        return (self.const + off) % n

    def val(self, off, mul, add):
        v = mul * (self.const + off) + add
        assert self.it is None or v > 0
        return v if self.it is None else self.it * (self.unroll * mul) + v

    def turned(self, off, per, n=3):
        v = per * ((self.const + off) // n + 1)
        assert self.it is None or v > 0
        return v if self.it is None else self.it * (self.unroll // n * per) + v


def ge(eng, sem, value):
    if not isinstance(value, int) or value > 0:
        eng.wait_ge(sem, value)


def over_steps(eng, step):
    for s in range(FIRST, LOOP0):
        step(At(None, s))
    with eng.Fori(0, TRIPS) as it:
        for j in range(UNROLL):
            step(At(it, LOOP0 + j))
    for s in range(LOOP0 + UNROLL * TRIPS, LAST + 1):
        step(At(None, s))


def over_tiles(eng, step):
    for s in range(-1, LOOP0_B):
        step(At(None, s, TILES, UNROLL_B))
    with eng.Fori(0, TRIPS_B) as it:
        for j in range(UNROLL_B):
            step(At(it, LOOP0_B + j, TILES, UNROLL_B))
    for s in range(LOOP0_B + UNROLL_B * TRIPS_B, TILES + 1):
        step(At(None, s, TILES, UNROLL_B))


def chunk_of(slot, lag):
    n = slot - lag
    return n // NCH, n % NCH


def build(nc, x, turns, poly, pos_table, ln_gamma, ln_beta, w_qkv1, w_qkv2, w_proj, b_proj, norm_w,
          lambda_1, lambda_2, xpos, wg, bg, w1, b1, w2, b2, out):
    ctx = ExitStack()
    with ctx:
        def sb(name, shape, dt):
            return ctx.enter_context(nc.sbuf_tensor(name, shape, dt))

        def bank(name, dt=F32):
            return ctx.enter_context(nc.psum_tensor(name, [P, 2048 // (4 if dt == F32 else 2)], dt))

        def sem(name):
            return ctx.enter_context(nc.semaphore(name))

        def mid(ap, n):
            return ap.unsqueeze(1).broadcast_to([ap.shape[0], n, ap.shape[1]])

        def last(ap, n):
            return ap.unsqueeze(len(ap.shape)).broadcast_to([*ap.shape, n])

        ident = sb("ident", [P, P], F32)
        ident16 = sb("ident16", [P, P], F16)
        earlier = sb("earlier", [P, P], F16)
        ones16 = sb("ones16", [P, P], F16)
        token_no = sb("token_no", [P, NB], I32)
        x_in = sb("x_in", [NB, P], I32)
        x_f = sb("x_f", [NB, P], F32)
        ids = sb("ids", [P, NB], I32)
        poly_sb = sb("poly_sb", [TURNS * POLY, D], F32)
        pos_sb = sb("pos_sb", [P, D], F32)
        gamma = sb("gamma", [P, D], F32)
        beta = sb("beta", [P, D], F32)
        bproj = sb("bproj", [P, D], F32)
        lam = sb("lam", [P, HEADS], F32)
        lam2 = sb("lam2", [P, HEADS], F32)
        bgate = sb("bgate", [P, EXPERTS], F32)
        normw = sb("normw", [P, 2], F32)
        mhalf = sb("mhalf", [P, GB], F32)
        wst = sb("wst", [P, 2, WC], F32)
        wqkv = sb("wqkv", [P, 2, 2, WC], F16)
        wpst = sb("wpst", [P, 2, D], F32)
        wp = sb("wp", [P, 2, 2, D], F16)
        wgst = sb("wgst", [P, 2, EXPERTS], F32)
        wgs = sb("wgs", [P, 2, 2, EXPERTS], F16)
        zrow = sb("zrow", [PAIRS, GT], F16)

        idx = sb("idx", [P, 3, GB], I32)
        turn = sb("turn", [P, 3, GB, TURNS], F32)
        powers = sb("powers", [P, GB, TURNS, POLY], F32)
        powersT = sb("powersT", [TURNS * POLY, GT], F32)
        emb = sb("emb", [P, GB, D], F32)
        bst = sb("bst", [P, GB, 6], F32)
        mv1 = sb("mv1", [P, GB, 2], F32)
        mv2 = sb("mv2", [P, GB, 2], F32)
        mv3 = sb("mv3", [P, GB, 2], F32)
        bst2 = sb("bst2", [P, GB, 6], F32)
        bst3 = sb("bst3", [P, GB, 6], F32)
        rs1 = sb("rs1", [P, 2, GB], F32)
        rs2 = sb("rs2", [P, 2, GB], F32)
        rs3 = sb("rs3", [P, 2, GB], F32)
        nb2 = sb("nb2", [P, 2, GB], F32)
        rms = sb("rms", [P, 2, GB], F32)
        sumsq = sb("sumsq", [P, GB], F32)
        sq = sb("sq", [P, GB, D], F32)
        e1 = sb("e1", [P, GB, D], F32)
        e2 = sb("e2", [P, GB, D], F32)
        h0 = sb("h0", [P, GB, D], F32)
        hb = sb("hb", [P, NB, D], F32)
        xn = sb("xn", [P, GB, D], F32)
        xs = sb("xs", [P, GB, SPLIT], F16)
        xT = sb("xT", [P, 3, GT], F16)
        qkh = sb("qkh", [P, 6, GT], F16)
        qkl = sb("qkl", [P, 6, GT], F16)
        Qs_all = sb("Qs_all", [P, 3, PAIRS, 2, GT], F16)
        Ks_all = sb("Ks_all", [P, 3, PAIRS, GT], F16)
        Qs = [Qs_all[:, c] for c in range(3)]
        Ks = [Ks_all[:, c] for c in range(3)]
        Vx = [sb(f"Vx{c}", [P, GB, HEADS, HD + 1], F32) for c in range(3)]
        nm = [sb(f"nm{c}", [P, GB, 2, PAIRS], F16) for c in range(3)]
        nmT = sb("nmT", [VH, GT], F16)
        probs = [sb(f"probs{c}", [P, 512], F32) for c in range(4)]
        ot = [sb(f"ot{c}", [P, 3 * P], F32) for c in range(2)]
        rc1 = sb("rc1", [P, HEADS], F32)
        rc2 = sb("rc2", [P, 2, HEADS], F32)
        o1 = sb("o1", [P, HEADS, HD], F32)
        o2 = sb("o2", [P, HEADS, HD], F32)
        oo = sb("oo", [P, GB, D], F32)
        os16 = sb("os16", [P, GB, SPLIT], F16)
        oT = sb("oT", [P, 3, GT], F16)
        row = [sb(f"row{c}", [P, GB, ROW], F32) for c in range(4)]
        xn3 = sb("xn3", [P, GB, D], F32)
        gT = sb("gT", [P, 3, GT], F16)
        ekey = sb("ekey", [P, EXPERTS], F32)
        ekey_i = sb("ekey_i", [P, EXPERTS], I32)
        base_i = sb("base_i", [P, EXPERTS], I32)
        base = sb("base", [P, GB, EXPERTS], F32)
        lg = sb("lg", [P, GB, EXPERTS], F32)
        top = sb("top", [P, GB], F32)
        hit = sb("hit", [P, GB, EXPERTS], F32)
        best = sb("best", [P, GB], F32)
        chosen = sb("chosen", [P, GB, EXPERTS], F16)
        where = sb("where", [P, GB, EXPERTS], F32)
        where2 = sb("where2", [P, GB, EXPERTS], F32)
        slot_f = sb("slot_f", [P, GB], F32)
        slot_i = [sb(f"slot_i{c}", [P, GB], I32) for c in range(3)]

        tokens = sb("tokens", [P, 2, 2], I32)
        b1r = sb("b1r", [EXPERTS * HT, P], F32)
        b1T = sb("b1T", [P, EXPERTS * HT], F32)
        b2_sb = sb("b2_sb", [P, EXPERTS * D], F32)
        steps_i = sb("steps_i", [1, MAXT + TILES], I32)
        steps_f = sb("steps_f", [1, MAXT + TILES], F32)
        first_row = sb("first_row", [P, EXPERTS], F32)
        cnt = sb("cnt", [1, EXPERTS], F32)
        over = sb("over", [1, EXPERTS, MAXT], F32)
        tl = sb("tl", [1, EXPERTS], F32)
        cum = sb("cum", [1, EXPERTS], F32)
        past = sb("past", [1, TILES, EXPERTS], F32)
        skips = sb("skips", [1, TILES, EXPERTS], F32)
        ef = sb("ef", [1, TILES], F32)
        skip = sb("skip", [1, TILES], F32)
        tr = [sb(f"tr{c}", [1, TILES], F32) for c in range(5)]
        tab_e = sb("tab_e", [1, TILES], I32)
        tab_row = sb("tab_row", [1, TILES], I32)
        pad_at = sb("pad_at", [1, EXPERTS], I32)

        stage = hb[:, 0:STAGE // D, :].rearrange("p n d -> p (n d)")
        W1N, W2N = EXPERTS * 2 * HIDDEN, EXPERTS * HT * D
        stage1 = stage[:, 0:W1N].rearrange("p (e r h) -> p e r h", e=EXPERTS, r=2)
        stage2 = stage[:, W1N:W1N + W2N].rearrange("p (e n) -> p e n", e=EXPERTS)
        w1f = Qs_all[:, 0:2].rearrange("p c t a n -> p (c t a n)")
        w2f = Ks_all[:, :].rearrange("p c t n -> p (c t n)")
        w1s = w1f.rearrange("p (e r x h) -> p e r x h", e=EXPERTS, r=2, x=2)
        w2s = w2f.rearrange("p (e x n) -> p e x n", e=EXPERTS, x=2)
        hid = Qs[2].rearrange("p t a n -> p (t a n)").rearrange("p (c x k n) -> p c x k n", c=2, x=2, k=HT)
        xe, xn_e, ysum = (xT, oT), (xn, xn3), e1

        s_bank = [bank(f"s_bank{c}") for c in range(2)]
        t_bank = [bank(f"t_bank{c}") for c in range(TBANKS)]
        o_bank = [bank(f"o_bank{c}") for c in range(OBANKS)]
        misc = [bank(f"misc{c}") for c in range(MISC)]
        u_bank, y_bank = s_bank + t_bank + misc[2:3], o_bank + misc[3:4]

        qk_dram = nc.dram_tensor("qk_dram", [2, QK, GT], F16, kind="Internal").ap()
        routed = nc.dram_tensor("routed", [ROWS, ROW], F32, kind="Internal").ap()

        names = ("x_in_done emb_in consts_in w_in wqkv_set ones_set pads_set setup_pool ids_t ids_x ids_done "
                 "setup_dve w_scaled small_set zero_set idx_set pw_set pw1 pw2 pw_ready f1_ready pwT_ready f2_ready "
                 "emb_set st1_set mv1_set v1_set rs1_set e1_set gm_set h0_set hb_set st2_set mv2_set v2_set "
                 "rs2_set nb2_set xn_set xh_set xs_set f3_ready xT_ready f4_ready qkh_set qkl_set v_ready v_set "
                 "scr_w1 scr_w2 s_ready s_used nm_ready nmT_set t_ready p_ready pv_done o_set ko_ready rc_set "
                 "o1_set rc2_set o2_set oo_set sq_set rq_set rms_set oh_set os_set kt_ready oT_set kp_ready h1_set "
                 "st3_set mv3_set v3_set rs3_set xn3_set x3h_set x3_set kg_ready gT_set gl_ready lg_set top_set "
                 "hit_set best_set chosen_set rk_ready wh_set wh2_set slotf_set slot_set base_set base1_set id_set "
                 "waits_apart b1_ready table table_set pads_out ffn_in w1h_set w2h_set ffn_set tT_ready xe_set "
                 "u_ready g_set hh_set hl_set dn_ready ysum_set token_set y_set").split()
        S = {n: sem(n) for n in names}
        turns_in = [sem(f"turns_in{c}") for c in range(3)]
        ops_in = [sem(f"ops_in{c}") for c in range(3)]
        nm_in = [sem(f"nm_in{c}") for c in range(3)]
        rows_out = [sem(f"rows_out{c}") for c in range(3)]
        tile_in = [sem(f"tile_in{c}") for c in range(4)]
        outs = [sem(f"outs{c}") for c in range(2)]

        def apart(eng, sem_, value):
            if isinstance(value, int):
                ge(eng, sem_, value)
            else:
                eng.wait_ge(sem_, value).then_inc(S["waits_apart"], 1)

        def write_pads(eng, experts):
            eng.wait_ge(S["pads_set"], 1)
            for e in experts:
                start = eng.value_load(pad_at[0:1, e:e + 1], min_val=e * CAP, max_val=e * CAP + TOK)
                eng.dma_start(routed[bass.ds(start, TILE)].rearrange("(p j) w -> p j w", j=2), row[3][:, :, :])\
                    .then_inc(S["pads_out"], 16)

        block = ctx.enter_context(nc.Block())

        @block.sync
        def _(sp):
            sp.dma_start(x_in[:, :], x).then_inc(S["x_in_done"], 16)
            for to, of in ((poly_sb[:, :], poly.rearrange("t p d -> (t p) d")), (pos_sb[:, :], pos_table[0:P, :]),
                           (gamma[:, :], ln_gamma.partition_broadcast(P)), (beta[:, :], ln_beta.partition_broadcast(P)),
                           (bproj[:, :], b_proj.partition_broadcast(P))):
                sp.dma_start(to, of).then_inc(S["emb_in"], 16)
            for rows, src, r in ((slice(0, P), slice(0, P), 0), (slice(0, TAIL), slice(P, D), 1),
                                 (slice(TAIL, P), slice(P, D), 1)):
                cols = wst[rows, r, :].rearrange("p (s d) -> p s d", d=D)
                sp.dma_start(cols[:, 0::2], w_qkv1[src, :].rearrange("p (s d) -> p s d", d=D)).then_inc(S["w_in"], 16)
                sp.dma_start(cols[:, 1::2], w_qkv2[src, 0:2 * D].rearrange("p (s d) -> p s d", d=D))\
                    .then_inc(S["w_in"], 16)
            def fixed(value):
                return value if isinstance(value, int) else sp.snap(value)

            def expert_weights():
                sp.wait_ge(S["h1_set"], STAGE // D)
                sp.wait_ge(S["small_set"], 7)
                sp.dma_start(routed[EXPERTS * CAP:ROWS].rearrange("(p j) w -> p j w", j=2), row[3][:, :, :])\
                    .then_inc(S["pads_out"], 16)
                sp.dma_start(stage1[:, :, 0, :], w1[:, 0:P, :].rearrange("e p h -> p e h")).then_inc(S["ffn_in"], 16)
                for r in (0, TAIL):
                    sp.dma_start(stage1[r:r + TAIL, :, 1, :], w1[:, P:D, :].rearrange("e p h -> p e h"))\
                        .then_inc(S["ffn_in"], 16)
                sp.dma_start(stage2.rearrange("p e (k d) -> p e k d", d=D),
                             w2.rearrange("e (k p) d -> p e k d", p=P)).then_inc(S["ffn_in"], 16)

            def step(at):
                if at.it is None and at.const == NG:
                    expert_weights()
                v_nm, v_qk1, v_qk = fixed(at.val(-1, 1, 1)), fixed(at.val(1, 3, 2)), fixed(at.val(1, 3, 3))
                v_scr, v_t = fixed(at.val(1, 32, 32)), fixed(at.val(1, NCH, -2 * NCH))
                neg_max(at, v_nm)
                if at.active(1):
                    apart(sp, S["qkh_set"], v_qk1)
                    apart(sp, S["qkl_set"], v_qk1)
                    to_dram(0, 4, S["scr_w1"])
                    apart(sp, S["qkh_set"], v_qk)
                    apart(sp, S["qkl_set"], v_qk)
                    to_dram(4, 6, S["scr_w2"])
                    c = at.par(1)
                    apart(sp, S["t_ready"], v_t)
                    if at.it is None and at.const + 1 < 3:
                        sp.wait_ge(S["zero_set"], at.const + 2)
                        sp.wait_ge(S["ones_set"], at.const + 2)
                    apart(sp, S["scr_w1"], v_scr)
                    stack(c, 0, (0, 0, 1))
                    for a in range(2):
                        sp.dma_start(Qs[c][64 * a + 48:64 * a + 49, :, a, :], zrow[:, :]).then_inc(ops_in[c], 16)
                    apart(sp, S["scr_w1"], v_scr)
                    apart(sp, S["scr_w2"], v_scr)
                    stack(c, 1, (0, 1, 0))

            def to_dram(t0, t1, done):
                for part, t in ((0, qkh), (1, qkl)):
                    sp.dma_start(qk_dram[part].rearrange("(t p) n -> p t n", p=P)[:, t0:t1], t[:, t0:t1, :])\
                        .then_inc(done, 16)

            def stack(c, side, parts):
                for a in range(2):
                    for r, part in enumerate(parts):
                        rows = slice(64 * a + HD * r, 64 * a + HD * r + HD)
                        src = qk_dram[part, side * 2 * D:(side + 1) * 2 * D].rearrange(
                            "(p a d) n -> a d p n", a=2, d=HD)[a]
                        sp.dma_start(Qs[c][rows, :, a, :] if side == 0 else Ks[c][rows, :, :], src)\
                            .then_inc(ops_in[c], 16)

            def neg_max(at, v_nm):
                if at.active(-1):
                    c = at.par(-1)
                    ge(sp, S["nmT_set"], v_nm)
                    for a in range(2):
                        sp.dma_start(Qs[c][64 * a + 48:64 * a + 49, :, a, :],
                                     nmT[PAIRS * a:PAIRS * a + PAIRS, :]).then_inc(nm_in[c], 16)

            over_steps(sp, step)
            write_pads(sp, (0, 1))
            sp.wait_ge(S["pads_out"], 16 * (EXPERTS + 1))
            sp.wait_ge(S["table_set"], 2)
            for c in range(3):
                sp.wait_ge(rows_out[c], 32 * ((NG - 1 - c) // 3 + 1))

            def load(at):
                if at.active(0):
                    c = at.par(0, 4)
                    start = sp.value_load(tab_row[0:1, bass.ds(at.val(0, 1, 0), 1)], min_val=0, max_val=EXPERTS * CAP)
                    if at.active(-4):
                        ge(sp, S["token_set"], at.val(-4, 1, 1))
                        apart(sp, S["y_set"], at.val(-4, 1, 1))
                    sp.dma_start(row[c][:, :, :], routed[bass.ds(start, TILE)].rearrange("(p j) w -> p j w", j=2))\
                        .then_inc(tile_in[c], 16)

            for t in range(4):
                load(At(None, t, TILES, UNROLL_B))
            with sp.Fori(0, TILES // 4 - 1) as it:
                for j in range(4):
                    load(At(it, 4 + j, TILES, UNROLL_B))
            for t in range(TILES // 4 * 4, TILES):
                load(At(None, t, TILES, UNROLL_B))
            for c in range(2):
                sp.wait_ge(outs[c], 32 * ((TILES - 1 - c) // 2 + 1))

        @block.gpsimd
        def _(pool):
            nsetup = 0

            def setup(ins):
                nonlocal nsetup
                nsetup += 1
                ins.then_inc(S["setup_pool"], 1)

            setup(pool.memset(ident[:, :], 0.0))
            setup(pool.memset(ident16[:, :], 0.0))
            setup(pool.memset(earlier[:, :], 1.0))
            setup(pool.memset(ones16[:, :], 1.0))
            setup(pool.memset(mhalf[:, :], -0.5))
            setup(pool.memset(powers[:, :, :, 0:1], 1.0))
            setup(pool.iota(token_no[:, :], pattern=[[P, NB]], base=0, channel_multiplier=1))
            setup(pool.iota(ekey_i[:, :], pattern=[[-1, EXPERTS]], base=EXPERTS, channel_multiplier=0))
            setup(pool.iota(base_i[:, :], pattern=[[CAP, EXPERTS]], base=0, channel_multiplier=0))
            setup(pool.iota(steps_i[:, 0:MAXT], pattern=[[TILE, MAXT]], base=0, channel_multiplier=0))
            setup(pool.iota(steps_i[:, MAXT:], pattern=[[1, TILES]], base=0, channel_multiplier=0))
            pool.wait_ge(S["setup_pool"], nsetup)
            for m in (ident, ident16):
                setup(pool.affine_select(out=m[:, :], in_=m[:, :], compare_op=ALU.not_equal, fill=1.0, base=0,
                                         pattern=[[-1, P]], channel_multiplier=1))
            setup(pool.affine_select(out=earlier[:, :], in_=earlier[:, :], compare_op=ALU.is_ge, fill=0.0, base=-1,
                                     pattern=[[1, P]], channel_multiplier=-1))
            assert nsetup == 14
            pool.memset(zrow[:, :], 0.0).then_inc(S["small_set"], 1)
            for c in range(3):
                pool.memset(row[c][:, :, IDW:ROW], 0.0).then_inc(S["small_set"], 1)
            pool.memset(row[3][:, :, 0:IDW], 0.0).then_inc(S["small_set"], 1)
            pool.memset(row[3][:, :, IDW:ROW].bitcast(I32), NO_TOKEN).then_inc(S["small_set"], 1)
            pool.memset(idx[:, :, :], 0).then_inc(S["small_set"], 1)
            pool.wait_ge(S["small_set"], 7)
            pool.wait_ge(S["ids_done"], 1)

            def rsqrt(dst, var, ready, value, mid_sem, done, eps, scale=1.0):
                apart(pool, ready, value)
                pool.tensor_scalar(dst[:, 0, :], var, scale, eps, ALU.mult, ALU.add).then_inc(mid_sem[0], 1)
                ge(pool, mid_sem[0], mid_sem[1])
                pool.tensor_tensor(dst[:, 1, :], dst[:, 0, :], mhalf[:, :], ALU.pow).then_inc(done, 1)

            def norm_terms(rs, mv, bias, at, off, mv_set, v_set, rs_set, b_set):
                apart(pool, mv_set, at.val(off, GB, GB))
                pool.tensor_scalar(rs[:, 0, :], mv[:, :, 1], 1.0, 1e-5, ALU.mult, ALU.add).then_inc(v_set, 1)
                pool.tensor_scalar(bias[:, 0, :], mv[:, :, 0], -1.0, 0.0, ALU.mult, ALU.add).then_inc(b_set, 1)
                ge(pool, v_set, at.val(off, 1, 1))
                pool.tensor_tensor(rs[:, 1, :], rs[:, 0, :], mhalf[:, :], ALU.pow).then_inc(rs_set, 1)
                ge(pool, b_set, at.val(off, 2, 1))
                ge(pool, rs_set, at.val(off, 1, 1))
                pool.tensor_tensor(bias[:, 1, :], bias[:, 0, :], rs[:, 1, :], ALU.mult).then_inc(b_set, 1)

            def low(dst, src, high_set, value, done):
                ge(pool, high_set, value)
                pool.tensor_tensor(dst[:, :, D:D + TAIL], src[:, :, P:D], dst[:, :, P:D], ALU.subtract)\
                    .then_inc(done, 1)
                pool.tensor_tensor(dst[:, :, D + TAIL:SPLIT], src[:, :, 0:P], dst[:, :, 0:P], ALU.subtract)\
                    .then_inc(done, 1)

            def step(at):
                for slot in range(SLOTS):
                    slot_step(at, slot)
                if at.it is None and at.const < FIRST + 3:
                    c = at.const - FIRST
                    pool.memset(Qs[c].rearrange("p t a n -> p (t a n)").bitcast(F32), 0.0).then_inc(S["zero_set"], 1)

            def slot_step(at, slot):
                def due(name):
                    return POOL_PLAN[name][0] == slot and at.active(POOL_PLAN[name][1])

                if due("SO"):
                    off = POOL_PLAN["SO"][1]
                    low(os16, oo, S["oh_set"], at.val(off, 1, 1), S["os_set"])
                if due("rms"):
                    off = POOL_PLAN["rms"][1]
                    rsqrt(rms, sumsq[:, :], S["sq_set"], at.val(off, GB, GB), (S["rq_set"], at.val(off, 1, 1)),
                          S["rms_set"], 1e-6, 1.0 / D)
                if due("R2"):
                    off = POOL_PLAN["R2"][1]
                    ge(pool, S["xh_set"], at.val(off, GB, 0))
                    ge(pool, S["xn_set"], at.val(off, GB, 0))
                    norm_terms(rs2, mv2, nb2, at, off, S["mv2_set"], S["v2_set"], S["rs2_set"], S["nb2_set"])
                if due("scatter"):
                    off = POOL_PLAN["scatter"][1]
                    c = at.par(off)
                    ge(pool, S["id_set"], at.val(off, 1, 1))
                    apart(pool, S["slot_set"], at.val(off, 1, 1))
                    for b in range(GB):
                        pool.indirect_dma_start(
                            out=routed, out_offset=bass.IndirectOffsetOnAxis(ap=slot_i[c][:, b:b + 1], axis=0),
                            in_=row[c][:, b, :], in_offset=None).then_inc(rows_out[c], 16)
                if due("XL"):
                    off = POOL_PLAN["XL"][1]
                    ge(pool, S["xn_set"], at.val(off, GB, GB))
                    low(xs, xn, S["xh_set"], at.val(off, GB, GB), S["xs_set"])
                if due("R1"):
                    off = POOL_PLAN["R1"][1]
                    rsqrt(rs1, mv1[:, :, 1], S["mv1_set"], at.val(off, GB, GB), (S["v1_set"], at.val(off, 1, 1)),
                          S["rs1_set"], 1e-12)
                if due("gather"):
                    off = POOL_PLAN["gather"][1]
                    c = at.par(off)
                    apart(pool, turns_in[c], at.turned(off - 3, 32) if at.active(off - 3) else 0)
                    pool.tensor_copy(idx[:, c, :], ids[:, bass.ds(at.val(off, GB, 0), GB)]).then_inc(S["idx_set"], 1)
                    ge(pool, S["pw_ready"], at.val(off, 1, -2))
                    apart(pool, S["idx_set"], at.val(off, 1, 1))
                    for b in range(GB):
                        pool.indirect_dma_start(
                            out=turn[:, c, b, :], out_offset=None, in_=turns,
                            in_offset=bass.IndirectOffsetOnAxis(ap=idx[:, c, b:b + 1], axis=0))\
                            .then_inc(turns_in[c], 16)
                if due("R3"):
                    off = POOL_PLAN["R3"][1]
                    rsqrt(rs3, mv3[:, :, 1], S["mv3_set"], at.val(off, GB, GB), (S["v3_set"], at.val(off, 1, 1)),
                          S["rs3_set"], 1e-5)
                if due("H0"):
                    off = POOL_PLAN["H0"][1]
                    ge(pool, S["e1_set"], at.val(off, GB, GB))
                    pool.tensor_tensor(e2[:, :, :], e1[:, :, :], mid(gamma[:, :], GB), ALU.mult)\
                        .then_inc(S["gm_set"], 1)
                    ge(pool, S["gm_set"], at.val(off, 1, 1))
                    ge(pool, S["xn_set"], at.val(off, GB, 0))
                    ge(pool, S["xh_set"], at.val(off, GB, 0))
                    pool.tensor_tensor(h0[:, :, :], e2[:, :, :], mid(beta[:, :], GB), ALU.add).then_inc(S["h0_set"], 1)
                    ge(pool, S["h0_set"], at.val(off, 1, 1))
                    pool.tensor_tensor(hb[:, bass.ds(at.val(off, GB, 0), GB), :], h0[:, :, :], mid(bproj[:, :], GB),
                                       ALU.add).then_inc(S["hb_set"], 1)
                if due("PW"):
                    off = POOL_PLAN["PW"][1]
                    t = turn[:, at.par(off)]
                    ge(pool, turns_in[at.par(off)], at.turned(off, 32))
                    apart(pool, S["f1_ready"], at.val(off, 1, 0))
                    pool.tensor_copy(powers[:, :, :, 1], t).then_inc(S["pw_set"], 1)
                    pool.tensor_tensor(powers[:, :, :, 2], t, t, ALU.mult).then_inc(S["pw1"], 1)
                    ge(pool, S["pw1"], at.val(off, 1, 1))
                    pool.tensor_tensor(powers[:, :, :, 3], powers[:, :, :, 2], t, ALU.mult).then_inc(S["pw2"], 1)
                    pool.tensor_tensor(powers[:, :, :, 4], powers[:, :, :, 2], powers[:, :, :, 2], ALU.mult)\
                        .then_inc(S["pw_ready"], 1)
                if due("X3L"):
                    off = POOL_PLAN["X3L"][1]
                    low(row[at.par(off)][:, :, 0:D].bitcast(F16), xn3, S["x3h_set"], at.val(off, 1, 1), S["x3_set"])

            over_steps(pool, step)

            def expert_step(at):
                if at.active(-1):
                    c = at.par(-1, 2)
                    ge(pool, S["token_set"], at.val(-1, 1, 1))
                    apart(pool, S["y_set"], at.val(-1, 1, 1))
                    for j in range(2):
                        pool.indirect_dma_start(
                            out=out.rearrange("b s d -> (b s) d"), out_offset=bass.IndirectOffsetOnAxis(
                                ap=tokens[:, c, j:j + 1], axis=0),
                            in_=xn_e[c][:, j, :], in_offset=None, bounds_check=TOK - 1, oob_is_err=False)\
                            .then_inc(outs[c], 16)

            over_tiles(pool, expert_step)

        @block.tensor
        def _(pe):
            pe.wait_ge(S["setup_pool"], 14)
            pe.wait_ge(S["ids_x"], 1)
            pe.transpose(misc[0][:, 0:NB], x_f[:, :], ident[0:NB, 0:NB]).then_inc(S["ids_t"], 1)
            pe.wait_ge(S["ids_done"], 1)
            pe.wait_ge(S["emb_in"], 5 * 16)
            def base_name(name):
                return name.rstrip("ab")

            def claim(at, name):
                n = PE_TASKS.index(name)
                if name.endswith("b"):
                    return misc[BANK_OF[base_name(name)]]
                order = [(at, t) for t in PE_TASKS[:n]][::-1] + [(at.before(), t) for t in PE_TASKS[::-1]]
                for at_, t in order:
                    if BANK_OF[base_name(t)] == BANK_OF[base_name(name)] and at_.active(PE_PLAN[t][1]):
                        sem_name, per, nth = READ_BY[base_name(t)]
                        ge(pe, S[sem_name], at_.val(PE_PLAN[t][1], per, nth))
                        break
                return misc[BANK_OF[base_name(name)]]

            TERMS = ((0, 0, 0), (0, 0, 1), (2, 0, 0), (1, 1, 0), (1, 1, 1))

            def transposes3(dst, src, ready):
                for k in range(3):
                    for b in range(GB):
                        mm = pe.transpose(dst[:, k * GT + b * P:k * GT + b * P + P], src[:, b, k * P:k * P + P],
                                          ident16[:, :])
                mm.then_inc(ready, 1)

            def tokens_by(dst, xT_, w, n, ready, rows=range(GB)):
                for b in rows:
                    for i, (k, r, part) in enumerate(TERMS):
                        mm = pe.matmul(dst[:, b * n:b * n + n], xT_[:, k, b * P:b * P + P], w[:, r, part],
                                       start=i == 0, stop=i == len(TERMS) - 1)
                if rows[-1] == GB - 1:
                    mm.then_inc(ready, 1)

            def task(at, name):
                off = PE_PLAN[name][1]
                if not at.active(off):
                    return
                m = claim(at, name)
                m16 = m[:, :].bitcast(F16)
                if name == "F1":
                    ge(pe, S["pw_ready"], at.val(off, 1, 1))
                    ge(pe, S["pw2"], at.val(off, 1, 1))
                    apart(pe, S["pw_set"], at.val(off, 1, 1))
                    for b in range(GB):
                        mm = pe.transpose(m[0:TURNS * POLY, b * P:b * P + P],
                                          powers[:, b].rearrange("s t p -> s (t p)"), ident[:, :])
                    mm.then_inc(S["f1_ready"], 1)
                elif name == "F2":
                    ge(pe, S["pwT_ready"], at.val(off, 1, 1))
                    for b in range(GB):
                        mm = pe.matmul(m[:, b * D:b * D + D], powersT[:, b * P:b * P + P], poly_sb[:, :],
                                       start=True, stop=True)
                    mm.then_inc(S["f2_ready"], 1)
                elif name == "F3":
                    ge(pe, S["xs_set"], at.val(off, 2, 2))
                    transposes3(m16, xs, S["f3_ready"])
                elif base_name(name) in ("F4", "F5", "F6"):
                    half = "ab".index(name[2])
                    if at.it is None and at.const + off == 0:
                        pe.wait_ge(S["wqkv_set"], 2)
                    t = 2 * (int(name[1]) - 4) + half
                    ge(pe, S["xT_ready"], at.val(off, 1, 1))
                    for i, (k, r, part) in enumerate(TERMS):
                        mm = pe.matmul(m[:, half * GT:half * GT + GT], wqkv[:, r, part, t * P:t * P + P],
                                       xT[:, k, :], start=i == 0, stop=i == len(TERMS) - 1)
                    if half == 1:
                        mm.then_inc(S["f4_ready"], 1)
                elif base_name(name) == "V":
                    tokens_by(m, xT, wqkv[:, :, :, QK:WC], D, S["v_ready"], ["ab".index(name[1])])
                elif name == "NM":
                    ge(pe, S["s_used"], at.val(off, NCH, NCH))
                    for b in range(GB):
                        mm = pe.transpose(m16[0:VH, b * P:b * P + P],
                                          nm[at.par(off)][:, b].rearrange("n a p -> n (a p)"), ident16[:, :])
                    mm.then_inc(S["nm_ready"], 1)
                elif name in ("KO0", "KO1", "KO2", "KO3"):
                    w = int(name[2])
                    ge(pe, S["o_set"], at.val(off, 4, w + 1))
                    for c in range(3):
                        mm = pe.transpose(m[:, c * P:c * P + P], ot[w % 2][:, c * P:c * P + P], ident[:, :])
                    mm.then_inc(S["ko_ready"], 1)
                elif name == "KT":
                    ge(pe, S["os_set"], at.val(off, 2, 2))
                    transposes3(m16, os16, S["kt_ready"])
                elif base_name(name) == "KP":
                    ge(pe, S["oT_set"], at.val(off, 1, 1))
                    tokens_by(m, oT, wp, D, S["kp_ready"], ["ab".index(name[2])])
                elif name == "KG":
                    ge(pe, S["x3_set"], at.val(off, 2, 2))
                    transposes3(m16, row[at.par(off)][:, :, 0:D].bitcast(F16), S["kg_ready"])
                elif name == "GL":
                    ge(pe, S["gT_set"], at.val(off, 1, 1))
                    tokens_by(m, gT, wgs, EXPERTS, S["gl_ready"])
                elif name == "RK":
                    ge(pe, S["chosen_set"], at.val(off, 1, 1))
                    E = EXPERTS
                    both = chosen[:, :, :].rearrange("n b e -> n (b e)")
                    pe.matmul(m[:, 0:GB * E], earlier[:, :], both, start=True, stop=True)
                    pe.matmul(m[:, GB * E:2 * GB * E], ones16[:, :], both, start=True, stop=True)\
                        .then_inc(S["rk_ready"], 1)

            def step(at):
                if at.it is None and at.const == 1:
                    pe.wait_ge(S["consts_in"], CONSTS * 16)
                    pe.transpose(o_bank[0][:, 0:EXPERTS * HT], b1r[:, :], ident[0:EXPERTS * HT, 0:EXPERTS * HT])\
                        .then_inc(S["b1_ready"], 1)
                    pe.wait_ge(S["setup_dve"], 1)
                for slot in range(SLOTS):
                    if at.active(0):
                        c, b, cc = at.par(0), slot // CH, slot % CH
                        if slot == 0:
                            ge(pe, ops_in[c], at.turned(0, 14 * 16))
                        ge(pe, S["s_used"], at.val(0, NCH, slot - 1))
                        for a in range(2):
                            for pp in range(2):
                                p = 2 * cc + pp
                                mm = pe.matmul(s_bank[slot % 2][:, (2 * a + pp) * P:(2 * a + pp) * P + P],
                                               Qs[c][:, p, a, b * P:b * P + P], Ks[c][:, p, b * P:b * P + P],
                                               start=True, stop=True)
                        mm.then_inc(S["s_ready"], 1)
                    off, k = chunk_of(slot, LAG_T)
                    if at.active(off):
                        c, b, cc = at.par(off), k // CH, k % CH
                        if k == 0:
                            ge(pe, nm_in[c], at.turned(off, 32))
                        ge(pe, S["p_ready"], at.val(off, NCH, k + 1 - TBANKS))
                        for pp in range(2):
                            p = 2 * cc + pp
                            mm = pe.matmul(t_bank[k % TBANKS][:, pp * 2 * P:(pp + 1) * 2 * P],
                                           Ks[c][:, p, b * P:b * P + P], Qs[c][:, p, :, b * P:b * P + P],
                                           start=True, stop=True)
                        mm.then_inc(S["t_ready"], 1)
                    off, k = chunk_of(slot, LAG_PV)
                    if at.active(off):
                        c, b, cc = at.par(off), k // CH, k % CH
                        w = k // 3
                        if k == 0:
                            ge(pe, S["v_set"], at.val(off, 1, 1))
                        if k % 3 == 0:
                            ge(pe, S["o_set"], at.val(off, 4, w + 1 - OBANKS))
                        ge(pe, S["p_ready"], at.val(off, NCH, k + 1))
                        for j in range(4):
                            head = (4 * cc + j) % HEADS
                            mm = pe.matmul(o_bank[w % OBANKS][32 * j:32 * j + HD + 1, (cc % 3) * P:(cc % 3) * P + P],
                                           Vx[c][:, b, head, :], probs[k % 4][:, j * P:j * P + P],
                                           start=True, stop=True)
                        mm.then_inc(S["pv_done"], 1)
                    for name in PE_TASKS:
                        if PE_PLAN[name][0] == slot:
                            task(at, name)

            over_steps(pe, step)

            pe.wait_ge(S["table_set"], 2)

            def expert_of(at, off):
                return pe.value_load(tab_e[0:1, bass.ds(at.val(off, 1, 0), 1)], min_val=0, max_val=EXPERTS - 1)

            def expert_step(at):
                e_up = expert_of(at, 0) if at.active(0) else None
                e_down = expert_of(at, -1) if at.active(-1) else None
                if at.active(1):
                    m = misc[at.par(1, 2)]
                    c = at.par(1, 4)
                    ge(pe, S["xe_set"], at.val(1, 1, -1))
                    ge(pe, tile_in[c], at.turned(1, 16, 4))
                    transposes3(m[:, :].bitcast(F16), row[c][:, :, 0:D].bitcast(F16), S["tT_ready"])
                if at.it is None and at.const == 0:
                    pe.wait_ge(S["ffn_set"], 2 * EXPERTS)
                if at.active(0):
                    ge(pe, S["xe_set"], at.val(0, 1, 1))
                    for k in range(3):
                        bank_ = u_bank[(3 * at.const + k) % 4]
                        ge(pe, S["g_set"], at.val(0, 6, 2 * (k - 3)))
                        for t in (2 * k, 2 * k + 1):
                            for i, (ck, r, part) in enumerate(TERMS):
                                at_w = e_up * (4 * HIDDEN) + ((2 * r + part) * HIDDEN + t * P)
                                mm = pe.matmul(bank_[:, (t - 2 * k) * GT:(t - 2 * k + 1) * GT],
                                               w1f[:, bass.ds(at_w, P)], xe[at.par(0, 2)][:, ck, :],
                                               start=i == 0, stop=i == len(TERMS) - 1)
                        mm.then_inc(S["u_ready"], 1)
                if at.active(-1):
                    c = at.par(-1, 2)
                    ge(pe, S["hl_set"], at.val(-1, 3, 3))
                    ge(pe, S["ysum_set"], at.val(-1, 1, -1))
                    for j in range(2):
                        n, steps = 0, [(k, x, w) for k in range(HT) for x, w in ((0, 0), (0, 1), (1, 0))]
                        for n, (k, x, w) in enumerate(steps):
                            mm = pe.matmul(y_bank[c][:, j * D:j * D + D], hid[:, c, x, k, j * P:j * P + P],
                                           w2f[:, bass.ds(e_down * (2 * HT * D) + (w * HT + k) * D, D)],
                                           start=n == 0, stop=n == len(steps) - 1)
                    mm.then_inc(S["dn_ready"], 1)

            over_tiles(pe, expert_step)

        @block.scalar
        def _(act):
            def copy(dst, src, done):
                nc.scalar.activation(dst, src, ACT.Copy).then_inc(done, 1)


            def load_constants():
                n = 0
                for to, of in ((wpst[:, 0, :], w_proj[0:P, :]), (wpst[0:TAIL, 1, :], w_proj[P:D, :]),
                               (wpst[TAIL:P, 1, :], w_proj[P:D, :]),
                               (normw[:, 0:1], norm_w[0:P].unsqueeze(1)),
                               (normw[0:TAIL, 1:2], norm_w[P:D].unsqueeze(1)),
                               (normw[TAIL:P, 1:2], norm_w[P:D].unsqueeze(1)),
                               (wgst[:, 0, :], wg[0:P, :]), (wgst[0:TAIL, 1, :], wg[P:D, :]),
                               (wgst[TAIL:P, 1, :], wg[P:D, :]), (lam[:, :], lambda_1.partition_broadcast(P)),
                               (lam2[:, :], lambda_2.partition_broadcast(P)),
                               (bgate[:, :], bg.partition_broadcast(P)),
                               (b1r[:, :], b1.rearrange("e (t p) -> (e t) p", p=P)),
                               (b2_sb[:, :], b2.rearrange("e d -> (e d)").partition_broadcast(P))):
                    nc.scalar.dma_start(to, of).then_inc(S["consts_in"], 16)
                    n += 1
                assert n == CONSTS

            def expert_weights(at, slot):
                e = {(NG + 1, 8): 0, (NG + 2, 5): 1, (NG + 2, 7): 2, (NG + 2, 9): 3}.get((at.const, slot))
                if at.it is None and e is not None:
                    act.wait_ge(S["ffn_in"], 64)
                    act.wait_ge(S["t_ready"], NCH * NG)
                    copy(w1s[:, e, :, 0, :], stage1[:, e], S["w1h_set"])
                    copy(w2s[:, e, 0, :], stage2[:, e], S["w2h_set"])
                if at.it is None and at.const == LAST and slot == SLOTS - 1:
                    nc.scalar.activation(sq[0:1, 0, 0:1], sumsq[0:1, 0:1], ACT.Gelu).then_inc(S["w2h_set"], 1)

            def step(at):
                for slot in range(SLOTS):
                    if at.it is None and (at.const, slot) == (FIRST + 1, 4):
                        load_constants()
                    expert_weights(at, slot)
                    off, k = chunk_of(slot, LAG_T)
                    if at.active(off):
                        ge(act, S["t_ready"], at.val(off, NCH, k + 1))
                        ge(act, S["pv_done"], at.val(off, NCH, k - 3))
                        nc.scalar.activation(probs[k % 4][:, :], t_bank[k % TBANKS][:, :], ACT.Exp, scale=SCALE)\
                            .then_inc(S["p_ready"], 1)
                    def due(name):
                        return ACT_PLAN[name][0] == slot and at.active(ACT_PLAN[name][1])

                    for w in range(4):
                        if due(f"o{w}"):
                            off = ACT_PLAN[f"o{w}"][1]
                            ge(act, S["pv_done"], at.val(off, NCH, 3 * w + 3))
                            ge(act, S["ko_ready"], at.val(off, 4, w - 1))
                            copy(ot[w % 2][:, :], o_bank[w % OBANKS][:, 0:3 * P], S["o_set"])
                    for t in range(3):
                        if due(f"qkh{t}"):
                            off = ACT_PLAN[f"qkh{t}"][1]
                            ge(act, S["f4_ready"], at.val(off, 3, t + 1))
                            ge(act, S["scr_w1"], at.val(off, 32, 0))
                            ge(act, S["scr_w2"], at.val(off, 32, 0))
                            copy(qkh[:, 2 * t:2 * t + 2, :].rearrange("p t n -> p (t n)"),
                                 misc[BANK_OF[f"F{4 + t}"]][:, :], S["qkh_set"])
                    if due("xT"):
                        off = ACT_PLAN["xT"][1]
                        ge(act, S["f3_ready"], at.val(off, 1, 1))
                        ge(act, S["v_ready"], at.val(off, 1, 0))
                        copy(xT[:, :, :].rearrange("p k n -> p (k n)"),
                             misc[BANK_OF["F3"]][:, :].bitcast(F16)[:, 0:3 * GT], S["xT_ready"])
                    if due("powersT"):
                        off = ACT_PLAN["powersT"][1]
                        ge(act, S["f1_ready"], at.val(off, 1, 1))
                        ge(act, S["f2_ready"], at.val(off, 1, 0))
                        copy(powersT[:, :], misc[BANK_OF["F1"]][0:TURNS * POLY, 0:GT], S["pwT_ready"])
                    if due("nmT"):
                        off = ACT_PLAN["nmT"][1]
                        ge(act, S["nm_ready"], at.val(off, 1, 1))
                        if at.active(off - 1):
                            ge(act, nm_in[at.par(off - 1)], at.turned(off - 1, 32))
                        copy(nmT[:, :], misc[BANK_OF["NM"]][:, :].bitcast(F16)[0:VH, 0:GT], S["nmT_set"])
                    if due("oh"):
                        off = ACT_PLAN["oh"][1]
                        ge(act, S["oo_set"], at.val(off, GB, GB))
                        ge(act, S["kt_ready"], at.val(off, 1, 0))
                        copy(os16[:, :, 0:D], oo[:, :, :], S["oh_set"])
                    if due("oT"):
                        off = ACT_PLAN["oT"][1]
                        ge(act, S["kt_ready"], at.val(off, 1, 1))
                        ge(act, S["kp_ready"], at.val(off, 1, 0))
                        copy(oT[:, :, :].rearrange("p k n -> p (k n)"),
                             misc[BANK_OF["KT"]][:, :].bitcast(F16)[:, 0:3 * GT], S["oT_set"])
                    if due("v"):
                        off = ACT_PLAN["v"][1]
                        ge(act, S["v_ready"], at.val(off, 1, 1))
                        ge(act, S["pv_done"], at.val(off, NCH, -2 * NCH))
                        copy(Vx[at.par(off)][:, :, :, 0:HD],
                             misc[BANK_OF["V"]][:, 0:GB * D].rearrange("p (b h d) -> p b h d", b=GB, h=HEADS),
                             S["v_set"])
                    for b in range(GB):
                        if due(f"xh{b}"):
                            off = ACT_PLAN[f"xh{b}"][1]
                            ge(act, S["nb2_set"], at.val(off, 2, 2))
                            ge(act, S["xs_set"], at.val(off, 2, 0))
                            ge(act, S["f3_ready"], at.val(off, 1, 0))
                            for to, done in ((xn[:, b, :], "xn_set"), (xs[:, b, 0:D], "xh_set")):
                                nc.scalar.activation(to, h0[:, b, :], ACT.Identity, scale=rs2[:, 1, b:b + 1],
                                                     bias=nb2[:, 1, b:b + 1]).then_inc(S[done], 1)
                    for b in range(GB):
                        if due(f"sq{b}"):
                            off = ACT_PLAN[f"sq{b}"][1]
                            ge(act, S["rq_set"], at.val(off, 1, 0))
                            ge(act, S["oo_set"], at.val(off, GB, b + 1))
                            ge(act, S["sq_set"], at.val(off, GB, b - 1))
                            nc.scalar.activation(sq[:, b, :], oo[:, b, :], ACT.Square,
                                                 accum_out=sumsq[:, b:b + 1]).then_inc(S["sq_set"], 1)
                    if due("x3h"):
                        off = ACT_PLAN["x3h"][1]
                        ge(act, S["xn3_set"], at.val(off, GB, GB))
                        copy(row[at.par(off)][:, :, 0:D].bitcast(F16)[:, :, 0:D], xn3[:, :, :], S["x3h_set"])
                    if due("gT"):
                        off = ACT_PLAN["gT"][1]
                        ge(act, S["kg_ready"], at.val(off, 1, 1))
                        ge(act, S["gl_ready"], at.val(off, 1, 0))
                        copy(gT[:, :, :].rearrange("p k n -> p (k n)"),
                             misc[BANK_OF["KG"]][:, :].bitcast(F16)[:, 0:3 * GT], S["gT_set"])

            over_steps(act, step)

            write_pads(act, (2, 3))
            act.wait_ge(S["table_set"], 2)

            def expert_step(at):
                if at.active(1):
                    ge(act, S["tT_ready"], at.val(1, 1, 1))
                    ge(act, S["u_ready"], at.val(1, 3, -3))
                    copy(xe[at.par(1, 2)][:, :, :].rearrange("p k n -> p (k n)"),
                         misc[at.par(1, 2)][:, :].bitcast(F16)[:, 0:3 * GT], S["xe_set"])
                if at.active(0):
                    e = act.value_load(tab_e[0:1, bass.ds(at.val(0, 1, 0), 1)], min_val=0, max_val=EXPERTS - 1)
                    for k in range(3):
                        u = (3 * at.const + k) % 4
                        ge(act, S["hl_set"], at.val(0, 3, k - 3))
                        ge(act, S["u_ready"], at.val(0, 3, k + 1))
                        for t in range(2):
                            nc.scalar.activation(probs[u][:, t * GT:t * GT + GT], u_bank[u][:, t * GT:t * GT + GT],
                                                 ACT.Gelu, bias=b1T[:, bass.ds(e * HT + (2 * k + t), 1)])\
                                .then_inc(S["g_set"], 1)

            over_tiles(act, expert_step)

        @block.vector
        def _(dve):
            V = nc.vector
            dve.wait_ge(S["x_in_done"], 16)
            V.tensor_copy(x_f[:, :], x_in[:, :]).then_inc(S["ids_x"], 1)
            dve.wait_ge(S["ids_t"], 1)
            V.tensor_copy(ids[:, :], misc[0][:, 0:NB]).then_inc(S["ids_done"], 1)

            def prepare(at):
                if at.const == FIRST + 2:
                    dve.wait_ge(S["w_in"], 6 * 16)
                    V.tensor_copy(wqkv[:, :, 0, :], wst[:, :, :]).then_inc(S["wqkv_set"], 1)
                    dve.wait_ge(S["wqkv_set"], 1)
                    V.tensor_tensor(wqkv[:, :, 1, :], wst[:, :, :], wqkv[:, :, 0, :], ALU.subtract)\
                        .then_inc(S["wqkv_set"], 1)
                if FIRST + 2 <= at.const < FIRST + 5:
                    c = at.const - FIRST - 2
                    V.memset(Ks[c].rearrange("p t n -> p (t n)").bitcast(I32), ONES16).then_inc(S["ones_set"], 1)
                    V.memset(Vx[c][:, :, :, HD:HD + 1], 1.0).then_inc(S["w_scaled"], 1)
                if at.const == 1:
                    dve.wait_ge(S["b1_ready"], 1)
                    V.tensor_copy(b1T[:, :], o_bank[0][:, 0:EXPERTS * HT]).then_inc(S["w_scaled"], 1)
                    dve.wait_ge(S["w_scaled"], 4)
                    V.memset(o_bank[0][:, :], 0.0).then_inc(S["w_scaled"], 1)
                    for r in range(2):
                        V.tensor_scalar(wpst[:, r, :], wpst[:, r, :], normw[:, r:r + 1], None, ALU.mult)\
                            .then_inc(S["w_scaled"], 1)
                    V.tensor_copy(wgs[:, :, 0, :], wgst[:, :, :]).then_inc(S["w_scaled"], 1)
                    V.tensor_tensor(lam[:, :], lam[:, :], lam2[:, :], ALU.subtract).then_inc(S["w_scaled"], 1)
                    dve.wait_ge(S["w_scaled"], 9)
                    V.tensor_tensor(wgs[:, :, 1, :], wgst[:, :, :], wgs[:, :, 0, :], ALU.subtract)\
                        .then_inc(S["w_scaled"], 1)
                    V.tensor_copy(wp[:, :, 0, :], wpst[:, :, :]).then_inc(S["w_scaled"], 1)
                    V.tensor_scalar(lam[:, :], lam[:, :], 0.1, None, ALU.add).then_inc(S["w_scaled"], 1)
                    dve.wait_ge(S["setup_pool"], 11)
                    V.tensor_copy(ekey[:, :], ekey_i[:, :]).then_inc(S["w_scaled"], 1)
                    V.tensor_copy(base[:, 0, :], base_i[:, :]).then_inc(S["w_scaled"], 1)
                    V.tensor_copy(first_row[:, :], base_i[:, :]).then_inc(S["w_scaled"], 1)
                    V.tensor_copy(steps_f[:, :], steps_i[:, :]).then_inc(S["w_scaled"], 1)
                    dve.wait_ge(S["w_scaled"], 16)
                    V.tensor_tensor(wp[:, :, 1, :], wpst[:, :, :], wp[:, :, 0, :], ALU.subtract)\
                        .then_inc(S["setup_dve"], 1)

            def expert_weights(*parts):
                for part in parts:
                    e = part // 2
                    if part % 2 == 0:
                        dve.wait_ge(S["w1h_set"], e + 1)
                        V.tensor_tensor(w1s[:, e, :, 1, :], stage1[:, e], w1s[:, e, :, 0, :], ALU.subtract)\
                            .then_inc(S["ffn_set"], 1)
                    else:
                        dve.wait_ge(S["w2h_set"], e + 1)
                        V.tensor_tensor(w2s[:, e, 1, :], stage2[:, e], w2s[:, e, 0, :], ALU.subtract)\
                            .then_inc(S["ffn_set"], 1)

            def stats(src, st, st_sem):
                for b in range(GB):
                    V.bn_stats(st[:, b, :], src[:, b, :]).then_inc(st_sem, 1)

            def aggregate(st, mv, at, off, st_sem, mv_sem):
                apart(dve, st_sem, at.val(off, GB, GB))
                for b in range(GB):
                    V.bn_aggr(mv[:, b, :], st[:, b, :]).then_inc(mv_sem, 1)

            def apply(dst, src, mv, rs, done):
                for b in range(GB):
                    V.tensor_scalar(dst[:, b, :], src[:, b, :], mv[:, b, 0:1], rs[:, 1, b:b + 1],
                                    ALU.subtract, ALU.mult).then_inc(done, 1)

            def step(at):
                if at.it is None:
                    prepare(at)
                for slot in range(SLOTS):
                    slot_step(at, slot)
                    if at.it is None and (at.const, slot) == (NG + 2, 5):
                        expert_weights(0, 1)
                    if at.it is None and (at.const, slot) == (NG + 3, 5):
                        expert_weights(2, 3)

            def maxima(at, slot):
                if at.active(0):
                    b, cc = slot // CH, slot % CH
                    ge(dve, S["s_ready"], at.val(0, NCH, slot + 1))
                    if slot == 0:
                        ge(dve, S["nm_ready"], at.val(0, 1, -2))
                    V.tensor_reduce(nm[at.par(0)][:, b, :, 2 * cc:2 * cc + 2],
                                    s_bank[slot % 2][:, :].rearrange("n (a p m) -> n a p m", a=2, p=2),
                                    AX.X, ALU.max, negate=True).then_inc(S["s_used"], 1)

            def slot_step(at, slot):
                E = EXPERTS

                def due(name):
                    return DVE_PLAN[name][0] == slot and at.active(DVE_PLAN[name][1])

                for w in range(4):
                    if due(f"c{w}"):
                        off, b = DVE_PLAN[f"c{w}"][1], w // 2
                        o = misc[BANK_OF[f"KO{w}"]][:, 0:3 * P].rearrange("n (h r) -> n h r", r=32)
                        ge(dve, S["ko_ready"], at.val(off, 4, w + 1))
                        if w % 2 == 0:
                            V.reciprocal(rc1[:, :], o[:, :, HD]).then_inc(S["rc_set"], 1)
                        else:
                            V.reciprocal(rc2[:, 0, :], o[:, :, HD]).then_inc(S["rc2_set"], 1)
                for name, st, mv, used, n in (("1", bst, mv1, "e1_set", GB), ("2", bst2, mv2, "nb2_set", 2),
                                              ("3", bst3, mv3, "xn3_set", GB)):
                    if due("ag" + name):
                        off = DVE_PLAN["ag" + name][1]
                        ge(dve, S[f"v{name}_set"], at.val(off, 1, 0))
                        ge(dve, S[used], at.val(off, n, 0))
                        aggregate(st, mv, at, off, S[f"st{name}_set"], S[f"mv{name}_set"])
                for b in range(GB):
                    if due(f"m{b}"):
                        off = DVE_PLAN[f"m{b}"][1]
                        o = misc[BANK_OF[f"KO{2 * b + 1}"]][:, 0:3 * P].rearrange("n (h r) -> n h r", r=32)
                        ge(dve, S["rc2_set"], at.val(off, 2 * GB, 2 * b + 2))
                        ge(dve, S["oo_set"], at.val(off, GB, b))
                        V.tensor_tensor(o2[:, :, :], o[:, :, 0:HD], last(rc2[:, 1, :], HD), ALU.mult)\
                            .then_inc(S["o2_set"], 1)
                for b in range(GB):
                    if due(f"oo{b}"):
                        off = DVE_PLAN[f"oo{b}"][1]
                        ge(dve, S["o2_set"], at.val(off, GB, b + 1))
                        ge(dve, S["o1_set"], at.val(off, GB, b + 1))
                        if b == 0:
                            ge(dve, S["os_set"], at.val(off, 2, 0))
                            ge(dve, S["sq_set"], at.val(off, GB, 0))
                        V.tensor_tensor(oo[:, b, :].rearrange("n (h d) -> n h d", d=HD), o1[:, :, :], o2[:, :, :],
                                        ALU.subtract).then_inc(S["oo_set"], 1)
                if due("g1"):
                    off = DVE_PLAN["g1"][1]
                    ge(dve, S["gl_ready"], at.val(off, 1, 1))
                    V.tensor_tensor(lg[:, :, :], misc[BANK_OF["GL"]][:, 0:GB * E].rearrange("n (b e) -> n b e", b=GB),
                                    mid(bgate[:, :], GB), ALU.add).then_inc(S["lg_set"], 1)
                if due("g2"):
                    off = DVE_PLAN["g2"][1]
                    ge(dve, S["top_set"], at.val(off, 1, 1))
                    V.tensor_tensor(hit[:, :, :], lg[:, :, :], last(top[:, :], E), ALU.is_ge).then_inc(S["hit_set"], 1)
                if due("g3"):
                    off = DVE_PLAN["g3"][1]
                    ge(dve, S["hit_set"], at.val(off, 2, 2))
                    V.tensor_reduce(best[:, :], hit[:, :, :], AX.X, ALU.max).then_inc(S["best_set"], 1)
                if due("r1"):
                    off = DVE_PLAN["r1"][1]
                    ge(dve, S["rk_ready"], at.val(off, 1, 1))
                    ge(dve, S["base_set"], at.val(off, 1, 0))
                    V.tensor_tensor(base[:, 1, :], base[:, 0, :], misc[BANK_OF["RK"]][:, 2 * E:3 * E], ALU.add)\
                        .then_inc(S["base1_set"], 1)
                if due("r2"):
                    off = DVE_PLAN["r2"][1]
                    ge(dve, S["wh_set"], at.val(off, 1, 1))
                    V.tensor_tensor(base[:, 0, :], base[:, 1, :], misc[BANK_OF["RK"]][:, 3 * E:4 * E], ALU.add)\
                        .then_inc(S["base_set"], 1)
                    V.tensor_tensor(where2[:, :, :], where[:, :, :], chosen[:, :, :], ALU.mult)\
                        .then_inc(S["wh2_set"], 1)
                    V.tensor_copy(row[at.par(off)][:, :, IDW:IDW + 1].bitcast(I32),
                                  token_no[:, bass.ds(at.val(off, GB, 0), GB)].unsqueeze(2)).then_inc(S["id_set"], 1)
                if due("r3"):
                    off = DVE_PLAN["r3"][1]
                    ge(dve, S["slotf_set"], at.val(off, 1, 1))
                    V.tensor_copy(slot_i[at.par(off)][:, :], slot_f[:, :]).then_inc(S["slot_set"], 1)

                maxima(at, slot)

                for w in range(4):
                    if due(f"c{w}"):
                        off, b = DVE_PLAN[f"c{w}"][1], w // 2
                        o = misc[BANK_OF[f"KO{w}"]][:, 0:3 * P].rearrange("n (h r) -> n h r", r=32)
                        if w % 2 == 0:
                            ge(dve, S["rc_set"], at.val(off, GB, b + 1))
                            ge(dve, S["oo_set"], at.val(off, GB, b))
                            V.tensor_tensor(o1[:, :, :], o[:, :, 0:HD], last(rc1[:, :], HD), ALU.mult)\
                                .then_inc(S["o1_set"], 1)
                        else:
                            ge(dve, S["rc2_set"], at.val(off, 2 * GB, 2 * b + 1))
                            ge(dve, S["o2_set"], at.val(off, GB, b))
                            V.tensor_tensor(rc2[:, 1, :], rc2[:, 0, :], lam[:, :], ALU.mult).then_inc(S["rc2_set"], 1)
                if due("g1"):
                    off = DVE_PLAN["g1"][1]
                    ge(dve, S["lg_set"], at.val(off, 1, 1))
                    V.tensor_reduce(top[:, :], lg[:, :, :], AX.X, ALU.max).then_inc(S["top_set"], 1)
                if due("g2"):
                    off = DVE_PLAN["g2"][1]
                    ge(dve, S["hit_set"], at.val(off, 2, 1))
                    V.tensor_tensor(hit[:, :, :], hit[:, :, :], mid(ekey[:, :], GB), ALU.mult).then_inc(S["hit_set"], 1)
                if due("g3"):
                    off = DVE_PLAN["g3"][1]
                    ge(dve, S["best_set"], at.val(off, 1, 1))
                    ge(dve, S["wh2_set"], at.val(off, 1, 0))
                    V.tensor_tensor(chosen[:, :, :], hit[:, :, :], last(best[:, :], E), ALU.is_equal)\
                        .then_inc(S["chosen_set"], 1)
                if due("r1"):
                    off = DVE_PLAN["r1"][1]
                    ge(dve, S["base1_set"], at.val(off, 1, 1))
                    V.tensor_tensor(where[:, :, :],
                                    misc[BANK_OF["RK"]][:, 0:GB * E].rearrange("n (b e) -> n b e", b=GB),
                                    base[:, :, :], ALU.add).then_inc(S["wh_set"], 1)
                if due("r2"):
                    off = DVE_PLAN["r2"][1]
                    ge(dve, S["wh2_set"], at.val(off, 1, 1))
                    V.tensor_reduce(slot_f[:, :], where2[:, :, :], AX.X, ALU.add).then_inc(S["slotf_set"], 1)
                for t in range(3):
                    if due(f"qkl{t}"):
                        off = DVE_PLAN[f"qkl{t}"][1]
                        ge(dve, S["qkh_set"], at.val(off, 3, t + 1))
                        V.tensor_tensor(qkl[:, 2 * t:2 * t + 2, :].rearrange("p t n -> p (t n)"),
                                        misc[BANK_OF[f"F{4 + t}"]][:, :],
                                        qkh[:, 2 * t:2 * t + 2, :].rearrange("p t n -> p (t n)"), ALU.subtract)\
                            .then_inc(S["qkl_set"], 1)
                if due("E1"):
                    off = DVE_PLAN["E1"][1]
                    ge(dve, S["f2_ready"], at.val(off, 1, 1))
                    ge(dve, S["e1_set"], at.val(off, GB, 0))
                    V.tensor_tensor(emb[:, :, :], misc[BANK_OF["F2"]][:, 0:GB * D].rearrange("n (b d) -> n b d", b=GB),
                                    mid(pos_sb[:, :], GB), ALU.add).then_inc(S["emb_set"], 1)
                if due("st1"):
                    off = DVE_PLAN["st1"][1]
                    ge(dve, S["emb_set"], at.val(off, 1, 1))
                    ge(dve, S["mv1_set"], at.val(off, GB, 0))
                    stats(emb, bst, S["st1_set"])
                if due("h1"):
                    off = DVE_PLAN["h1"][1]
                    c = at.par(off)
                    ge(dve, S["kp_ready"], at.val(off, 1, 1))
                    ge(dve, S["rms_set"], at.val(off, 1, 1))
                    if at.active(off - 3):
                        ge(dve, rows_out[c], at.turned(off - 3, 32))
                    for b in range(GB):
                        V.scalar_tensor_tensor(
                            out=row[c][:, b, D:2 * D], in0=misc[BANK_OF["KP"]][:, b * D:b * D + D],
                            scalar=rms[:, 1, b:b + 1],
                            in1=hb[:, bass.ds(at.val(off, GB, b), 1), :].rearrange("n o d -> n (o d)"),
                            op0=ALU.mult, op1=ALU.add).then_inc(S["h1_set"], 1)
                if due("st3"):
                    off = DVE_PLAN["st3"][1]
                    ge(dve, S["h1_set"], at.val(off, GB, GB))
                    ge(dve, S["mv3_set"], at.val(off, GB, 0))
                    stats(row[at.par(off)][:, :, D:2 * D], bst3, S["st3_set"])
                if due("E2"):
                    off = DVE_PLAN["E2"][1]
                    ge(dve, S["rs1_set"], at.val(off, 1, 1))
                    ge(dve, S["gm_set"], at.val(off, 1, 0))
                    apply(e1, emb, mv1, rs1, S["e1_set"])
                if due("xn3"):
                    off = DVE_PLAN["xn3"][1]
                    ge(dve, S["rs3_set"], at.val(off, 1, 1))
                    ge(dve, S["x3_set"], at.val(off, 2, 0))
                    apply(xn3, row[at.par(off)][:, :, D:2 * D], mv3, rs3, S["xn3_set"])
                if due("st2"):
                    off = DVE_PLAN["st2"][1]
                    ge(dve, S["h0_set"], at.val(off, 1, 1))
                    ge(dve, S["mv2_set"], at.val(off, GB, 0))
                    stats(h0, bst2, S["st2_set"])

            over_steps(dve, step)

            steps_256, tiles_ = steps_f[:, 0:MAXT], steps_f[:, MAXT:MAXT + TILES]
            done = 0

            def link(ins):
                nonlocal done
                done += 1
                ins.then_inc(S["table"], 1)
                dve.wait_ge(S["table"], done)

            dve.wait_ge(S["base_set"], NG)
            V.tensor_copy(pad_at[:, :], base[0:1, 0, :]).then_inc(S["pads_set"], 1)
            link(V.tensor_tensor(cnt[:, :], base[0:1, 0, :], first_row[0:1, :], ALU.subtract))
            link(V.tensor_tensor(over[:, :, :], last(cnt[:, :], MAXT), mid(steps_256, EXPERTS), ALU.is_gt))
            link(V.tensor_reduce(tl[:, :], over[:, :, :], AX.X, ALU.add))
            link(V.tensor_copy(cum[:, 0:1], tl[:, 0:1]))
            for e in range(1, EXPERTS):
                link(V.tensor_tensor(cum[:, e:e + 1], cum[:, e - 1:e], tl[:, e:e + 1], ALU.add))
            link(V.tensor_tensor(past[:, :, :], last(tiles_, EXPERTS), mid(cum[:, :], TILES), ALU.is_ge))
            link(V.tensor_reduce(ef[:, :], past[:, :, 0:EXPERTS - 1], AX.X, ALU.add))
            V.tensor_copy(tab_e[:, :], ef[:, :]).then_inc(S["table_set"], 1)
            link(V.tensor_tensor(skips[:, :, :], past[:, :, :], mid(tl[:, :], TILES), ALU.mult))
            link(V.tensor_reduce(skip[:, :], skips[:, :, 0:EXPERTS - 1], AX.X, ALU.add))
            link(V.scalar_tensor_tensor(out=tr[0][:, :], in0=ef[:, :], scalar=float(CAP // TILE), in1=tiles_,
                                        op0=ALU.mult, op1=ALU.add))
            link(V.tensor_tensor(tr[1][:, :], tr[0][:, :], skip[:, :], ALU.subtract))
            link(V.tensor_scalar(tr[2][:, :], tr[1][:, :], -1.0, float(EXPERTS * CAP // TILE), ALU.mult, ALU.add))
            link(V.tensor_tensor(tr[3][:, :], tr[2][:, :], past[:, :, EXPERTS - 1], ALU.mult))
            link(V.tensor_tensor(tr[4][:, :], tr[1][:, :], tr[3][:, :], ALU.add))
            V.tensor_scalar(tab_row[:, :], tr[4][:, :], float(TILE), None, ALU.mult).then_inc(S["table_set"], 1)
            expert_weights(4, 5, 6, 7)
            dve.wait_ge(S["table_set"], 2)

            def expert_step(at):
                if at.active(0):
                    for k in range(3):
                        c, g = at.par(0, 2), probs[(3 * at.const + k) % 4]
                        g = g[:, :].rearrange("p (t n) -> p t n", t=2)
                        ge(dve, S["g_set"], at.val(0, 6, 2 * k + 2))
                        V.tensor_copy(hid[:, c, 0, 2 * k:2 * k + 2, :], g).then_inc(S["hh_set"], 1)
                        ge(dve, S["hh_set"], at.val(0, 3, k + 1))
                        V.tensor_tensor(hid[:, c, 1, 2 * k:2 * k + 2, :], g, hid[:, c, 0, 2 * k:2 * k + 2, :],
                                        ALU.subtract).then_inc(S["hl_set"], 1)
                if at.active(-1):
                    c = at.par(-1, 2)
                    e = dve.value_load(tab_e[0:1, bass.ds(at.val(-1, 1, 0), 1)], min_val=0, max_val=EXPERTS - 1)
                    ge(dve, S["dn_ready"], at.val(-1, 1, 1))
                    ge(dve, S["y_set"], at.val(-1, 1, 0))
                    V.tensor_tensor(ysum[:, :, :], y_bank[c][:, 0:GB * D].rearrange("n (j d) -> n j d", j=2),
                                    mid(b2_sb[:, bass.ds(e * D, D)], 2), ALU.add).then_inc(S["ysum_set"], 1)
                    ge(dve, S["ysum_set"], at.val(-1, 1, 1))
                    if at.active(-3):
                        ge(dve, outs[c], at.turned(-3, 32, 2))
                    V.tensor_copy(tokens[:, c, :].unsqueeze(2), row[at.par(-1, 4)][:, :, IDW:IDW + 1].bitcast(I32))\
                        .then_inc(S["token_set"], 1)
                    V.tensor_tensor(xn_e[c][:, :, :], ysum[:, :, :], row[at.par(-1, 4)][:, :, D:2 * D], ALU.add)\
                        .then_inc(S["y_set"], 1)

            over_tiles(dve, expert_step)


_INS = ['x', 'L0_tok_turns', 'L0_tok_poly_coeffs', 'L0_tok_pos_table', 'L0_tok_ln_gamma', 'L0_tok_ln_beta',
        'L0_attn_W_qkv1', 'L0_attn_W_qkv2', 'L0_attn_W_proj', 'L0_attn_b_proj', 'L0_attn_norm_w', 'L0_attn_lambda_1',
        'L0_attn_lambda_2', 'L0_attn_xpos', 'L0_ffn_Wg', 'L0_ffn_bg', 'L0_ffn_W1', 'L0_ffn_b1', 'L0_ffn_W2',
        'L0_ffn_b2']


def kernel(**inputs):
    import numpy as np
    import concourse.bacc as bacc
    from concourse.bass_utils import run_bass_kernel_spmd

    nc = bacc.Bacc("TRN2", target_bir_lowering=False, num_devices=1)
    arrays, args = {}, []
    for name in _INS:
        a = np.ascontiguousarray(inputs[name])
        arrays[f"in_{name}_dram"] = a
        args.append(nc.dram_tensor(f"in_{name}_dram", a.shape, mybir.dt.from_np(a.dtype), kind="ExternalInput").ap())
    args.append(nc.dram_tensor("out_0_dram", (NB, P, D), F32, kind="ExternalOutput").ap())
    build(nc, *args)
    r = run_bass_kernel_spmd(nc, [arrays], core_ids=[0])
    return r.results[0]["out_0_dram"]
```
